# Optimizing a Trainium2 kernel written in Bass

```python
import numpy as np
import jax
import jax.numpy as jnp

def _softmax(x, axis=-1):
    return jax.nn.softmax(x, axis=axis)

def _gelu(x):
    return jax.nn.gelu(x, approximate=True)

def _silu(x):
    return jax.nn.silu(x)

def _sigmoid(x):
    return jax.nn.sigmoid(x)

def _layernorm(x, axis=-1, eps=1e-05):
    m = jnp.mean(x, axis=axis, keepdims=True)
    v = jnp.var(x, axis=axis, keepdims=True)
    return (x - m) / jnp.sqrt(v + eps)

def _scatter_add(tgt, idx, src, axis=0):
    return tgt.at[idx].add(src)

def _segment_sum(src, seg, n):
    return jax.ops.segment_sum(src, seg, n)
kernel_name = 'mk_decoder_postln_d1_seqx_r8_846ae0'

def setup_inputs(seed: int=0):
    np.random.seed(seed)
    _w = jnp.asarray

    def _rec_inputs():
        import jax
        import jax.numpy as jnp
        _rk = jax.random.key(seed)
        x = 7.22e-05 + 1 * jax.random.normal(jax.random.fold_in(_rk, 1), (64, 64, 256), jnp.float32)
        _lenS = 64 - jax.random.randint(jax.random.fold_in(_rk, 7), (64,), 0, max(1, 64 // 4) + 1, jnp.int32)
        _lenS2 = 64 - jax.random.randint(jax.random.fold_in(_rk, 8), (64,), 0, max(1, 64 // 4) + 1, jnp.int32)
        _ctx_1024P = jax.random.normal(jax.random.fold_in(_rk, 11), (64, 16, 128), jnp.float32)
        _ctx_1024c = jax.random.dirichlet(jax.random.fold_in(_rk, 511), 0.3 * jnp.ones((16,), jnp.float32), (64, 64))
        _ctx_1024t = jnp.einsum('bsk,bkd->bsd', _ctx_1024c, _ctx_1024P)
        _ctx_1024t = _ctx_1024t * jax.lax.rsqrt(jnp.mean(jnp.square(_ctx_1024t)) + 1e-12) * 0.953939
        ctx_1024 = -1.39393e-06 + 0.999914 * (_ctx_1024t + 0.3 * jax.random.normal(jax.random.fold_in(_rk, 611), (64, 64, 128), jnp.float32))
        fside_BxSx2_0 = jax.random.uniform(jax.random.fold_in(_rk, 12), (64, 64, 2), jnp.float32, 0.0, 0.999707)
        return (x, ctx_1024, fside_BxSx2_0)
    x, ctx_1024, fside_BxSx2_0 = _rec_inputs()

    def _L0_attn_setup():
        import jax, jax.numpy as jnp
        import numpy as np
        DIM = 256
        D_STATE = 128
        D_CONV = 4
        N_HEADS = 48
        N_GROUPS = 1
        D_HEAD = 64
        D_INNER = N_HEADS * D_HEAD
        EPS = 1e-05
        RES_MULT = 1.0
        SEQ = 128
        BATCH = 1

        def _rms(x, w, eps=EPS):
            return x * jax.lax.rsqrt(jnp.mean(x * x, axis=-1, keepdims=True) + eps) * w

        def _forward(x, norm_w, in_proj_w, conv_w, conv_b, dt_bias, A_log, D_param, inner_norm_w, out_proj_w, conv_state, ssm_state):
            b, s, _ = x.shape
            xn = _rms(x, norm_w)
            proj = xn @ in_proj_w.T
            gn = N_GROUPS * D_STATE
            z, xc, B, C, dt = jnp.split(proj, [D_INNER, 2 * D_INNER, 2 * D_INNER + gn, 2 * D_INNER + 2 * gn], axis=-1)
            xc = jnp.moveaxis(xc, 1, 2)
            xp = jnp.concatenate([jnp.broadcast_to(conv_state, (b, D_INNER, D_CONV - 1)), xc], axis=-1)
            conv_out = conv_b[None, :, None] + sum((conv_w[None, :, k, None] * xp[:, :, k:k + s] for k in range(D_CONV)))
            xc = jax.nn.silu(conv_out)
            x_ssm = jnp.moveaxis(xc, 1, 2).reshape(b, s, N_HEADS, D_HEAD)
            hpg = N_HEADS // N_GROUPS
            B = jnp.repeat(B.reshape(b, s, N_GROUPS, D_STATE), hpg, axis=2)
            C = jnp.repeat(C.reshape(b, s, N_GROUPS, D_STATE), hpg, axis=2)
            dt = jax.nn.softplus(dt + dt_bias)
            A = -jnp.exp(A_log)
            h0 = jnp.broadcast_to(ssm_state, (b, N_HEADS, D_STATE, D_HEAD))

            def step(h, ins):
                x_t, B_t, C_t, dt_t = ins
                dA = jnp.exp(A * dt_t)[..., None, None]
                h = dA * h + B_t[..., :, None] * x_t[..., None, :]
                y_t = jnp.einsum('bhnp,bhn->bhp', h, C_t) + D_param[None, :, None] * x_t
                return (h, y_t)
            _, ys = jax.lax.scan(step, h0, (jnp.moveaxis(x_ssm, 1, 0), jnp.moveaxis(B, 1, 0), jnp.moveaxis(C, 1, 0), jnp.moveaxis(dt, 1, 0)))
            y = jnp.moveaxis(ys, 0, 1).reshape(b, s, D_INNER)
            y = _rms(y, inner_norm_w)
            y = y * jax.nn.silu(z)
            out = y @ out_proj_w.T
            return x + out * RES_MULT
        key = jax.random.key(seed)
        ks = jax.random.split(key, 12)
        d_in_proj = 2 * D_INNER + 2 * N_GROUPS * D_STATE + N_HEADS
        return {'x': jax.random.normal(ks[0], (BATCH, SEQ, DIM), jnp.float32), 'norm_w': jnp.ones((DIM,), jnp.float32), 'in_proj_w': 0.02 * jax.random.normal(ks[1], (d_in_proj, DIM), jnp.float32), 'conv_w': 0.02 * jax.random.normal(ks[2], (D_INNER, D_CONV), jnp.float32), 'conv_b': 0.01 * jax.random.normal(ks[3], (D_INNER,), jnp.float32), 'dt_bias': 0.1 * jax.random.normal(ks[4], (N_HEADS,), jnp.float32), 'A_log': 0.1 * jax.random.normal(ks[5], (N_HEADS,), jnp.float32), 'D_param': 0.1 * jax.random.normal(ks[6], (N_HEADS,), jnp.float32), 'inner_norm_w': jnp.ones((D_INNER,), jnp.float32), 'out_proj_w': 0.02 * jax.random.normal(ks[7], (DIM, D_INNER), jnp.float32), 'conv_state': jnp.zeros((1, D_INNER, D_CONV - 1), jnp.float32), 'ssm_state': jnp.zeros((1, N_HEADS, D_STATE, D_HEAD), jnp.float32)}
    _L0_attn_all = _L0_attn_setup()
    _L0_attn_in = {k: v for k, v in _L0_attn_all.items() if k in ('norm_w', 'in_proj_w', 'conv_w', 'conv_b', 'dt_bias', 'A_log', 'D_param', 'inner_norm_w', 'out_proj_w', 'conv_state', 'ssm_state')}
    del _L0_attn_all

    def _L0_xattn_setup():
        import jax, jax.numpy as jnp
        import numpy as np
        DIM = 256
        CTX_DIM = 128
        N_HEADS = 32
        HEAD_DIM = DIM // N_HEADS
        POS_DIM = 2
        B, N, CTXN = (2, 256, 256)
        ROPE_BASE = 10000.0

        def apply_axial_rope(x, pos):
            b, n, h, d = x.shape
            p = pos.shape[-1]
            dpa = d // p
            half = dpa // 2
            freqs = ROPE_BASE ** (-jnp.arange(half, dtype=x.dtype) / half)
            ang = pos[..., :, None] * freqs
            cos = jnp.cos(ang)[:, :, None, :, :]
            sin = jnp.sin(ang)[:, :, None, :, :]
            xr = x.reshape(b, n, h, p, half, 2)
            x1, x2 = (xr[..., 0], xr[..., 1])
            out = jnp.stack([x1 * cos - x2 * sin, x1 * sin + x2 * cos], axis=-1)
            return out.reshape(b, n, h, d)
        key = jax.random.key(seed)
        ks = jax.random.split(key, 8)
        x = jax.random.normal(ks[0], (B, N, DIM), jnp.float32)
        ctx = jax.random.normal(ks[1], (B, CTXN, CTX_DIM), jnp.float32)
        pos_map = jax.random.uniform(ks[2], (B, N, POS_DIM), jnp.float32)
        ctx_pos_map = jax.random.uniform(ks[3], (B, CTXN, POS_DIM), jnp.float32)
        Wq = jax.random.normal(ks[4], (DIM, DIM), jnp.float32) / np.sqrt(DIM)
        Wkv = jax.random.normal(ks[5], (CTX_DIM, 2 * DIM), jnp.float32) / np.sqrt(CTX_DIM)
        Wout = jax.random.normal(ks[6], (DIM, DIM), jnp.float32) / np.sqrt(DIM)
        bout = jnp.zeros((DIM,), jnp.float32)
        return {'x': x, 'ctx': ctx, 'pos_map': pos_map, 'ctx_pos_map': ctx_pos_map, 'Wq': Wq, 'Wkv': Wkv, 'Wout': Wout, 'bout': bout}
    _L0_xattn_all = _L0_xattn_setup()
    _L0_xattn_in = {k: v for k, v in _L0_xattn_all.items() if k in ('Wq', 'Wkv', 'Wout', 'bout')}
    del _L0_xattn_all

    def _L0_ffn_setup():
        import jax, jax.numpy as jnp
        import numpy as np
        DIM = 256
        HID = 704
        ZERO_POINT = 128.0

        def _qlinear(x, wq, scale):
            W = (wq.astype(jnp.float32) - ZERO_POINT) * scale[:, None]
            return jnp.einsum('bsd,hd->bsh', x, W)
        key = jax.random.key(seed)
        ks = jax.random.split(key, 7)
        B, S = (4, 256)
        sg = jax.random.uniform(ks[1], (HID,)) * (0.02 / np.sqrt(DIM)) + 0.0001
        su = jax.random.uniform(ks[3], (HID,)) * (0.02 / np.sqrt(DIM)) + 0.0001
        sd = jax.random.uniform(ks[5], (DIM,)) * (0.02 / np.sqrt(HID)) + 0.0001
        return {'x': jax.random.normal(ks[0], (B, S, DIM), dtype=jnp.float32), 'wq_gate': jax.random.randint(ks[2], (HID, DIM), 0, 32, dtype=jnp.int32), 's_gate': sg, 'wq_up': jax.random.randint(ks[4], (HID, DIM), 0, 32, dtype=jnp.int32), 's_up': su, 'wq_down': jax.random.randint(ks[6], (DIM, HID), 0, 32, dtype=jnp.int32), 's_down': sd}
    _L0_ffn_all = _L0_ffn_setup()
    _L0_ffn_in = {k: v for k, v in _L0_ffn_all.items() if k in ('wq_gate', 's_gate', 'wq_up', 's_up', 'wq_down', 's_down')}
    del _L0_ffn_all
    return {'x': x, 'ctx_1024': ctx_1024, 'fside_BxSx2_0': fside_BxSx2_0, 'L0_attn_norm_w': _L0_attn_in['norm_w'], 'L0_attn_in_proj_w': _L0_attn_in['in_proj_w'], 'L0_attn_conv_w': _L0_attn_in['conv_w'], 'L0_attn_conv_b': _L0_attn_in['conv_b'], 'L0_attn_dt_bias': _L0_attn_in['dt_bias'], 'L0_attn_A_log': _L0_attn_in['A_log'], 'L0_attn_D_param': _L0_attn_in['D_param'], 'L0_attn_inner_norm_w': _L0_attn_in['inner_norm_w'], 'L0_attn_out_proj_w': _L0_attn_in['out_proj_w'], 'L0_attn_conv_state': _L0_attn_in['conv_state'], 'L0_attn_ssm_state': _L0_attn_in['ssm_state'], 'L0_xattn_Wq': _L0_xattn_in['Wq'], 'L0_xattn_Wkv': _L0_xattn_in['Wkv'], 'L0_xattn_Wout': _L0_xattn_in['Wout'], 'L0_xattn_bout': _L0_xattn_in['bout'], 'L0_ffn_wq_gate': _L0_ffn_in['wq_gate'], 'L0_ffn_s_gate': _L0_ffn_in['s_gate'], 'L0_ffn_wq_up': _L0_ffn_in['wq_up'], 'L0_ffn_s_up': _L0_ffn_in['s_up'], 'L0_ffn_wq_down': _L0_ffn_in['wq_down'], 'L0_ffn_s_down': _L0_ffn_in['s_down']}

def reference(x, ctx_1024, fside_BxSx2_0, L0_attn_norm_w, L0_attn_in_proj_w, L0_attn_conv_w, L0_attn_conv_b, L0_attn_dt_bias, L0_attn_A_log, L0_attn_D_param, L0_attn_inner_norm_w, L0_attn_out_proj_w, L0_attn_conv_state, L0_attn_ssm_state, L0_xattn_Wq, L0_xattn_Wkv, L0_xattn_Wout, L0_xattn_bout, L0_ffn_wq_gate, L0_ffn_s_gate, L0_ffn_wq_up, L0_ffn_s_up, L0_ffn_wq_down, L0_ffn_s_down):
    import jax
    import jax.numpy as jnp

    def _L0_attn_ref(x, norm_w, in_proj_w, conv_w, conv_b, dt_bias, A_log, D_param, inner_norm_w, out_proj_w, conv_state, ssm_state):
        import jax, jax.numpy as jnp
        import numpy as np
        DIM = 256
        D_STATE = 128
        D_CONV = 4
        N_HEADS = 48
        N_GROUPS = 1
        D_HEAD = 64
        D_INNER = N_HEADS * D_HEAD
        EPS = 1e-05
        RES_MULT = 1.0
        SEQ = 128
        BATCH = 1

        def _rms(x, w, eps=EPS):
            return x * jax.lax.rsqrt(jnp.mean(x * x, axis=-1, keepdims=True) + eps) * w

        def _forward(x, norm_w, in_proj_w, conv_w, conv_b, dt_bias, A_log, D_param, inner_norm_w, out_proj_w, conv_state, ssm_state):
            b, s, _ = x.shape
            xn = _rms(x, norm_w)
            proj = xn @ in_proj_w.T
            gn = N_GROUPS * D_STATE
            z, xc, B, C, dt = jnp.split(proj, [D_INNER, 2 * D_INNER, 2 * D_INNER + gn, 2 * D_INNER + 2 * gn], axis=-1)
            xc = jnp.moveaxis(xc, 1, 2)
            xp = jnp.concatenate([jnp.broadcast_to(conv_state, (b, D_INNER, D_CONV - 1)), xc], axis=-1)
            conv_out = conv_b[None, :, None] + sum((conv_w[None, :, k, None] * xp[:, :, k:k + s] for k in range(D_CONV)))
            xc = jax.nn.silu(conv_out)
            x_ssm = jnp.moveaxis(xc, 1, 2).reshape(b, s, N_HEADS, D_HEAD)
            hpg = N_HEADS // N_GROUPS
            B = jnp.repeat(B.reshape(b, s, N_GROUPS, D_STATE), hpg, axis=2)
            C = jnp.repeat(C.reshape(b, s, N_GROUPS, D_STATE), hpg, axis=2)
            dt = jax.nn.softplus(dt + dt_bias)
            A = -jnp.exp(A_log)
            h0 = jnp.broadcast_to(ssm_state, (b, N_HEADS, D_STATE, D_HEAD))

            def step(h, ins):
                x_t, B_t, C_t, dt_t = ins
                dA = jnp.exp(A * dt_t)[..., None, None]
                h = dA * h + B_t[..., :, None] * x_t[..., None, :]
                y_t = jnp.einsum('bhnp,bhn->bhp', h, C_t) + D_param[None, :, None] * x_t
                return (h, y_t)
            _, ys = jax.lax.scan(step, h0, (jnp.moveaxis(x_ssm, 1, 0), jnp.moveaxis(B, 1, 0), jnp.moveaxis(C, 1, 0), jnp.moveaxis(dt, 1, 0)))
            y = jnp.moveaxis(ys, 0, 1).reshape(b, s, D_INNER)
            y = _rms(y, inner_norm_w)
            y = y * jax.nn.silu(z)
            out = y @ out_proj_w.T
            return x + out * RES_MULT
        return _forward(x, norm_w, in_proj_w, conv_w, conv_b, dt_bias, A_log, D_param, inner_norm_w, out_proj_w, conv_state, ssm_state)

    def _L0_xattn_ref(x, ctx, pos_map, ctx_pos_map, Wq, Wkv, Wout, bout):
        import jax, jax.numpy as jnp
        import numpy as np
        DIM = 256
        CTX_DIM = 128
        N_HEADS = 32
        HEAD_DIM = DIM // N_HEADS
        POS_DIM = 2
        B, N, CTXN = (2, 256, 256)
        ROPE_BASE = 10000.0

        def apply_axial_rope(x, pos):
            b, n, h, d = x.shape
            p = pos.shape[-1]
            dpa = d // p
            half = dpa // 2
            freqs = ROPE_BASE ** (-jnp.arange(half, dtype=x.dtype) / half)
            ang = pos[..., :, None] * freqs
            cos = jnp.cos(ang)[:, :, None, :, :]
            sin = jnp.sin(ang)[:, :, None, :, :]
            xr = x.reshape(b, n, h, p, half, 2)
            x1, x2 = (xr[..., 0], xr[..., 1])
            out = jnp.stack([x1 * cos - x2 * sin, x1 * sin + x2 * cos], axis=-1)
            return out.reshape(b, n, h, d)
        b, n, _ = x.shape
        ctx_n = ctx.shape[1]
        q = (x @ Wq).reshape(b, n, N_HEADS, HEAD_DIM)
        k, v = jnp.split(ctx @ Wkv, 2, axis=-1)
        k = k.reshape(b, ctx_n, N_HEADS, HEAD_DIM)
        v = v.reshape(b, ctx_n, N_HEADS, HEAD_DIM)
        q = apply_axial_rope(q, pos_map)
        k = apply_axial_rope(k, ctx_pos_map)
        scale = 1.0 / np.sqrt(HEAD_DIM).astype(np.float32)
        logits = jnp.einsum('bqhd,bkhd->bhqk', q, k) * scale
        w = jax.nn.softmax(logits, axis=-1)
        attn = jnp.einsum('bhqk,bkhd->bqhd', w, v)
        attn = attn.reshape(b, n, N_HEADS * HEAD_DIM)
        return attn @ Wout + bout

    def _L0_ffn_ref(x, wq_gate, s_gate, wq_up, s_up, wq_down, s_down):
        import jax, jax.numpy as jnp
        import numpy as np
        DIM = 256
        HID = 704
        ZERO_POINT = 128.0

        def _qlinear(x, wq, scale):
            W = (wq.astype(jnp.float32) - ZERO_POINT) * scale[:, None]
            return jnp.einsum('bsd,hd->bsh', x, W)
        gate = _qlinear(x, wq_gate, s_gate)
        gate = jax.nn.silu(gate)
        up = _qlinear(x, wq_up, s_up)
        return _qlinear(gate * up, wq_down, s_down)
    x = _layernorm(x + _L0_attn_ref(x, L0_attn_norm_w, L0_attn_in_proj_w, L0_attn_conv_w, L0_attn_conv_b, L0_attn_dt_bias, L0_attn_A_log, L0_attn_D_param, L0_attn_inner_norm_w, L0_attn_out_proj_w, L0_attn_conv_state, L0_attn_ssm_state), axis=-1)
    x = _layernorm(x + _L0_xattn_ref(x, ctx_1024, fside_BxSx2_0, fside_BxSx2_0, L0_xattn_Wq, L0_xattn_Wkv, L0_xattn_Wout, L0_xattn_bout), axis=-1)
    x = _layernorm(x + _L0_ffn_ref(x, L0_ffn_wq_gate, L0_ffn_s_gate, L0_ffn_wq_up, L0_ffn_s_up, L0_ffn_wq_down, L0_ffn_s_down), axis=-1)
    return x

_drawn_inputs = setup_inputs


def setup_inputs(seed=0):
    import zlib

    import numpy as np

    out = dict(_drawn_inputs(seed))
    spreads = {'L0_attn_norm_w': (1.0, 0.2),
     'L0_attn_inner_norm_w': (1.0, 0.6),
     'L0_attn_conv_state': (0.0, 0.8),
     'L0_attn_ssm_state': (0.0, 0.1),
     'L0_xattn_bout': (0.0, 0.1)}
    factors = {'L0_attn_dt_bias': 8.0,
     'L0_attn_A_log': 6.158,
     'L0_attn_D_param': 5.247,
     'L0_ffn_s_gate': 8.0,
     'L0_ffn_s_up': 8.0,
     'L0_ffn_s_down': 8.0}
    for name, (base, spread) in spreads.items():
        noise = np.random.default_rng([zlib.crc32(name.encode()), seed]).standard_normal(out[name].shape)
        drawn = base * np.exp(spread * noise) if base else spread * noise
        out[name] = jnp.asarray(drawn.astype(out[name].dtype))
    for name, factor in factors.items():
        out[name] = (out[name] * factor).astype(out[name].dtype)
    return out
```

```python
import concourse.bass as bass
from concourse import mybir
from contextlib import ExitStack

F32 = mybir.dt.float32
F32R = mybir.dt.float32r
I32 = mybir.dt.int32
ALU = mybir.AluOpType
ACT = mybir.ActivationFunctionType
AX = mybir.AxisListType

P = 128
SEQS, S, D = 64, 64, 256
TOKENS = SEQS * S
KT = D // P
GT = 512
GROUPS = TOKENS // GT
TILES = GT // P
HEADS, HP, N = 48, 64, 128
INNER = HEADS * HP
PAIRS = HEADS // 2
TAPS = 4
BATCH = 3
RMS_EPS = 1e-5
LN_EPS = 1e-5
R_MOV, R_STA = 4, 16
R_ALL = R_MOV + R_STA + S
C_W, C_CB, C_IW, C_CS, C_EDGE, C_N = 0, 4, 5, 6, 9, 12
ROW_DMAS = 16
LN_STEPS = 8 + 2 * TILES
CONST_STEPS = 2 + 9 + 1 + 4 + 1
AUX = 2 * N + HEADS


def pools(nc, ctx):
    def sb(name, shape, dt=F32):
        return ctx.enter_context(nc.sbuf_tensor(name, shape, dt))

    def ps(name, shape=(P, 512)):
        return ctx.enter_context(nc.psum_tensor(name, list(shape), F32))

    def sem(name):
        return ctx.enter_context(nc.semaphore(name))

    return sb, ps, sem


def spread(ap, axis, n):
    ap = ap.unsqueeze(axis)
    shape = list(ap.shape)
    shape[axis] = n
    return ap.to_broadcast(shape)


def setup_weights(nc, pair_w, pair_split):
    cols = pair_w.shape[2]
    with ExitStack() as ctx:
        sb, ps, sem = pools(nc, ctx)
        raw = sb("raw", [P, 2, cols])
        hl = sb("hl", [P, 2, 2, cols], F32R)
        raw_in = [sem("raw_in0"), sem("raw_in1")]
        hl_out = [sem("hl_out0"), sem("hl_out1")]
        hi_done, lo_done = sem("hi_done"), sem("lo_done")
        block = ctx.enter_context(nc.Block())

        @block.sync
        def _(sp):
            for k in range(PAIRS):
                q = k % 2
                if k >= 2:
                    sp.wait_ge(lo_done, k - 1)
                sp.dma_start(raw[:, q, :], pair_w[k]).then_inc(raw_in[q], 16)
                if k >= 1:
                    sp.wait_ge(lo_done, k)
                    sp.dma_start(pair_split[k - 1], hl[:, 1 - q].bitcast(F32)).then_inc(hl_out[1 - q], 16)
            sp.wait_ge(lo_done, PAIRS)
            sp.dma_start(pair_split[PAIRS - 1], hl[:, 1].bitcast(F32)).then_inc(hl_out[1], 16)
            sp.wait_ge(hl_out[0], 16 * (PAIRS // 2))
            sp.wait_ge(hl_out[1], 16 * (PAIRS // 2))

        @block.scalar
        def _(act):
            for k in range(PAIRS):
                q = k % 2
                act.wait_ge(raw_in[q], 16 * (k // 2 + 1))
                if k >= 2:
                    act.wait_ge(hl_out[q], 16 * (k // 2))
                act.activation(hl[:, q, 0, :], raw[:, q, :], ACT.Copy).then_inc(hi_done, 1)

        @block.vector
        def _(dve):
            for k in range(PAIRS):
                q = k % 2
                dve.wait_ge(hi_done, k + 1)
                dve.tensor_tensor(hl[:, q, 1, :], raw[:, q, :], hl[:, q, 0, :].bitcast(F32),
                                  ALU.subtract).then_inc(lo_done, 1)


def mixer(nc, x, pair_split, aux_w, dt_par, chan_par, d_rows, norm_w, wout, x1,
          mov_rows, sta_rows, ec_rows,
          k_ident, k_eye2, k_reset, k_mov, k_sta, k_sel):
    xg = x.rearrange("(g t p) d -> g p t d", p=P, t=TILES)
    x1g = x1.rearrange("(g t p) d -> g p t d", p=P, t=TILES)
    with ExitStack() as ctx:
        sb, ps, sem = pools(nc, ctx)
        ident = sb("ident", [P, P])
        ones = sb("ones", [P, 1])
        reset = sb("reset", [HEADS, GT])
        norm_c = sb("norm_c", [P, KT])
        aux_hi = sb("aux_hi", [P, KT, AUX], F32R)
        aux_lo = sb("aux_lo", [P, KT, AUX], F32R)
        dtp = sb("dtp", [HEADS, 2])
        a_neg = sb("a_neg", [HEADS, 1])
        par = sb("par", [P, PAIRS, C_N])
        dd = sb("dd", [P, PAIRS, 2, S])
        wo = sb("wo", [P, PAIRS, D])
        mov = sb("mov", [R_ALL, 2, BATCH, GT], F32R)
        sta = sb("sta", [R_ALL, 2, BATCH, P], F32R)
        raw_sta = sb("raw_sta", [R_ALL, P])
        raw_sel = sb("raw_sel", [4, P])
        ec_sel = sb("ec_sel", [4, P], F32R)
        eye2 = sb("eye2", [P, S])
        d_all = sb("d_all", [P, HEADS])
        edge = sb("edge", [P, PAIRS])
        xa = sb("xa", [P, TILES, D])
        mhalf = sb("mhalf", [P, TILES])
        ss = sb("ss", [P, TILES])
        rstd = sb("rstd", [P, TILES])
        xs = sb("xs", [P, TILES, D])
        xh = sb("xh", [P, KT, GT], F32R)
        xl = sb("xl", [P, KT, GT], F32R)
        c_sb = sb("c_sb", [P, GT])
        ch = sb("ch", [P, GT], F32R)
        cl = sb("cl", [P, GT], F32R)
        cum = sb("cum", [HEADS, GT])
        rowsr = sb("rowsr", [HEADS, 4, GT], F32R)
        g_sb = sb("g_sb", [P, TILES, S])
        e_sb = sb("e_sb", [P, PAIRS, TILES, 2, S])
        wst = sb("wst", [P, 2, 2, 5 * P], F32R)
        ecr = sb("ecr", [4, 2, GT], F32R)
        gd = sb("gd", [P, 2, TILES, 2, S])
        mb = sb("mb", [P, 2, TILES, 2, P])
        acc = sb("acc", [P, 2, GT])
        xt = sb("xt", [P, 2, TILES, P])
        sz = sb("sz", [P, 2, GT])
        eb = sb("eb", [P, 2, GT])
        ce = sb("ce", [P, 2, GT])
        y = sb("y", [P, 2, GT])
        yz = sb("yz", [P, 2, GT])
        sq = sb("sq", [P, 2, GT])
        ssq = sb("ssq", [P, GT])
        raw_mov = acc[0:R_ALL, 0]
        aux_raw = ce[:].rearrange("p a b -> p (a b)")[:, 0:KT * AUX].rearrange("p (k c) -> p k c", k=KT)
        b_sb = y[:, 0]
        dv = sq[0:HEADS]
        ecs = yz[0:HEADS, 0]
        ry = sb("ry", [P, TILES])
        r1 = xs
        st6 = sb("st6", [P, TILES, 6])
        mv = sb("mv", [P, TILES, 3])
        rl = sb("rl", [P, TILES])
        xo = sb("xo", [P, TILES, D])

        b_xc, b_z, b_ch, b_ec, b_xt, b_y = (ps(f"bank_{n}") for n in ("xc", "z", "ch", "ec", "xt", "y"))
        b_out = [ps("bank_out0"), ps("bank_out1")]

        names = ("par_in fill con con_act x_in sq_x rs_x xs_done tr_done xh_done xl_done aux_done "
                 "bc_act cc_done v_done dt_dve sp_act cum_done cum_hl ec_hl ec_act rows_out g_pe g_done "
                 "rows_in0 rows_in1 diff_done exp_done "
                 "wst0 wst1 pe_xc pe_z pe_ch pe_ec pe_xt pe_intra pe_out "
                 "act_conv act_ec act_z act_xt act_sq dve_tap dve_ce dve_m dve_yadd dve_gate "
                 "pool_gd pool_m pool_sq pool_pow var_done sum_pe r_done ln_a ln_done out_st").split()
        s = {n: sem("m_" + n) for n in names}
        block = ctx.enter_context(nc.Block())

        @block.sync
        def _(sp):
            for dst, src in ((norm_c[:], norm_w), (aux_raw, aux_w), (dtp[:], dt_par),
                             (par[:, :, 0:C_EDGE], chan_par), (wo[:], wout),
                             (d_all[:], d_rows.partition_broadcast(P)), (ident[:], k_ident),
                             (eye2[:], k_eye2), (reset[:], k_reset), (raw_mov, k_mov), (raw_sta[:], k_sta),
                             (raw_sel[:], k_sel)):
                sp.dma_start(dst, src).then_inc(s["par_in"], 16)
            with sp.Fori(0, GROUPS) as g:
                sp.wait_ge(s["ln_a"], LN_STEPS * g)
                sp.dma_start(xa[:], xg[bass.ds(g, 1)].squeeze(0)).then_inc(s["x_in"], 16)
                sp.wait_ge(s["cum_hl"], 2 * (g + 1))
                for hl in range(2):
                    for hh in range(2):
                        src = rowsr[hh * PAIRS:(hh + 1) * PAIRS].bitcast(F32)
                        for b in range(2):
                            sp.dma_start(mov_rows[:, hl, b, :, hh, :], src[:, hl].rearrange(
                                "k (t b s) -> k t b s", b=2, s=S)[:, :, b]).then_inc(s["rows_out"], 16)
                        sp.dma_start(sta_rows[:, hl, :, hh, :],
                                     src[:, hl].rearrange("k (t p) -> k t p", p=P)).then_inc(s["rows_out"], 16)
                sp.wait_ge(s["ec_hl"], 2 * (g + 1))
                for hl in range(2):
                    for hh in range(2):
                        sp.dma_start(ec_rows[:, hl, hh, :],
                                     rowsr[hh * PAIRS:(hh + 1) * PAIRS, 2 + hl].bitcast(F32)).then_inc(s["rows_out"], 16)
                sp.wait_ge(s["rows_out"], 16 * ROW_DMAS * (g + 1))
                for b in range(PAIRS // BATCH):
                    q = b % 2
                    if b >= 2:
                        sp.wait_ge(s["diff_done"], g * PAIRS + (b - 1) * BATCH)
                    sp.dma_start(mov[0:R_MOV, q].bitcast(F32), mov_rows[b * BATCH:(b + 1) * BATCH].rearrange(
                        "k l b t h s -> (l b) k (t h s)")).then_inc(s[f"rows_in{q}"], 16)
                    sp.dma_start(sta[R_MOV:R_MOV + R_STA, q].bitcast(F32), sta_rows[b * BATCH:(b + 1) * BATCH].rearrange(
                        "k l t h p -> (l t h) k p")).then_inc(s[f"rows_in{q}"], 16)

                def stage(k, q, free):
                    if free:
                        sp.wait_ge(s["pe_ec"], g * PAIRS + k - 1)
                    sp.dma_start(wst[:, q].bitcast(F32), pair_split[bass.ds(k, 1)].squeeze(0)).then_inc(s[f"wst{q}"], 16)
                    sp.dma_start(ecr[:, q].bitcast(F32), ec_rows[bass.ds(k, 1)].rearrange("k l h t -> (k l h) t")
                                 ).then_inc(s[f"wst{q}"], 16)
                sp.wait_ge(s["pe_ec"], g * PAIRS)
                stage(0, 0, False)
                stage(1, 1, False)
                with sp.Fori(1, PAIRS // 2) as j:
                    stage(2 * j, 0, True)
                    stage(2 * j + 1, 1, True)
                sp.wait_ge(s["ln_done"], TILES * (g + 1))
                sp.dma_start(x1g[bass.ds(g, 1)].squeeze(0), xo[:]).then_inc(s["out_st"], 16)
            sp.wait_ge(s["out_st"], 16 * GROUPS)

        @block.gpsimd
        def _(pool):
            pool.memset(mb[:], 0.0).then_inc(s["fill"], 1)
            pool.memset(ones[:], 1.0).then_inc(s["fill"], 1)
            pool.memset(mhalf[:], -0.5).then_inc(s["fill"], 1)
            pool.wait_ge(s["fill"], 3)
            with pool.Fori(0, GROUPS) as g:
                def gdk(k, q, first):
                    pool.wait_ge(s["pool_m"], g * PAIRS + k)
                    if first:
                        pool.wait_ge(s["g_done"], 2 * (g + 1))
                    else:
                        pool.wait_ge(s["dve_m"], g * PAIRS + k - 1)
                    pool.tensor_tensor(gd[:, q], spread(g_sb[:], 2, 2), spread(
                        dd[:, bass.ds(k, 1)].squeeze(1), 1, TILES), ALU.add).then_inc(s["pool_gd"], 1)

                def mk(k, q, first):
                    pool.wait_ge(s["pool_gd"], g * PAIRS + k + 1)
                    pool.wait_ge(s["exp_done"], (g + 1) * PAIRS)
                    if not first:
                        pool.wait_ge(s["pe_intra"], g * PAIRS + k - 1)
                    pool.tensor_tensor(mb[S:P, q, :, :, S:P], e_sb[S:P, bass.ds(k, 1)].squeeze(1),
                                       gd[S:P, q], ALU.mult).then_inc(s["pool_m"], 1)

                last_pair = PAIRS - 1

                def sumsq(k, q):
                    pool.wait_ge(s["act_sq"], g * PAIRS + k + 1)
                    pool.wait_ge(s["pool_sq"], g * PAIRS + k)
                    if k is not last_pair:
                        pool.wait_ge(s["pool_m"], g * PAIRS + k + 2)
                    pool.tensor_tensor(ssq[:], ssq[:], sq[:, q], ALU.add).then_inc(s["pool_sq"], 1)

                pool.wait_ge(s["rs_x"], g + 1)
                pool.tensor_tensor(rstd[:], rstd[:], mhalf[:], ALU.pow).then_inc(s["pool_pow"], 1)
                gdk(0, 0, True)
                mk(0, 0, True)
                gdk(1, 1, True)
                mk(1, 1, True)
                pool.wait_ge(s["act_sq"], g * PAIRS + 1)
                pool.wait_ge(s["pool_m"], g * PAIRS + 2)
                pool.wait_ge(s["sum_pe"], g)
                pool.tensor_tensor(ssq[:], sq[:, 0], ones[:].to_broadcast([P, GT]), ALU.mult).then_inc(s["pool_sq"], 1)
                with pool.Fori(1, PAIRS // 2) as j:
                    for q in range(2):
                        k = 2 * j + q
                        gdk(k, q, False)
                        mk(k, q, False)
                        sumsq(k - 1, 1 - q)
                sumsq(last_pair, 1)
                pool.wait_ge(s["ln_a"], LN_STEPS * g + 1)
                pool.tensor_tensor(ry[:], ry[:], mhalf[:], ALU.pow).then_inc(s["pool_pow"], 1)
                pool.wait_ge(s["var_done"], g + 1)
                pool.tensor_tensor(rl[:], rl[:], mhalf[:], ALU.pow).then_inc(s["pool_pow"], 1)

        @block.scalar
        def _(act):
            act.wait_ge(s["par_in"], 16 * 12)
            act.activation(aux_hi[:], aux_raw, ACT.Copy).then_inc(s["con_act"], 1)
            act.activation(a_neg[:], dtp[:, 1:2], ACT.Exp).then_inc(s["con_act"], 1)
            with act.Fori(0, GROUPS) as g:
                act.wait_ge(s["x_in"], 16 * (g + 1))
                for t in range(TILES):
                    act.activation(xs[:, t], xa[:, t], ACT.Square, accum_out=ss[:, t:t + 1]).then_inc(s["sq_x"], 1)
                act.wait_ge(s["tr_done"], g + 1)
                for kt, bank in ((0, b_xc), (1, b_z)):
                    act.activation(xh[:, kt], bank[:], ACT.Copy, scale=norm_c[:, kt:kt + 1]).then_inc(s["xh_done"], 1)
                act.wait_ge(s["aux_done"], 3 * (g + 1))
                act.activation(b_sb, b_y[:], ACT.Copy).then_inc(s["bc_act"], 1)
                act.activation(c_sb[:], b_xt[:], ACT.Copy).then_inc(s["bc_act"], 1)
                act.wait_ge(s["v_done"], g + 1)
                act.activation(dv[:, 1], dv[:, 0], ACT.Abs).then_inc(s["sp_act"], 1)
                act.wait_ge(s["sp_act"], 3 * g + 1)
                act.activation(dv[:, 1], dv[:, 1], ACT.Exp, scale=-1.0).then_inc(s["sp_act"], 1)
                act.wait_ge(s["sp_act"], 3 * g + 2)
                act.activation(dv[:, 1], dv[:, 1], ACT.Ln, bias=1.0).then_inc(s["sp_act"], 1)
                act.wait_ge(s["cum_done"], g + 1)
                act.activation(ecs, cum[:], ACT.Exp).then_inc(s["ec_act"], 1)
                for k in range(PAIRS):
                    act.wait_ge(s["diff_done"], g * PAIRS + k + 1)
                    act.activation(e_sb[:, k], (b_xc, b_z, b_ch, b_ec)[k % 4][:].rearrange(
                        "p (t h s) -> p t h s", t=TILES, h=2), ACT.Exp).then_inc(s["exp_done"], 1)

                def conv0(k, q, first):
                    act.wait_ge(s["pe_xc"], g * PAIRS + k + 1)
                    if not first:
                        act.wait_ge(s["pe_xt"], g * PAIRS + k - 1)
                    pk = par[:, bass.ds(k, 1)].squeeze(1)
                    act.activation(acc[:, q], b_xc[:], ACT.Identity, scale=pk[:, 3:4],
                                   bias=pk[:, C_CB:C_CB + 1]).then_inc(s["act_conv"], 1)

                def rest(k, q, first):
                    act.wait_ge(s["pe_z"], g * PAIRS + k + 1)
                    if not first:
                        act.wait_ge(s["dve_gate"], g * PAIRS + k - 1)
                    act.activation(sz[:, q], b_z[:], ACT.Silu).then_inc(s["act_z"], 1)
                    act.wait_ge(s["pe_ec"], g * PAIRS + k + 1)
                    if not first:
                        act.wait_ge(s["dve_ce"], g * PAIRS + k - 1)
                    act.activation(eb[:, q], b_ec[:], ACT.Copy).then_inc(s["act_ec"], 1)
                    act.wait_ge(s["pe_xt"], g * PAIRS + k + 1)
                    if not first:
                        act.wait_ge(s["pe_intra"], g * PAIRS + k - 1)
                    act.activation(xt[:, q], b_xt[:].rearrange("p (t c) -> p t c", c=P),
                                   ACT.Silu).then_inc(s["act_xt"], 1)

                def square(k, q, first):
                    act.wait_ge(s["dve_yadd"], g * PAIRS + k + 1)
                    if not first:
                        act.wait_ge(s["pool_sq"], g * PAIRS + k - 1)
                    act.activation(sq[:, q], y[:, q], ACT.Square).then_inc(s["act_sq"], 1)

                conv0(0, 0, True)
                rest(0, 0, True)
                conv0(1, 1, True)
                square(0, 0, True)
                rest(1, 1, True)
                with act.Fori(1, PAIRS // 2) as j:
                    for q in range(2):
                        k = 2 * j + q
                        conv0(k, q, False)
                        square(k - 1, 1 - q, False)
                        rest(k, q, False)
                square(PAIRS - 1, 1, False)

        @block.vector
        def _(dve):
            dve.wait_ge(s["con_act"], 2)
            n_con = [0]

            def const(ins):
                ins.then_inc(s["con"], 1)
                n_con[0] += 1
                dve.wait_ge(s["con"], n_con[0])

            const(dve.tensor_tensor(aux_lo[:], aux_raw, aux_hi[:].bitcast(F32), ALU.subtract))
            const(dve.tensor_scalar(a_neg[:], a_neg[:], -1.0, None, ALU.mult))
            for t in range(TAPS - 1):
                for i in range(TAPS - 1 - t):
                    into = par[:, :, C_EDGE + t] if i == 0 else edge[:]
                    const(dve.tensor_tensor(into, par[:, :, C_W + i], par[:, :, C_CS + t + i], ALU.mult))
                    if i:
                        const(dve.tensor_tensor(par[:, :, C_EDGE + t], par[:, :, C_EDGE + t], edge[:], ALU.add))
            const(dve.tensor_tensor(dd[:].rearrange("p k h s -> p (k h) s"), spread(d_all[:], 2, S),
                                    spread(eye2[:], 1, HEADS), ALU.mult))
            for q in range(2):
                const(dve.tensor_copy(mov[:, q], spread(raw_mov, 1, BATCH)))
                const(dve.tensor_copy(sta[:, q], spread(raw_sta[:], 1, BATCH)))
            const(dve.tensor_copy(ec_sel[:], raw_sel[:]))

            with dve.Fori(0, GROUPS) as g:
                dve.wait_ge(s["sq_x"], TILES * (g + 1))
                dve.tensor_scalar(rstd[:], ss[:], 1.0 / D, RMS_EPS, ALU.mult, ALU.add).then_inc(s["rs_x"], 1)
                dve.wait_ge(s["pool_pow"], 3 * g + 1)
                for t in range(TILES):
                    dve.tensor_scalar(xs[:, t], xa[:, t], rstd[:, t:t + 1], None, ALU.mult).then_inc(s["xs_done"], 1)
                dve.wait_ge(s["xh_done"], KT * (g + 1))
                for kt, bank in ((0, b_xc), (1, b_z)):
                    dve.scalar_tensor_tensor(xl[:, kt], bank[:], norm_c[:, kt:kt + 1], xh[:, kt].bitcast(F32),
                                             ALU.mult, ALU.subtract).then_inc(s["xl_done"], 1)
                dve.wait_ge(s["aux_done"], 3 * (g + 1))
                dve.tensor_scalar(dv[:, 0], b_ch[0:HEADS, :], dtp[:, 0:1], None, ALU.add).then_inc(s["v_done"], 1)
                dve.wait_ge(s["bc_act"], 2 * (g + 1))
                dve.tensor_copy(ch[:], c_sb[:]).then_inc(s["cc_done"], 1)
                dve.wait_ge(s["cc_done"], 2 * g + 1)
                dve.tensor_tensor(cl[:], c_sb[:], ch[:].bitcast(F32), ALU.subtract).then_inc(s["cc_done"], 1)
                dve.wait_ge(s["sp_act"], 3 * (g + 1))
                dve.scalar_tensor_tensor(dv[:, 1], dv[:, 0], 0.0, dv[:, 1], ALU.max, ALU.add).then_inc(s["dt_dve"], 1)
                dve.wait_ge(s["dt_dve"], 2 * g + 1)
                dve.tensor_scalar(dv[:, 0], dv[:, 1], a_neg[:], None, ALU.mult).then_inc(s["dt_dve"], 1)
                dve.wait_ge(s["dt_dve"], 2 * g + 2)
                dve.tensor_tensor_scan(cum[:], reset[:], dv[:, 0], 0.0, ALU.mult, ALU.add).then_inc(s["cum_done"], 1)
                dve.wait_ge(s["cum_done"], g + 1)
                dve.wait_ge(s["rows_out"], 16 * ROW_DMAS * g)
                dve.tensor_copy(rowsr[:, 0], cum[:]).then_inc(s["cum_hl"], 1)
                dve.wait_ge(s["cum_hl"], 2 * g + 1)
                dve.tensor_tensor(rowsr[:, 1], cum[:], rowsr[:, 0].bitcast(F32), ALU.subtract).then_inc(s["cum_hl"], 1)
                dve.wait_ge(s["ec_act"], g + 1)
                dve.tensor_copy(rowsr[:, 2], ecs).then_inc(s["ec_hl"], 1)
                dve.wait_ge(s["ec_hl"], 2 * g + 1)
                dve.tensor_tensor(rowsr[:, 3], ecs, rowsr[:, 2].bitcast(F32), ALU.subtract).then_inc(s["ec_hl"], 1)
                dve.wait_ge(s["g_pe"], g + 1)
                for half in range(2):
                    pr = slice(half * S, half * S + S)
                    dve.tensor_copy(g_sb[pr], b_out[0][pr].rearrange("p (t c) -> p t c", c=P)[:, :, pr]
                                    ).then_inc(s["g_done"], 1)
                dve.wait_ge(s["g_done"], 2 * (g + 1))
                dve.wait_ge(s["exp_done"], (g + 1) * PAIRS)

                def tap(k, q, j):
                    n = g * PAIRS + k
                    a3 = acc[:, q].rearrange("p (b s) -> p b s", s=S)
                    x3 = b_xc[:].rearrange("p (b s) -> p b s", s=S)
                    if j == 1:
                        dve.wait_ge(s["act_conv"], n + 1)
                    else:
                        dve.wait_ge(s["dve_tap"], TAPS * n + j - 1)
                    w = par[:, bass.ds(k, 1)].squeeze(1)[:, TAPS - 1 - j:TAPS - j]
                    dve.scalar_tensor_tensor(a3[:, :, j:S], x3[:, :, 0:S - j], w, a3[:, :, j:S],
                                             ALU.mult, ALU.add).then_inc(s["dve_tap"], 1)

                def front(k, q):
                    a3 = acc[:, q].rearrange("p (b s) -> p b s", s=S)[:, :, 0:TAPS - 1]
                    dve.wait_ge(s["dve_tap"], TAPS * (g * PAIRS + k) + TAPS - 1)
                    dve.tensor_tensor(a3, a3, spread(par[:, bass.ds(k, 1)].squeeze(1)[:, C_EDGE:C_N], 1, 2 * TILES),
                                      ALU.add).then_inc(s["dve_tap"], 1)

                def init_term(k, q):
                    n = g * PAIRS + k
                    dve.wait_ge(s["pe_ch"], n + 1)
                    dve.wait_ge(s["act_ec"], n + 1)
                    dve.tensor_tensor(ce[:, q], b_ch[:], eb[:, q], ALU.mult).then_inc(s["dve_ce"], 1)

                def decay_mat(k, q, first):
                    n = g * PAIRS + k
                    dve.wait_ge(s["pool_gd"], n + 1)
                    if not first:
                        dve.wait_ge(s["pe_intra"], n - 1)
                    dve.tensor_tensor(mb[0:S, q, :, :, 0:S], e_sb[0:S, bass.ds(k, 1)].squeeze(1), gd[0:S, q],
                                      ALU.mult).then_inc(s["dve_m"], 1)

                def add_init(k, q, first):
                    n = g * PAIRS + k
                    dve.wait_ge(s["pe_intra"], n + 1)
                    dve.wait_ge(s["dve_ce"], n + 1)
                    if not first:
                        dve.wait_ge(s["act_sq"], n - 1)
                    dve.tensor_tensor(y[:, q], b_y[:], ce[:, q], ALU.add).then_inc(s["dve_yadd"], 1)

                def gate(k, q, first):
                    n = g * PAIRS + k
                    dve.wait_ge(s["dve_yadd"], n + 1)
                    dve.wait_ge(s["act_z"], n + 1)
                    if not first:
                        dve.wait_ge(s["pe_out"], n - 1)
                    dve.scalar_tensor_tensor(yz[:, q], y[:, q], par[:, bass.ds(k, 1)].squeeze(1)[:, C_IW:C_IW + 1],
                                             sz[:, q], ALU.mult, ALU.mult).then_inc(s["dve_gate"], 1)

                tap(0, 0, 1)
                tap(0, 0, 2)
                tap(0, 0, 3)
                front(0, 0)
                decay_mat(0, 0, True)
                init_term(0, 0)
                tap(1, 1, 1)
                add_init(0, 0, True)
                tap(1, 1, 2)
                gate(0, 0, True)
                tap(1, 1, 3)
                front(1, 1)
                decay_mat(1, 1, True)
                init_term(1, 1)
                with dve.Fori(1, PAIRS // 2) as j:
                    for q in range(2):
                        k = 2 * j + q
                        tap(k, q, 1)
                        add_init(k - 1, 1 - q, False)
                        tap(k, q, 2)
                        gate(k - 1, 1 - q, False)
                        tap(k, q, 3)
                        front(k, q)
                        decay_mat(k, q, False)
                        init_term(k, q)
                add_init(PAIRS - 1, 1, False)
                gate(PAIRS - 1, 1, False)

                dve.wait_ge(s["sum_pe"], g + 1)
                la = 0

                def step(ins):
                    nonlocal la
                    la += 1
                    ins.then_inc(s["ln_a"], 1)

                def upto():
                    dve.wait_ge(s["ln_a"], LN_STEPS * g + la)

                step(dve.tensor_scalar(ry[:], b_y[:, 0:TILES], 1.0 / INNER, RMS_EPS, ALU.mult, ALU.add))
                upto()
                step(dve.tensor_scalar(r1[:], xa[:], 2.0, None, ALU.mult))
                upto()
                dve.wait_ge(s["pool_pow"], 3 * g + 2)
                for t in range(TILES):
                    step(dve.scalar_tensor_tensor(r1[:, t], b_out[t // 2][:, (t % 2) * D:(t % 2) * D + D],
                                                  ry[:, t:t + 1], r1[:, t], ALU.mult, ALU.add))
                upto()
                for t in range(TILES):
                    step(dve.bn_stats(st6[:, t], r1[:, t]))
                upto()
                step(dve.tensor_tensor(mv[:, :, 0], st6[:, :, 1], st6[:, :, 4], ALU.add))
                step(dve.tensor_tensor(mv[:, :, 1], st6[:, :, 1], st6[:, :, 4], ALU.subtract))
                step(dve.tensor_tensor(mv[:, :, 2], st6[:, :, 2], st6[:, :, 5], ALU.add))
                upto()
                step(dve.tensor_scalar(mv[:, :, 0], mv[:, :, 0], 0.5, None, ALU.mult))
                step(dve.tensor_tensor(mv[:, :, 1], mv[:, :, 1], mv[:, :, 1], ALU.mult))
                step(dve.tensor_scalar(mv[:, :, 2], mv[:, :, 2], 1.0 / D, LN_EPS, ALU.mult, ALU.add))
                upto()
                dve.scalar_tensor_tensor(rl[:], mv[:, :, 1], 0.25, mv[:, :, 2], ALU.mult, ALU.add
                                         ).then_inc(s["var_done"], 1)
                dve.wait_ge(s["pool_pow"], 3 * g + 3)
                dve.wait_ge(s["out_st"], 16 * g)
                for t in range(TILES):
                    dve.tensor_scalar(xo[:, t], r1[:, t], mv[:, t, 0:1], rl[:, t:t + 1], ALU.subtract,
                                      ALU.mult).then_inc(s["ln_done"], 1)
                assert la == LN_STEPS

        @block.tensor
        def _(pe):
            def split_mm(out, w, xs_):
                ops = [(wh, xv) for (wh, wl), (xhv, xlv) in zip(w, xs_) for wh, xv in
                       ((wh, xhv), (wh, xlv), (wl, xhv))]
                for i, (a, b) in enumerate(ops):
                    last = pe.matmul(out, a, b, start=i == 0, stop=i == len(ops) - 1)
                return last

            xparts = [(xh[:, kt], xl[:, kt]) for kt in range(KT)]
            pe.wait_ge(s["par_in"], 16 * 12)
            pe.wait_ge(s["con"], CONST_STEPS)
            pe.wait_ge(s["fill"], 3)
            with pe.Fori(0, GROUPS) as g:
                for t in range(TILES):
                    pe.wait_ge(s["xs_done"], TILES * g + t + 1)
                    for kt, bank in ((0, b_xc), (1, b_z)):
                        last = pe.transpose(bank[:, t * P:(t + 1) * P], xs[:, t, kt * P:(kt + 1) * P], ident[:])
                last.then_inc(s["tr_done"], 1)
                pe.wait_ge(s["xl_done"], KT * (g + 1))
                for bank, lo, n in ((b_ch, 2 * N, HEADS), (b_y, 0, N), (b_xt, N, N)):
                    split_mm(bank[0:n, :], [(aux_hi[:, kt, lo:lo + n], aux_lo[:, kt, lo:lo + n]) for kt in range(KT)],
                             xparts).then_inc(s["aux_done"], 1)
                pe.wait_ge(s["bc_act"], 2 * (g + 1))
                pe.wait_ge(s["ln_a"], LN_STEPS * g)
                for t in range(TILES):
                    ts = slice(t * P, (t + 1) * P)
                    last = pe.matmul(b_out[0][:, ts], b_sb[:, ts], c_sb[:, ts], start=True, stop=True)
                last.then_inc(s["g_pe"], 1)
                pe.wait_ge(s["v_done"], g + 1)
                for k in range(PAIRS):
                    b, q = k // BATCH, (k // BATCH) % 2
                    if k % BATCH == 0:
                        pe.wait_ge(s[f"rows_in{q}"], 32 * (g * (PAIRS // BATCH // 2) + b // 2 + 1))
                    if k >= 4:
                        pe.wait_ge(s["exp_done"], g * PAIRS + k - 3)
                    pe.matmul((b_xc, b_z, b_ch, b_ec)[k % 4][:], sta[:, q, k % BATCH], mov[:, q, k % BATCH],
                              start=True, stop=True).then_inc(s["diff_done"], 1)
                pe.wait_ge(s["exp_done"], (g + 1) * PAIRS)
                pe.wait_ge(s["cc_done"], 2 * (g + 1))
                pe.wait_ge(s["g_done"], 2 * (g + 1))

                def wparts(q, which):
                    c = which * KT * P
                    return [(wst[:, q, 0, c + kt * P:c + (kt + 1) * P], wst[:, q, 1, c + kt * P:c + (kt + 1) * P])
                            for kt in range(KT)]

                def proj_x(k, j, q):
                    n = g * PAIRS + k
                    pe.wait_ge(s[f"wst{q}"], 32 * (g * (PAIRS // 2) + j + 1))
                    pe.wait_ge(s["dve_tap"], TAPS * n)
                    split_mm(b_xc[:], wparts(q, 0), xparts).then_inc(s["pe_xc"], 1)

                def proj_rest(k, q):
                    n = g * PAIRS + k
                    pe.wait_ge(s["act_z"], n)
                    split_mm(b_z[:], wparts(q, 1), xparts).then_inc(s["pe_z"], 1)
                    pe.wait_ge(s["dve_ce"], n)
                    c = 2 * KT * P
                    split_mm(b_ch[:], [(wst[:, q, 0, c:c + P], wst[:, q, 1, c:c + P])], [(ch[:], cl[:])]
                             ).then_inc(s["pe_ch"], 1)
                    pe.wait_ge(s["act_ec"], n)
                    pe.matmul(b_ec[:], ec_sel[:], ecr[:, q], start=True, stop=True).then_inc(s["pe_ec"], 1)

                def to_tokens(k, q):
                    n = g * PAIRS + k
                    pe.wait_ge(s["dve_tap"], TAPS * (n + 1))
                    pe.wait_ge(s["act_xt"], n)
                    for t in range(TILES):
                        last = pe.transpose(b_xt[:, t * P:(t + 1) * P], acc[:, q, t * P:(t + 1) * P], ident[:])
                    last.then_inc(s["pe_xt"], 1)

                def intra(k, q):
                    n = g * PAIRS + k
                    pe.wait_ge(s["act_xt"], n + 1)
                    pe.wait_ge(s["dve_m"], n + 1)
                    pe.wait_ge(s["pool_m"], n + 1)
                    pe.wait_ge(s["dve_yadd"], n)
                    for t in range(TILES):
                        for h in range(2):
                            last = pe.matmul(b_y[h * HP:(h + 1) * HP, t * P:(t + 1) * P],
                                             xt[:, q, t, h * HP:(h + 1) * HP], mb[:, q, t, h], start=True, stop=True)
                    last.then_inc(s["pe_intra"], 1)

                def out_proj(k, q, start=False, stop=False):
                    pe.wait_ge(s["dve_gate"], g * PAIRS + k + 1)
                    for t in range(TILES):
                        last = pe.matmul(b_out[t // 2][:, (t % 2) * D:(t % 2) * D + D], yz[:, q, t * P:(t + 1) * P],
                                         wo[:, bass.ds(k, 1)].squeeze(1), start=start and t % 2 == 0, stop=stop,
                                         skip_group_check=True)
                    last.then_inc(s["pe_out"], 1)

                def step(k, j, q, age):
                    proj_x(k, j, q)
                    if age > 0:
                        intra(k - 1, 1 - q)
                    proj_rest(k, q)
                    if age > 1:
                        out_proj(k - 2, q, start=age == 2)
                    to_tokens(k, q)

                step(0, 0, 0, age=0)
                step(1, 0, 1, age=1)
                step(2, 1, 0, age=2)
                step(3, 1, 1, age=3)
                with pe.Fori(2, PAIRS // 2) as j:
                    step(2 * j, j, 0, age=4)
                    step(2 * j + 1, j, 1, age=5)
                intra(PAIRS - 1, 1)
                out_proj(PAIRS - 2, 0)
                out_proj(PAIRS - 1, 1, stop=True)
                pe.wait_ge(s["pool_sq"], (g + 1) * PAIRS)
                pe.wait_ge(s["dve_yadd"], (g + 1) * PAIRS)
                for t in range(TILES):
                    last = pe.matmul(b_y[:, t:t + 1], ssq[:, t * P:(t + 1) * P], ones[:], start=True, stop=True)
                last.then_inc(s["sum_pe"], 1)


X_HEADS, XD, CTX = 32, 8, 128
CT = D // P
NT = TOKENS // P
LN_T = 6
PI2 = 6.283185307179586
PI2_HI = 6.28125
PI2_LO = PI2 - PI2_HI
ROUND = 12582912.0


def cross(nc, x1, ctx_in, pos, wq, wkv, wout, bout, x2, k_ident, k_freq, k_heads, k_ones4):
    x1t = x1.rearrange("(t p) d -> t p d", p=P)
    ctt = ctx_in.rearrange("(t p) d -> t p d", p=P)
    x2t = x2.rearrange("(t p) d -> t p d", p=P)
    with ExitStack() as ctx:
        sb, ps, sem = pools(nc, ctx)
        ident = sb("c_ident", [P, P])
        freq = sb("c_freq", [P, 2])
        heads4 = sb("c_heads4", [P, 4, S])
        ones4 = sb("c_ones4", [P, P])
        mhalf = sb("c_mhalf", [P, 1])
        wq_s = sb("c_wq", [P, KT, D])
        wkv_s = sb("c_wkv", [P, 2 * D])
        wo_s = sb("c_wo", [P, CT, D])
        bo_s = sb("c_bo", [P, D])
        pos_s = sb("c_pos", [P, NT, 2])
        ang = sb("c_ang", [P, NT, 4])
        tmp = sb("c_tmp", [P, NT, 4])
        red = sb("c_red", [P, NT, 4])
        trig = sb("c_trig", [P, 3, NT, 4])
        xin = sb("c_xin", [P, 2, D])
        cin = sb("c_cin", [P, 2, CTX])
        xT = sb("c_xT", [P, 2, 3 * P])
        cdup = sb("c_cdup", [P, 2, 2, 2, S])
        rt = sb("c_rt", [P, 2, 2 * X_HEADS, 4, 2])
        ru = sb("c_ru", [P, 2, 2 * X_HEADS, 4, 2])
        rqk = sb("c_rqk", [P, 2, 2 * D])
        qT = sb("c_qT", [P, 2, CT, P])
        kbd = sb("c_kbd", [P, 2, 2 * CT, 4, S])
        v4 = sb("c_v4", [P, 2, 2, 8, 2, S])
        xb = sb("c_xb", [P, 2, D])
        mx = sb("c_mx", [P, 4, 8])
        pr = sb("c_pr", [P, 4, 8, S])
        pT = sb("c_pT", [P, 4, 4, P])
        rec = sb("c_rec", [P, CT * P])
        aT = sb("c_aT", [P, CT * P])
        r1 = sb("c_r1", [P, D])
        st6 = sb("c_st6", [P, 6])
        mv = sb("c_mv", [P, 3])
        rl = sb("c_rl", [P, 1])
        xo = sb("c_xo", [P, D])
        b_s = [ps(f"c_bank_s{i}") for i in range(4)]
        b_tx, b_qk, b_v, b_t = (ps(f"c_bank_{n}") for n in ("tx", "qk", "v", "t"))

        names = ("par fill trig_dve trig_act in0 in1 t_x act_x act_cd p_qk p_v ropet ropeu ropeu2 rope2 p_t act_q kbd v4 xb "
                 "p_s mx sub ex p_pt pt_act pt_dve p_pv rec at p_out ln lnb var pw xo out").split()
        s = {n: sem("c_" + n) for n in names}
        block = ctx.enter_context(nc.Block())
        N_PAR = 10

        def stages(eng, a, b):
            a(0, 0, True)
            a(1, 1, True)
            b(0, 0, True)
            with eng.Fori(1, NT // 2) as j:
                for q in range(2):
                    i = 2 * j + q
                    a(i, q, False)
                    b(i - 1, 1 - q, False)
            b(NT - 1, 1, False)

        @block.sync
        def _(sp):
            for dst, src in ((ident[:], k_ident), (freq[:], k_freq), (heads4[:], k_heads), (ones4[:], k_ones4),
                             (wq_s[:], wq.rearrange("(k p) n -> p k n", p=P)), (wkv_s[:], wkv),
                             (wo_s[:], wout.rearrange("(k p) n -> p k n", p=P)),
                             (bo_s[:], bout.partition_broadcast(P)),
                             (pos_s[:], pos.rearrange("(t p) a -> p t a", p=P))):
                sp.dma_start(dst, src).then_inc(s["par"], 16)

            def load(i, q, first):
                if not first:
                    sp.wait_ge(s["t_x"], i - 1)
                    sp.wait_ge(s["xb"], i - 1)
                sp.dma_start(xin[:, q], x1t[bass.ds(i, 1)].squeeze(0)).then_inc(s[f"in{q}"], 16)
                sp.dma_start(cin[:, q], ctt[bass.ds(i, 1)].squeeze(0)).then_inc(s[f"in{q}"], 16)

            def store(i, q, first):
                sp.wait_ge(s["xo"], i + 1)
                sp.dma_start(x2t[bass.ds(i, 1)].squeeze(0), xo[:]).then_inc(s["out"], 16)

            stages(sp, load, store)
            sp.wait_ge(s["out"], 16 * NT)

        @block.gpsimd
        def _(pool):
            pool.memset(v4[:], 0.0).then_inc(s["fill"], 1)
            pool.memset(mhalf[:], -0.5).then_inc(s["fill"], 1)
            pool.wait_ge(s["fill"], 2)
            pool.wait_ge(s["par"], 16 * 9)

            def first_half(i, q, first):
                pool.wait_ge(s[f"in{q}"], 16 * 2 * (i - q) // 2 + 32 if isinstance(i, int) else 16 * (i - q) + 32)
                if not first:
                    pool.wait_ge(s["ln"], LN_T * (i - 1))
                pool.tensor_tensor(xb[:, q], xin[:, q], bo_s[:], ALU.add).then_inc(s["xb"], 1)
                pool.wait_ge(s["ropet"], i + 1)
                pool.wait_ge(s["ropeu"], 2 * (i + 1))
                if not first:
                    pool.wait_ge(s["p_t"], i - 1)
                pool.tensor_tensor(rqk[:, q], rt[:, q].rearrange("p h a b -> p (h a b)"),
                                   ru[:, q].rearrange("p h a b -> p (h a b)"), ALU.add).then_inc(s["rope2"], 1)

            def second_half(i, q, first):
                pool.wait_ge(s["var"], i + 1)
                pool.tensor_tensor(rl[:], rl[:], mhalf[:], ALU.pow).then_inc(s["pw"], 1)

            stages(pool, first_half, second_half)

        @block.scalar
        def _(act):
            act.wait_ge(s["trig_dve"], TRIG_STEPS)
            act.activation(trig[:, 1], ang[:], ACT.Sin).then_inc(s["trig_act"], 1)
            act.activation(trig[:, 0], red[:], ACT.Sin).then_inc(s["trig_act"], 1)

            def first_half(i, q, first):
                act.wait_ge(s["t_x"], i + 1)
                if not first:
                    act.wait_ge(s["p_v"], i - 1)
                act.activation(xT[:, q], b_tx[:, 0:3 * P], ACT.Copy).then_inc(s["act_x"], 1)
                act.activation(cdup[:, q], spread(b_tx[:, 2 * P:3 * P].rearrange("p (b k) -> p b k", b=2), 2, 2),
                               ACT.Copy).then_inc(s["act_cd"], 1)
                act.wait_ge(s["kbd"], i + 1)
                if not first:
                    act.wait_ge(s["p_s"], 4 * (i - 1))
                act.activation(qT[:, q], b_t[:, 0:CT * P].rearrange("p (c t) -> p c t", c=CT),
                               ACT.Copy).then_inc(s["act_q"], 1)

            def second_half(i, q, first):
                for r in range(4):
                    act.wait_ge(s["sub"], 4 * i + r + 1)
                    act.activation(pr[:, r], pr[:, r], ACT.Exp, scale=XD ** -0.5).then_inc(s["ex"], 1)
                for r in range(2):
                    act.wait_ge(s["p_pt"], 4 * i + r + 1)
                    if r == 0:
                        act.wait_ge(s["p_pv"], i)
                    act.activation(pT[:, r], b_s[r][:].rearrange("p (n t) -> p n t", t=P),
                                   ACT.Copy).then_inc(s["pt_act"], 1)

            stages(act, first_half, second_half)

        @block.vector
        def _(dve):
            n_trig = [0]

            def trig_step(ins):
                ins.then_inc(s["trig_dve"], 1)
                n_trig[0] += 1
                dve.wait_ge(s["trig_dve"], n_trig[0])

            dve.wait_ge(s["par"], 16 * 9)
            trig_step(dve.tensor_tensor(ang[:].rearrange("p t (a f) -> p (t a) f", f=2),
                                        spread(pos_s[:].rearrange("p t a -> p (t a)"), 2, 2),
                                        spread(freq[:], 1, NT * 2), ALU.mult))
            trig_step(dve.tensor_scalar(red[:], ang[:], PI2 / 4, None, ALU.add))
            for a in (ang, red):
                trig_step(dve.tensor_scalar(tmp[:], a[:], 1.0 / PI2, ROUND, ALU.mult, ALU.add))
                trig_step(dve.tensor_scalar(tmp[:], tmp[:], -ROUND, None, ALU.add))
                for part in (PI2_HI, PI2_LO):
                    trig_step(dve.scalar_tensor_tensor(a[:], tmp[:], -part, a[:], ALU.mult, ALU.add))
            dve.wait_ge(s["trig_act"], 2)
            dve.tensor_scalar(trig[:, 2], trig[:, 1], -1.0, None, ALU.mult).then_inc(s["trig_dve"], 1)
            dve.wait_ge(s["trig_dve"], n_trig[0] + 1)
            assert n_trig[0] == TRIG_STEPS

            def first_half(i, q, first):
                qk = b_qk[:].rearrange("p (h a b) -> p h a b", a=4, b=2)
                tr = [trig[:, n, bass.ds(i, 1)].squeeze(1) for n in range(3)]
                dve.wait_ge(s["p_qk"], i + 1)
                if not first:
                    dve.wait_ge(s["rope2"], i - 1)
                dve.tensor_tensor(rt[:, q], qk, spread(spread(tr[0], 2, 2), 1, 2 * X_HEADS),
                                  ALU.mult).then_inc(s["ropet"], 1)
                for half, t3 in ((0, tr[2]), (1, tr[1])):
                    dve.tensor_tensor(ru[:, q, :, :, half], qk[:, :, :, 1 - half], spread(t3, 1, 2 * X_HEADS),
                                      ALU.mult).then_inc(s["ropeu"], 1)
                dve.wait_ge(s["p_v"], i + 1)
                if not first:
                    dve.wait_ge(s["p_pv"], i - 1)
                for b in range(2):
                    for hp in range(2):
                        h = slice(hp * S, hp * S + S)
                        dve.tensor_copy(v4[h, q, b, :, :, hp * XD:(hp + 1) * XD], b_v[h, b * D:(b + 1) * D].rearrange(
                            "p (g r h d) -> p g r h d", g=8, r=2, h=2)[:, :, :, hp]).then_inc(s["v4"], 1)
                dve.wait_ge(s["p_t"], i + 1)
                if not first:
                    dve.wait_ge(s["p_s"], 4 * (i - 1))
                dve.tensor_tensor(kbd[:, q], spread(b_t[:, CT * P:2 * CT * P].rearrange("p (c k) -> p c k", k=S), 2, 4),
                                  spread(heads4[:], 1, 2 * CT), ALU.mult).then_inc(s["kbd"], 1)

            def second_half(i, q, first):
                for r in range(4):
                    dve.wait_ge(s["p_s"], 4 * i + r + 1)
                    b3 = b_s[r][:].rearrange("p (h k) -> p h k", k=S)
                    dve.tensor_reduce(mx[:, r], b3, AX.X, ALU.max).then_inc(s["mx"], 1)
                    dve.wait_ge(s["mx"], 4 * i + r + 1)
                    dve.wait_ge(s["p_pt"], 4 * i + 0)
                    dve.tensor_tensor(pr[:, r], b3, spread(mx[:, r], 2, S), ALU.subtract).then_inc(s["sub"], 1)
                for r in range(2, 4):
                    dve.wait_ge(s["p_pt"], 4 * i + r + 1)
                    if r == 2:
                        dve.wait_ge(s["p_pv"], i)
                    dve.tensor_copy(pT[:, r], b_s[r][:].rearrange("p (n t) -> p n t", t=P)).then_inc(s["pt_dve"], 1)
                dve.wait_ge(s["p_pv"], i + 1)
                dve.reciprocal(rec[:], b_v[:, CT * P:2 * CT * P]).then_inc(s["rec"], 1)
                dve.wait_ge(s["rec"], i + 1)
                dve.tensor_tensor(aT[:], b_v[:, 0:CT * P], rec[:], ALU.mult).then_inc(s["at"], 1)
                dve.wait_ge(s["p_out"], i + 1)
                dve.tensor_tensor(r1[:], b_tx[:, 0:D], xb[:, q], ALU.add).then_inc(s["ln"], 1)
                layernorm_tile(dve, s, i, r1, st6, mv, rl)
                dve.wait_ge(s["pw"], i + 1)
                dve.wait_ge(s["out"], 16 * i)
                dve.tensor_scalar(xo[:], r1[:], mv[:, 0:1], rl[:], ALU.subtract, ALU.mult).then_inc(s["xo"], 1)

            stages(dve, first_half, second_half)

        @block.tensor
        def _(pe):
            pe.wait_ge(s["par"], 16 * 9)
            pe.wait_ge(s["fill"], 2)

            def first_half(i, q, first):
                pe.wait_ge(s[f"in{q}"], 32 if isinstance(i, int) else 16 * (i - q) + 32)
                if not first:
                    pe.wait_ge(s["ln"], LN_T * (i - 1))
                for c in range(CT):
                    pe.transpose(b_tx[:, c * P:(c + 1) * P], xin[:, q, c * P:(c + 1) * P], ident[:])
                pe.transpose(b_tx[:, 2 * P:3 * P], cin[:, q], ident[:]).then_inc(s["t_x"], 1)
                pe.wait_ge(s["act_x"], i + 1)
                if not (isinstance(i, int) and i == 0):
                    pe.wait_ge(s["ropeu"], 2 * i)
                    pe.wait_ge(s["ropet"], i)
                for c in range(KT):
                    pe.matmul(b_qk[:, 0:D], xT[:, q, c * P:(c + 1) * P], wq_s[:, c], start=c == 0, stop=c == KT - 1)
                pe.matmul(b_qk[:, D:2 * D], xT[:, q, 2 * P:3 * P], wkv_s[:, 0:D], start=True, stop=True
                          ).then_inc(s["p_qk"], 1)
                pe.wait_ge(s["act_cd"], i + 1)
                if not (isinstance(i, int) and i == 0):
                    pe.wait_ge(s["v4"], 4 * i)
                if not first:
                    pe.wait_ge(s["at"], i - 1)
                for b in range(2):
                    last = pe.matmul(b_v[:, b * D:(b + 1) * D], cdup[:, q, b].rearrange("p a k -> p (a k)"),
                                     wkv_s[:, D:2 * D], start=True, stop=True)
                last.then_inc(s["p_v"], 1)
                pe.wait_ge(s["rope2"], i + 1)
                if not (isinstance(i, int) and i == 0):
                    pe.wait_ge(s["act_q"], i)
                    pe.wait_ge(s["kbd"], i)
                for c in range(2 * CT):
                    last = pe.transpose(b_t[:, c * P:(c + 1) * P], rqk[:, q, c * P:(c + 1) * P], ident[:])
                last.then_inc(s["p_t"], 1)

            def second_half(i, q, first):
                pe.wait_ge(s["act_q"], i + 1)
                pe.wait_ge(s["kbd"], i + 1)
                if not first:
                    pe.wait_ge(s["pt_act"], 2 * i)
                    pe.wait_ge(s["pt_dve"], 2 * i)
                for r in range(4):
                    rows = slice(32 * r, 32 * r + 32)
                    for c in range(CT):
                        for b in range(2):
                            last = pe.matmul(b_s[r][b * S:(b + 1) * S, c * 4 * S:(c + 1) * 4 * S],
                                             qT[rows, q, c, b * S:(b + 1) * S],
                                             kbd[rows, q, 2 * c + b].rearrange("p a k -> p (a k)"),
                                             start=True, stop=True)
                    last.then_inc(s["p_s"], 1)
                for r in range(4):
                    pe.wait_ge(s["ex"], 4 * i + r + 1)
                    for n in range(4):
                        last = pe.transpose(b_s[r][:, n * P:(n + 1) * P],
                                            pr[:, r, 2 * n:2 * n + 2].rearrange("p h k -> p (h k)"), ident[:])
                    last.then_inc(s["p_pt"], 1)
                pe.wait_ge(s["pt_act"], 2 * (i + 1))
                pe.wait_ge(s["pt_dve"], 2 * (i + 1))
                pe.wait_ge(s["v4"], 4 * (i + 2) if not LASTT[0] else 4 * (i + 1))
                for r in range(4):
                    for c in range(CT):
                        for b in range(2):
                            out = (slice(32 * r, 32 * r + 32), slice(c * P + b * S, c * P + b * S + S))
                            for kind in range(2):
                                for n in range(2):
                                    v = v4[:, q, b, c * 4 + r].rearrange("p a k -> p (a k)") if kind == 0 else ones4[:]
                                    o = out[1] if kind == 0 else slice(out[1].start + CT * P, out[1].stop + CT * P)
                                    last = pe.matmul(b_v[out[0], o], v[:, 48 * n:48 * n + 32],
                                                     pT[:, r, 2 * c + n, b * S:(b + 1) * S], start=n == 0, stop=n == 1)
                last.then_inc(s["p_pv"], 1)
                pe.wait_ge(s["at"], i + 1)
                pe.wait_ge(s["act_cd"], i + 2 if not LASTT[0] else i + 1)
                for c in range(CT):
                    last = pe.matmul(b_tx[:, 0:D], aT[:, c * P:(c + 1) * P], wo_s[:, c], start=c == 0, stop=c == CT - 1)
                last.then_inc(s["p_out"], 1)

            LASTT = [False]
            first_half(0, 0, True)
            first_half(1, 1, True)
            second_half(0, 0, True)
            with pe.Fori(1, NT // 2) as j:
                for q in range(2):
                    i = 2 * j + q
                    first_half(i, q, False)
                    second_half(i - 1, 1 - q, False)
            LASTT[0] = True
            second_half(NT - 1, 1, False)


TRIG_STEPS = 10


def layernorm_tile(dve, s, i, r1, st6, mv, rl):
    n = LN_T * i
    dve.wait_ge(s["ln"], n + 1)
    dve.bn_stats(st6[:], r1[:]).then_inc(s["ln"], 1)
    dve.wait_ge(s["ln"], n + 2)
    dve.tensor_tensor(mv[:, 0:2], st6[:, 1:3], st6[:, 4:6], ALU.add).then_inc(s["ln"], 1)
    dve.tensor_tensor(mv[:, 2:3], st6[:, 1:2], st6[:, 4:5], ALU.subtract).then_inc(s["ln"], 1)
    dve.wait_ge(s["ln"], n + 4)
    dve.tensor_scalar(mv[:, 0:1], mv[:, 0:1], 0.5, None, ALU.mult).then_inc(s["ln"], 1)
    dve.tensor_tensor(mv[:, 2:3], mv[:, 2:3], mv[:, 2:3], ALU.mult).then_inc(s["ln"], 1)
    dve.wait_ge(s["ln"], n + 6)
    dve.tensor_scalar(rl[:], mv[:, 1:2], 1.0 / D, LN_EPS, ALU.mult, ALU.add).then_inc(s["lnb"], 1)
    dve.wait_ge(s["lnb"], i + 1)
    dve.scalar_tensor_tensor(rl[:], mv[:, 2:3], 0.25, rl[:], ALU.mult, ALU.add).then_inc(s["var"], 1)


HID = 704
HC = (HID + P - 1) // P


def ffn(nc, x2, wg, wu, wd, sc, sdown, out, k_ident):
    x2g = x2.rearrange("(g t p) d -> g p t d", p=P, t=TILES)
    og = out.rearrange("(g t p) d -> g p t d", p=P, t=TILES)
    with ExitStack() as ctx:
        sb, ps, sem = pools(nc, ctx)
        ident = sb("f_ident", [P, P])
        raw = sb("f_raw", [P, KT, 2, HID], I32)
        w = sb("f_w", [P, KT, 2, HID])
        raw_d = sb("f_rawdown", [P, HC, D], I32)
        w_d = sb("f_wdown", [P, HC, D])
        scl = sb("f_scl", [P, 2, HC])
        sd = sb("f_sdown", [P, D])
        mhalf = sb("f_mhalf", [P, TILES])
        xin = sb("f_xin", [P, 2, TILES, D])
        xT = sb("f_xT", [P, 2, KT, GT])
        sg = sb("f_sg", [P, 2, GT])
        hid = sb("f_hid", [P, 2, GT])
        r1 = sb("f_r1", [P, TILES, D])
        st6 = sb("f_st6", [P, TILES, 6])
        mv = sb("f_mv", [P, TILES, 3])
        rl = sb("f_rl", [P, TILES])
        xo = sb("f_xo", [P, TILES, D])
        b_t = [ps(f"f_bank_t{i}") for i in range(2)]
        b_g = [ps(f"f_bank_g{i}") for i in range(2)]
        b_u = [ps(f"f_bank_u{i}") for i in range(2)]
        b_o = [ps(f"f_bank_o{i}") for i in range(2)]
        names = "par fill con in0 in1 t_x act_x p_g p_u sg hid p_o ln var pw xo out".split()
        s = {n: sem("f_" + n) for n in names}
        block = ctx.enter_context(nc.Block())
        LN_G = 8 + TILES
        sizes = [min(P, HID - c * P) for c in range(HC)]

        @block.sync
        def _(sp):
            for dst, src in ((ident[:], k_ident), (raw[:, :, 0], wg), (raw[:, :, 1], wu), (raw_d[:], wd),
                             (scl[:], sc), (sd[:], sdown.partition_broadcast(P))):
                sp.dma_start(dst, src).then_inc(s["par"], 16)
            with sp.Fori(0, GROUPS // 2) as j:
                for q in range(2):
                    g = 2 * j + q
                    if q == 0:
                        sp.wait_ge(s["ln"], LN_G * 2 * j)
                    sp.dma_start(xin[:, q], x2g[bass.ds(g, 1)].squeeze(0)).then_inc(s[f"in{q}"], 16)
                for q in range(2):
                    g = 2 * j + q
                    sp.wait_ge(s["xo"], TILES * (g + 1))
                    sp.dma_start(og[bass.ds(g, 1)].squeeze(0), xo[:]).then_inc(s["out"], 16)
            sp.wait_ge(s["out"], 16 * GROUPS)

        @block.gpsimd
        def _(pool):
            pool.memset(mhalf[:], -0.5).then_inc(s["fill"], 1)
            pool.wait_ge(s["fill"], 1)
            pool.wait_ge(s["par"], 16 * 6)
            with pool.Fori(0, GROUPS) as g:
                pool.wait_ge(s["var"], g + 1)
                pool.tensor_tensor(rl[:], rl[:], mhalf[:], ALU.pow).then_inc(s["pw"], 1)

        @block.scalar
        def _(act):
            act.wait_ge(s["par"], 16 * 6)
            with act.Fori(0, GROUPS // 2) as j:
                for q in range(2):
                    g = 2 * j + q
                    act.wait_ge(s["t_x"], g + 1)
                    for kt in range(KT):
                        act.activation(xT[:, q, kt], b_t[kt][:], ACT.Copy).then_inc(s["act_x"], 1)
                    for c, n in enumerate(sizes):
                        act.wait_ge(s["p_g"], g * HC + c + 1)
                        if c >= 2:
                            act.wait_ge(s["hid"], g * HC + c - 1)
                        else:
                            act.wait_ge(s["hid"], g * HC)
                        act.activation(sg[0:n, c % 2], b_g[c % 2][0:n, :], ACT.Silu,
                                       scale=scl[0:n, 0, c:c + 1]).then_inc(s["sg"], 1)

        @block.vector
        def _(dve):
            dve.wait_ge(s["par"], 16 * 6)
            dve.tensor_scalar(w[:], raw[:], -128.0, None, ALU.add).then_inc(s["con"], 1)
            dve.tensor_scalar(w_d[:], raw_d[:], -128.0, None, ALU.add).then_inc(s["con"], 1)
            dve.wait_ge(s["con"], 2)
            dve.tensor_tensor(w_d[:], w_d[:], spread(sd[:], 1, HC), ALU.mult).then_inc(s["con"], 1)
            with dve.Fori(0, GROUPS // 2) as j:
                for q in range(2):
                    g = 2 * j + q
                    for c, n in enumerate(sizes):
                        dve.wait_ge(s["p_u"], g * HC + c + 1)
                        dve.wait_ge(s["sg"], g * HC + c + 1)
                        if c >= 2:
                            dve.wait_ge(s["p_o"], g * HC + c - 1)
                        else:
                            dve.wait_ge(s["p_o"], g * HC)
                        dve.scalar_tensor_tensor(hid[0:n, c % 2], b_u[c % 2][0:n, :], scl[0:n, 1, c:c + 1],
                                                 sg[0:n, c % 2], ALU.mult, ALU.mult).then_inc(s["hid"], 1)
                    la = 0

                    def step(ins):
                        nonlocal la
                        la += 1
                        ins.then_inc(s["ln"], 1)

                    def upto():
                        dve.wait_ge(s["ln"], LN_G * g + la)

                    dve.wait_ge(s["p_o"], g * HC + HC)
                    for half in range(2):
                        h = slice(2 * half, 2 * half + 2)
                        step(dve.tensor_tensor(r1[:, h], b_o[half][:].rearrange("p (t d) -> p t d", d=D),
                                               xin[:, q, h], ALU.add))
                    upto()
                    for t in range(TILES):
                        step(dve.bn_stats(st6[:, t], r1[:, t]))
                    upto()
                    step(dve.tensor_tensor(mv[:, :, 0], st6[:, :, 1], st6[:, :, 4], ALU.add))
                    step(dve.tensor_tensor(mv[:, :, 1], st6[:, :, 1], st6[:, :, 4], ALU.subtract))
                    step(dve.tensor_tensor(mv[:, :, 2], st6[:, :, 2], st6[:, :, 5], ALU.add))
                    upto()
                    step(dve.tensor_scalar(mv[:, :, 0], mv[:, :, 0], 0.5, None, ALU.mult))
                    step(dve.tensor_tensor(mv[:, :, 1], mv[:, :, 1], mv[:, :, 1], ALU.mult))
                    step(dve.tensor_scalar(mv[:, :, 2], mv[:, :, 2], 1.0 / D, LN_EPS, ALU.mult, ALU.add))
                    upto()
                    dve.scalar_tensor_tensor(rl[:], mv[:, :, 1], 0.25, mv[:, :, 2], ALU.mult, ALU.add
                                             ).then_inc(s["var"], 1)
                    dve.wait_ge(s["pw"], g + 1)
                    dve.wait_ge(s["out"], 16 * g)
                    for t in range(TILES):
                        last = dve.tensor_scalar(xo[:, t], r1[:, t], mv[:, t, 0:1], rl[:, t:t + 1], ALU.subtract,
                                                 ALU.mult).then_inc(s["xo"], 1)
                    assert la == LN_G

        @block.tensor
        def _(pe):
            pe.wait_ge(s["par"], 16 * 6)
            pe.wait_ge(s["con"], 3)
            with pe.Fori(0, GROUPS // 2) as j:
                for q in range(2):
                    g = 2 * j + q
                    pe.wait_ge(s[f"in{q}"], 16 * (j + 1))
                    pe.wait_ge(s["act_x"], KT * g)
                    for t in range(TILES):
                        for kt in range(KT):
                            last = pe.transpose(b_t[kt][:, t * P:(t + 1) * P], xin[:, q, t, kt * P:(kt + 1) * P],
                                                ident[:])
                    last.then_inc(s["t_x"], 1)
                    pe.wait_ge(s["act_x"], KT * (g + 1))
                    for c in range(HC + 1):
                        if c < HC:
                            n = sizes[c]
                            pe.wait_ge(s["sg"], g * HC + max(c - 1, 0))
                            pe.wait_ge(s["hid"], g * HC + max(c - 1, 0))
                            for u, bank, name in ((0, b_g, "p_g"), (1, b_u, "p_u")):
                                for kt in range(KT):
                                    last = pe.matmul(bank[c % 2][0:n, :], w[:, kt, u, c * P:c * P + n], xT[:, q, kt],
                                                     start=kt == 0, stop=kt == KT - 1)
                                last.then_inc(s[name], 1)
                        if c >= 1:
                            n = sizes[c - 1]
                            pe.wait_ge(s["hid"], g * HC + c)
                            if c == 1:
                                pe.wait_ge(s["ln"], LN_G * g)
                            for t in range(TILES):
                                last = pe.matmul(b_o[t // 2][:, (t % 2) * D:(t % 2) * D + D],
                                                 hid[0:n, (c - 1) % 2, t * P:(t + 1) * P], w_d[0:n, c - 1],
                                                 start=c == 1 and t % 2 == 0, stop=c == HC, skip_group_check=True)
                            last.then_inc(s["p_o"], 1)


_SCRATCH = {"pair_split": (PAIRS, P, 2, 5 * P), "mov_rows": (PAIRS, 2, 2, TILES, 2, S),
            "sta_rows": (PAIRS, 2, TILES, 2, P), "ec_rows": (PAIRS, 2, 2, GT),
            "x1": (TOKENS, D), "x2": (TOKENS, D)}


def constants(np):
    r, col = np.arange(R_ALL)[:, None], np.arange(GT)[None]
    mask_row = r - R_MOV - R_STA
    mov = np.where(((r - R_MOV) % 8 == col // S) & (r >= R_MOV) & (mask_row < 0), -1.0, 0.0)
    mov = np.where((mask_row >= 0) & (mask_row > col % S), -1e30, mov)
    p = np.arange(P)[None]
    sta = np.where((r < R_MOV) & (r % 2 == p // S), 1.0, 0.0)
    sta = np.where((mask_row >= 0) & (mask_row == p % S), 1.0, sta)
    pc = np.arange(P)[:, None]
    own = (np.arange(P)[None] % S) // XD == pc // S
    consts = {
        "k_ident": np.eye(P), "k_eye2": np.tile(np.eye(S), (2, 1)),
        "k_reset": np.tile((np.arange(GT) % S != 0) * 1.0, (HEADS, 1)),
        "k_mov": mov, "k_sta": sta,
        "k_sel": (np.arange(4)[:, None] % 2 == p // HP) * 1.0,
        "k_freq": np.tile([[1.0, 10000.0 ** -0.5]], (P, 1)),
        "k_heads": np.repeat((pc % 32 // XD == np.arange(4)[None]) * 1.0, S, axis=1).reshape(P, 4, S),
        "k_ones4": own * 1.0,
    }
    return {k: np.ascontiguousarray(v, np.float32) for k, v in consts.items()}


def arrange(np, i):
    w = i["L0_attn_in_proj_w"]
    wz, wx = w[:INNER], w[INNER:2 * INNER]
    wb, wc, wd = np.split(w[2 * INNER:], [N, 2 * N])
    order = np.concatenate([np.arange(0, HEADS, 2), np.arange(1, HEADS, 2)])

    def pair_major(m):
        return m.reshape(PAIRS, P, KT, P).transpose(0, 3, 2, 1).reshape(PAIRS, P, KT * P)

    def padded(m):
        return np.concatenate([m, np.zeros((HC * P - HID,) + m.shape[1:], m.dtype)])

    h0 = i["L0_attn_ssm_state"][0].reshape(PAIRS, 2, N, HP).transpose(0, 2, 1, 3).reshape(PAIRS, N, P)
    chan = np.concatenate([i["L0_attn_conv_w"], i["L0_attn_conv_b"][:, None], i["L0_attn_inner_norm_w"][:, None],
                           i["L0_attn_conv_state"][0]], axis=1)
    out = {
        "x": i["x"].reshape(TOKENS, D),
        "pair_w": np.concatenate([pair_major(wx), pair_major(wz), h0], axis=2),
        "aux_w": np.concatenate([wb, wc, wd[order]]).T.reshape(KT, P, AUX).transpose(1, 0, 2),
        "dt_par": np.stack([i["L0_attn_dt_bias"][order], i["L0_attn_A_log"][order]], axis=1),
        "chan_par": chan.reshape(PAIRS, P, C_EDGE).transpose(1, 0, 2),
        "d_rows": i["L0_attn_D_param"],
        "norm_w": i["L0_attn_norm_w"].reshape(KT, P).T,
        "wout": i["L0_attn_out_proj_w"].T.reshape(PAIRS, P, D).transpose(1, 0, 2),
        "ctx": i["ctx_1024"].reshape(TOKENS, CTX),
        "pos": i["fside_BxSx2_0"].reshape(TOKENS, 2),
        "x_wq": i["L0_xattn_Wq"], "x_wkv": i["L0_xattn_Wkv"], "x_wout": i["L0_xattn_Wout"], "x_bout": i["L0_xattn_bout"],
        "f_wg": i["L0_ffn_wq_gate"].T.reshape(KT, P, HID).transpose(1, 0, 2),
        "f_wu": i["L0_ffn_wq_up"].T.reshape(KT, P, HID).transpose(1, 0, 2),
        "f_wd": padded(i["L0_ffn_wq_down"].T).reshape(HC, P, D).transpose(1, 0, 2),
        "f_sc": np.stack([padded(i["L0_ffn_s_gate"]), padded(i["L0_ffn_s_up"])]).reshape(2, HC, P).transpose(2, 0, 1),
        "f_sd": i["L0_ffn_s_down"],
    }
    return {k: np.ascontiguousarray(v) for k, v in out.items()}


def program(nc, d, out):
    setup_weights(nc, d["pair_w"], d["pair_split"])
    mixer(nc, d["x"], d["pair_split"], d["aux_w"], d["dt_par"], d["chan_par"], d["d_rows"], d["norm_w"], d["wout"],
          d["x1"], d["mov_rows"], d["sta_rows"], d["ec_rows"],
          d["k_ident"], d["k_eye2"], d["k_reset"], d["k_mov"], d["k_sta"], d["k_sel"])
    cross(nc, d["x1"], d["ctx"], d["pos"], d["x_wq"], d["x_wkv"], d["x_wout"], d["x_bout"], d["x2"],
          d["k_ident"], d["k_freq"], d["k_heads"], d["k_ones4"])
    ffn(nc, d["x2"], d["f_wg"], d["f_wu"], d["f_wd"], d["f_sc"], d["f_sd"], out, d["k_ident"])


def kernel(**inputs):
    import numpy as np
    import concourse.bacc as bacc
    from concourse.bass_utils import run_bass_kernel_spmd

    nc = bacc.Bacc("TRN2", target_bir_lowering=False, num_devices=1)
    arrays = {**arrange(np, {k: np.asarray(v) for k, v in inputs.items()}), **constants(np)}
    d = {k: nc.dram_tensor(k, v.shape, mybir.dt.from_np(v.dtype), kind="ExternalInput").ap() for k, v in arrays.items()}
    d.update({k: nc.dram_tensor(k, shape, F32).ap() for k, shape in _SCRATCH.items()})
    out = nc.dram_tensor("out", (TOKENS, D), F32, kind="ExternalOutput").ap()
    program(nc, d, out)
    r = run_bass_kernel_spmd(nc, [arrays], core_ids=[0])
    return r.results[0]["out"].reshape(SEQS, S, D)
```

```python
import concourse.bass as bass
from concourse import mybir
from contextlib import ExitStack

F32 = mybir.dt.float32
F32R = mybir.dt.float32r
I32 = mybir.dt.int32
ALU = mybir.AluOpType
ACT = mybir.ActivationFunctionType
AX = mybir.AxisListType

P = 128
SEQS, S, D = 64, 64, 256
TOKENS = SEQS * S
KT = D // P
GT = 512
GROUPS = TOKENS // GT
TILES = GT // P
HEADS, HP, N = 48, 64, 128
INNER = HEADS * HP
PAIRS = HEADS // 2
TAPS = 4
BATCH = 3
RMS_EPS = 1e-5
LN_EPS = 1e-5
R_MOV, R_STA = 4, 16
R_ALL = R_MOV + R_STA + S
C_W, C_CB, C_IW, C_CS, C_EDGE, C_N = 0, 4, 5, 6, 9, 12
ROW_DMAS = 16
LN_STEPS = 8 + 2 * TILES
CONST_STEPS = 2 + 9 + 1 + 4 + 1
AUX = 2 * N + HEADS


def pools(nc, ctx):
    def sb(name, shape, dt=F32):
        return ctx.enter_context(nc.sbuf_tensor(name, shape, dt))

    def ps(name, shape=(P, 512)):
        return ctx.enter_context(nc.psum_tensor(name, list(shape), F32))

    def sem(name):
        return ctx.enter_context(nc.semaphore(name))

    return sb, ps, sem


def spread(ap, axis, n):
    ap = ap.unsqueeze(axis)
    shape = list(ap.shape)
    shape[axis] = n
    return ap.to_broadcast(shape)


def setup_weights(nc, pair_w, pair_split):
    cols = pair_w.shape[2]
    with ExitStack() as ctx:
        sb, ps, sem = pools(nc, ctx)
        raw = sb("raw", [P, 2, cols])
        hl = sb("hl", [P, 2, 2, cols], F32R)
        raw_in = [sem("raw_in0"), sem("raw_in1")]
        hl_out = [sem("hl_out0"), sem("hl_out1")]
        hi_done, lo_done = sem("hi_done"), sem("lo_done")
        block = ctx.enter_context(nc.Block())

        @block.sync
        def _(sp):
            for k in range(PAIRS):
                q = k % 2
                if k >= 2:
                    sp.wait_ge(lo_done, k - 1)
                sp.dma_start(raw[:, q, :], pair_w[k]).then_inc(raw_in[q], 16)
                if k >= 1:
                    sp.wait_ge(lo_done, k)
                    sp.dma_start(pair_split[k - 1], hl[:, 1 - q].bitcast(F32)).then_inc(hl_out[1 - q], 16)
            sp.wait_ge(lo_done, PAIRS)
            sp.dma_start(pair_split[PAIRS - 1], hl[:, 1].bitcast(F32)).then_inc(hl_out[1], 16)
            sp.wait_ge(hl_out[0], 16 * (PAIRS // 2))
            sp.wait_ge(hl_out[1], 16 * (PAIRS // 2))

        @block.scalar
        def _(act):
            for k in range(PAIRS):
                q = k % 2
                act.wait_ge(raw_in[q], 16 * (k // 2 + 1))
                if k >= 2:
                    act.wait_ge(hl_out[q], 16 * (k // 2))
                act.activation(hl[:, q, 0, :], raw[:, q, :], ACT.Copy).then_inc(hi_done, 1)

        @block.vector
        def _(dve):
            for k in range(PAIRS):
                q = k % 2
                dve.wait_ge(hi_done, k + 1)
                dve.tensor_tensor(hl[:, q, 1, :], raw[:, q, :], hl[:, q, 0, :].bitcast(F32),
                                  ALU.subtract).then_inc(lo_done, 1)


def mixer(nc, x, pair_split, aux_w, dt_par, chan_par, d_rows, norm_w, wout, x1,
          mov_rows, sta_rows, ec_rows,
          k_ident, k_eye2, k_reset, k_mov, k_sta, k_sel):
    xg = x.rearrange("(g t p) d -> g p t d", p=P, t=TILES)
    x1g = x1.rearrange("(g t p) d -> g p t d", p=P, t=TILES)
    with ExitStack() as ctx:
        sb, ps, sem = pools(nc, ctx)
        ident = sb("ident", [P, P])
        ones = sb("ones", [P, 1])
        reset = sb("reset", [HEADS, GT])
        norm_c = sb("norm_c", [P, KT])
        aux_hi = sb("aux_hi", [P, KT, AUX], F32R)
        aux_lo = sb("aux_lo", [P, KT, AUX], F32R)
        dtp = sb("dtp", [HEADS, 2])
        a_neg = sb("a_neg", [HEADS, 1])
        par = sb("par", [P, PAIRS, C_N])
        dd = sb("dd", [P, PAIRS, 2, S])
        wo = sb("wo", [P, PAIRS, D])
        mov = sb("mov", [R_ALL, 2, BATCH, GT], F32R)
        sta = sb("sta", [R_ALL, 2, BATCH, P], F32R)
        raw_sta = sb("raw_sta", [R_ALL, P])
        raw_sel = sb("raw_sel", [4, P])
        ec_sel = sb("ec_sel", [4, P], F32R)
        eye2 = sb("eye2", [P, S])
        d_all = sb("d_all", [P, HEADS])
        edge = sb("edge", [P, PAIRS])
        xa = sb("xa", [P, TILES, D])
        mhalf = sb("mhalf", [P, TILES])
        ss = sb("ss", [P, TILES])
        rstd = sb("rstd", [P, TILES])
        xs = sb("xs", [P, TILES, D])
        xh = sb("xh", [P, KT, GT], F32R)
        xl = sb("xl", [P, KT, GT], F32R)
        c_sb = sb("c_sb", [P, GT])
        ch = sb("ch", [P, GT], F32R)
        cl = sb("cl", [P, GT], F32R)
        cum = sb("cum", [HEADS, GT])
        rowsr = sb("rowsr", [HEADS, 4, GT], F32R)
        g_sb = sb("g_sb", [P, TILES, S])
        e_sb = sb("e_sb", [P, PAIRS, TILES, 2, S])
        wst = sb("wst", [P, 2, 2, 5 * P], F32R)
        ecr = sb("ecr", [4, 2, GT], F32R)
        gd = sb("gd", [P, 2, TILES, 2, S])
        mb = sb("mb", [P, 2, TILES, 2, P])
        acc = sb("acc", [P, 2, GT])
        xt = sb("xt", [P, 2, TILES, P])
        sz = sb("sz", [P, 2, GT])
        eb = sb("eb", [P, 2, GT])
        ce = sb("ce", [P, 2, GT])
        y = sb("y", [P, 2, GT])
        yz = sb("yz", [P, 2, GT])
        sq = sb("sq", [P, 2, GT])
        ssq = sb("ssq", [P, GT])
        raw_mov = acc[0:R_ALL, 0]
        aux_raw = ce[:].rearrange("p a b -> p (a b)")[:, 0:KT * AUX].rearrange("p (k c) -> p k c", k=KT)
        b_sb = y[:, 0]
        dv = sq[0:HEADS]
        ecs = yz[0:HEADS, 0]
        ry = sb("ry", [P, TILES])
        r1 = xs
        st6 = sb("st6", [P, TILES, 6])
        mv = sb("mv", [P, TILES, 3])
        rl = sb("rl", [P, TILES])
        xo = sb("xo", [P, TILES, D])

        b_xc, b_z, b_ch, b_ec, b_xt, b_y = (ps(f"bank_{n}") for n in ("xc", "z", "ch", "ec", "xt", "y"))
        b_out = [ps("bank_out0"), ps("bank_out1")]

        names = ("par_in fill con con_act x_in sq_x rs_x xs_done tr_done xh_done xl_done aux_done "
                 "bc_act cc_done v_done dt_dve sp_act cum_done cum_hl ec_hl ec_act rows_out g_pe g_done "
                 "rows_in0 rows_in1 diff_done exp_done "
                 "wst0 wst1 pe_xc pe_z pe_ch pe_ec pe_xt pe_intra pe_out "
                 "act_conv act_ec act_z act_xt act_sq dve_tap dve_ce dve_m dve_yadd dve_gate "
                 "pool_gd pool_m pool_sq pool_pow var_done sum_pe r_done ln_a ln_done out_st").split()
        s = {n: sem("m_" + n) for n in names}
        block = ctx.enter_context(nc.Block())

        @block.sync
        def _(sp):
            for dst, src in ((norm_c[:], norm_w), (aux_raw, aux_w), (dtp[:], dt_par),
                             (par[:, :, 0:C_EDGE], chan_par), (wo[:], wout),
                             (d_all[:], d_rows.partition_broadcast(P)), (ident[:], k_ident),
                             (eye2[:], k_eye2), (reset[:], k_reset), (raw_mov, k_mov), (raw_sta[:], k_sta),
                             (raw_sel[:], k_sel)):
                sp.dma_start(dst, src).then_inc(s["par_in"], 16)
            with sp.Fori(0, GROUPS) as g:
                sp.wait_ge(s["ln_a"], LN_STEPS * g)
                sp.dma_start(xa[:], xg[bass.ds(g, 1)].squeeze(0)).then_inc(s["x_in"], 16)
                sp.wait_ge(s["cum_hl"], 2 * (g + 1))
                for hl in range(2):
                    for hh in range(2):
                        src = rowsr[hh * PAIRS:(hh + 1) * PAIRS].bitcast(F32)
                        for b in range(2):
                            sp.dma_start(mov_rows[:, hl, b, :, hh, :], src[:, hl].rearrange(
                                "k (t b s) -> k t b s", b=2, s=S)[:, :, b]).then_inc(s["rows_out"], 16)
                        sp.dma_start(sta_rows[:, hl, :, hh, :],
                                     src[:, hl].rearrange("k (t p) -> k t p", p=P)).then_inc(s["rows_out"], 16)
                sp.wait_ge(s["ec_hl"], 2 * (g + 1))
                for hl in range(2):
                    for hh in range(2):
                        sp.dma_start(ec_rows[:, hl, hh, :],
                                     rowsr[hh * PAIRS:(hh + 1) * PAIRS, 2 + hl].bitcast(F32)).then_inc(s["rows_out"], 16)
                sp.wait_ge(s["rows_out"], 16 * ROW_DMAS * (g + 1))
                for b in range(PAIRS // BATCH):
                    q = b % 2
                    if b >= 2:
                        sp.wait_ge(s["diff_done"], g * PAIRS + (b - 1) * BATCH)
                    sp.dma_start(mov[0:R_MOV, q].bitcast(F32), mov_rows[b * BATCH:(b + 1) * BATCH].rearrange(
                        "k l b t h s -> (l b) k (t h s)")).then_inc(s[f"rows_in{q}"], 16)
                    sp.dma_start(sta[R_MOV:R_MOV + R_STA, q].bitcast(F32), sta_rows[b * BATCH:(b + 1) * BATCH].rearrange(
                        "k l t h p -> (l t h) k p")).then_inc(s[f"rows_in{q}"], 16)

                def stage(k, q, free):
                    if free:
                        sp.wait_ge(s["pe_ec"], g * PAIRS + k - 1)
                    sp.dma_start(wst[:, q].bitcast(F32), pair_split[bass.ds(k, 1)].squeeze(0)).then_inc(s[f"wst{q}"], 16)
                    sp.dma_start(ecr[:, q].bitcast(F32), ec_rows[bass.ds(k, 1)].rearrange("k l h t -> (k l h) t")
                                 ).then_inc(s[f"wst{q}"], 16)
                sp.wait_ge(s["pe_ec"], g * PAIRS)
                stage(0, 0, False)
                stage(1, 1, False)
                with sp.Fori(1, PAIRS // 2) as j:
                    stage(2 * j, 0, True)
                    stage(2 * j + 1, 1, True)
                sp.wait_ge(s["ln_done"], TILES * (g + 1))
                sp.dma_start(x1g[bass.ds(g, 1)].squeeze(0), xo[:]).then_inc(s["out_st"], 16)
            sp.wait_ge(s["out_st"], 16 * GROUPS)

        @block.gpsimd
        def _(pool):
            pool.memset(mb[:], 0.0).then_inc(s["fill"], 1)
            pool.memset(ones[:], 1.0).then_inc(s["fill"], 1)
            pool.memset(mhalf[:], -0.5).then_inc(s["fill"], 1)
            pool.wait_ge(s["fill"], 3)
            with pool.Fori(0, GROUPS) as g:
                def gdk(k, q, first):
                    pool.wait_ge(s["pool_m"], g * PAIRS + k)
                    if first:
                        pool.wait_ge(s["g_done"], 2 * (g + 1))
                    else:
                        pool.wait_ge(s["dve_m"], g * PAIRS + k - 1)
                    pool.tensor_tensor(gd[:, q], spread(g_sb[:], 2, 2), spread(
                        dd[:, bass.ds(k, 1)].squeeze(1), 1, TILES), ALU.add).then_inc(s["pool_gd"], 1)

                def mk(k, q, first):
                    pool.wait_ge(s["pool_gd"], g * PAIRS + k + 1)
                    pool.wait_ge(s["exp_done"], (g + 1) * PAIRS)
                    if not first:
                        pool.wait_ge(s["pe_intra"], g * PAIRS + k - 1)
                    pool.tensor_tensor(mb[S:P, q, :, :, S:P], e_sb[S:P, bass.ds(k, 1)].squeeze(1),
                                       gd[S:P, q], ALU.mult).then_inc(s["pool_m"], 1)

                last_pair = PAIRS - 1

                def sumsq(k, q):
                    pool.wait_ge(s["act_sq"], g * PAIRS + k + 1)
                    pool.wait_ge(s["pool_sq"], g * PAIRS + k)
                    if k is not last_pair:
                        pool.wait_ge(s["pool_m"], g * PAIRS + k + 2)
                    pool.tensor_tensor(ssq[:], ssq[:], sq[:, q], ALU.add).then_inc(s["pool_sq"], 1)

                pool.wait_ge(s["rs_x"], g + 1)
                pool.tensor_tensor(rstd[:], rstd[:], mhalf[:], ALU.pow).then_inc(s["pool_pow"], 1)
                gdk(0, 0, True)
                mk(0, 0, True)
                gdk(1, 1, True)
                mk(1, 1, True)
                pool.wait_ge(s["act_sq"], g * PAIRS + 1)
                pool.wait_ge(s["pool_m"], g * PAIRS + 2)
                pool.wait_ge(s["sum_pe"], g)
                pool.tensor_tensor(ssq[:], sq[:, 0], ones[:].to_broadcast([P, GT]), ALU.mult).then_inc(s["pool_sq"], 1)
                with pool.Fori(1, PAIRS // 2) as j:
                    for q in range(2):
                        k = 2 * j + q
                        gdk(k, q, False)
                        mk(k, q, False)
                        sumsq(k - 1, 1 - q)
                sumsq(last_pair, 1)
                pool.wait_ge(s["ln_a"], LN_STEPS * g + 1)
                pool.tensor_tensor(ry[:], ry[:], mhalf[:], ALU.pow).then_inc(s["pool_pow"], 1)
                pool.wait_ge(s["var_done"], g + 1)
                pool.tensor_tensor(rl[:], rl[:], mhalf[:], ALU.pow).then_inc(s["pool_pow"], 1)

        @block.scalar
        def _(act):
            act.wait_ge(s["par_in"], 16 * 12)
            act.activation(aux_hi[:], aux_raw, ACT.Copy).then_inc(s["con_act"], 1)
            act.activation(a_neg[:], dtp[:, 1:2], ACT.Exp).then_inc(s["con_act"], 1)
            with act.Fori(0, GROUPS) as g:
                act.wait_ge(s["x_in"], 16 * (g + 1))
                for t in range(TILES):
                    act.activation(xs[:, t], xa[:, t], ACT.Square, accum_out=ss[:, t:t + 1]).then_inc(s["sq_x"], 1)
                act.wait_ge(s["tr_done"], g + 1)
                for kt, bank in ((0, b_xc), (1, b_z)):
                    act.activation(xh[:, kt], bank[:], ACT.Copy, scale=norm_c[:, kt:kt + 1]).then_inc(s["xh_done"], 1)
                act.wait_ge(s["aux_done"], 3 * (g + 1))
                act.activation(b_sb, b_y[:], ACT.Copy).then_inc(s["bc_act"], 1)
                act.activation(c_sb[:], b_xt[:], ACT.Copy).then_inc(s["bc_act"], 1)
                act.wait_ge(s["v_done"], g + 1)
                act.activation(dv[:, 1], dv[:, 0], ACT.Abs).then_inc(s["sp_act"], 1)
                act.wait_ge(s["sp_act"], 3 * g + 1)
                act.activation(dv[:, 1], dv[:, 1], ACT.Exp, scale=-1.0).then_inc(s["sp_act"], 1)
                act.wait_ge(s["sp_act"], 3 * g + 2)
                act.activation(dv[:, 1], dv[:, 1], ACT.Ln, bias=1.0).then_inc(s["sp_act"], 1)
                act.wait_ge(s["cum_done"], g + 1)
                act.activation(ecs, cum[:], ACT.Exp).then_inc(s["ec_act"], 1)
                for k in range(PAIRS):
                    act.wait_ge(s["diff_done"], g * PAIRS + k + 1)
                    act.activation(e_sb[:, k], (b_xc, b_z, b_ch, b_ec)[k % 4][:].rearrange(
                        "p (t h s) -> p t h s", t=TILES, h=2), ACT.Exp).then_inc(s["exp_done"], 1)

                def conv0(k, q, first):
                    act.wait_ge(s["pe_xc"], g * PAIRS + k + 1)
                    if not first:
                        act.wait_ge(s["pe_xt"], g * PAIRS + k - 1)
                    pk = par[:, bass.ds(k, 1)].squeeze(1)
                    act.activation(acc[:, q], b_xc[:], ACT.Identity, scale=pk[:, 3:4],
                                   bias=pk[:, C_CB:C_CB + 1]).then_inc(s["act_conv"], 1)

                def rest(k, q, first):
                    act.wait_ge(s["pe_z"], g * PAIRS + k + 1)
                    if not first:
                        act.wait_ge(s["dve_gate"], g * PAIRS + k - 1)
                    act.activation(sz[:, q], b_z[:], ACT.Silu).then_inc(s["act_z"], 1)
                    act.wait_ge(s["pe_ec"], g * PAIRS + k + 1)
                    if not first:
                        act.wait_ge(s["dve_ce"], g * PAIRS + k - 1)
                    act.activation(eb[:, q], b_ec[:], ACT.Copy).then_inc(s["act_ec"], 1)
                    act.wait_ge(s["pe_xt"], g * PAIRS + k + 1)
                    if not first:
                        act.wait_ge(s["pe_intra"], g * PAIRS + k - 1)
                    act.activation(xt[:, q], b_xt[:].rearrange("p (t c) -> p t c", c=P),
                                   ACT.Silu).then_inc(s["act_xt"], 1)

                def square(k, q, first):
                    act.wait_ge(s["dve_yadd"], g * PAIRS + k + 1)
                    if not first:
                        act.wait_ge(s["pool_sq"], g * PAIRS + k - 1)
                    act.activation(sq[:, q], y[:, q], ACT.Square).then_inc(s["act_sq"], 1)

                conv0(0, 0, True)
                rest(0, 0, True)
                conv0(1, 1, True)
                square(0, 0, True)
                rest(1, 1, True)
                with act.Fori(1, PAIRS // 2) as j:
                    for q in range(2):
                        k = 2 * j + q
                        conv0(k, q, False)
                        square(k - 1, 1 - q, False)
                        rest(k, q, False)
                square(PAIRS - 1, 1, False)

        @block.vector
        def _(dve):
            dve.wait_ge(s["con_act"], 2)
            n_con = [0]

            def const(ins):
                ins.then_inc(s["con"], 1)
                n_con[0] += 1
                dve.wait_ge(s["con"], n_con[0])

            const(dve.tensor_tensor(aux_lo[:], aux_raw, aux_hi[:].bitcast(F32), ALU.subtract))
            const(dve.tensor_scalar(a_neg[:], a_neg[:], -1.0, None, ALU.mult))
            for t in range(TAPS - 1):
                for i in range(TAPS - 1 - t):
                    into = par[:, :, C_EDGE + t] if i == 0 else edge[:]
                    const(dve.tensor_tensor(into, par[:, :, C_W + i], par[:, :, C_CS + t + i], ALU.mult))
                    if i:
                        const(dve.tensor_tensor(par[:, :, C_EDGE + t], par[:, :, C_EDGE + t], edge[:], ALU.add))
            const(dve.tensor_tensor(dd[:].rearrange("p k h s -> p (k h) s"), spread(d_all[:], 2, S),
                                    spread(eye2[:], 1, HEADS), ALU.mult))
            for q in range(2):
                const(dve.tensor_copy(mov[:, q], spread(raw_mov, 1, BATCH)))
                const(dve.tensor_copy(sta[:, q], spread(raw_sta[:], 1, BATCH)))
            const(dve.tensor_copy(ec_sel[:], raw_sel[:]))

            with dve.Fori(0, GROUPS) as g:
                dve.wait_ge(s["sq_x"], TILES * (g + 1))
                dve.tensor_scalar(rstd[:], ss[:], 1.0 / D, RMS_EPS, ALU.mult, ALU.add).then_inc(s["rs_x"], 1)
                dve.wait_ge(s["pool_pow"], 3 * g + 1)
                for t in range(TILES):
                    dve.tensor_scalar(xs[:, t], xa[:, t], rstd[:, t:t + 1], None, ALU.mult).then_inc(s["xs_done"], 1)
                dve.wait_ge(s["xh_done"], KT * (g + 1))
                for kt, bank in ((0, b_xc), (1, b_z)):
                    dve.scalar_tensor_tensor(xl[:, kt], bank[:], norm_c[:, kt:kt + 1], xh[:, kt].bitcast(F32),
                                             ALU.mult, ALU.subtract).then_inc(s["xl_done"], 1)
                dve.wait_ge(s["aux_done"], 3 * (g + 1))
                dve.tensor_scalar(dv[:, 0], b_ch[0:HEADS, :], dtp[:, 0:1], None, ALU.add).then_inc(s["v_done"], 1)
                dve.wait_ge(s["bc_act"], 2 * (g + 1))
                dve.tensor_copy(ch[:], c_sb[:]).then_inc(s["cc_done"], 1)
                dve.wait_ge(s["cc_done"], 2 * g + 1)
                dve.tensor_tensor(cl[:], c_sb[:], ch[:].bitcast(F32), ALU.subtract).then_inc(s["cc_done"], 1)
                dve.wait_ge(s["sp_act"], 3 * (g + 1))
                dve.scalar_tensor_tensor(dv[:, 1], dv[:, 0], 0.0, dv[:, 1], ALU.max, ALU.add).then_inc(s["dt_dve"], 1)
                dve.wait_ge(s["dt_dve"], 2 * g + 1)
                dve.tensor_scalar(dv[:, 0], dv[:, 1], a_neg[:], None, ALU.mult).then_inc(s["dt_dve"], 1)
                dve.wait_ge(s["dt_dve"], 2 * g + 2)
                dve.tensor_tensor_scan(cum[:], reset[:], dv[:, 0], 0.0, ALU.mult, ALU.add).then_inc(s["cum_done"], 1)
                dve.wait_ge(s["cum_done"], g + 1)
                dve.wait_ge(s["rows_out"], 16 * ROW_DMAS * g)
                dve.tensor_copy(rowsr[:, 0], cum[:]).then_inc(s["cum_hl"], 1)
                dve.wait_ge(s["cum_hl"], 2 * g + 1)
                dve.tensor_tensor(rowsr[:, 1], cum[:], rowsr[:, 0].bitcast(F32), ALU.subtract).then_inc(s["cum_hl"], 1)
                dve.wait_ge(s["ec_act"], g + 1)
                dve.tensor_copy(rowsr[:, 2], ecs).then_inc(s["ec_hl"], 1)
                dve.wait_ge(s["ec_hl"], 2 * g + 1)
                dve.tensor_tensor(rowsr[:, 3], ecs, rowsr[:, 2].bitcast(F32), ALU.subtract).then_inc(s["ec_hl"], 1)
                dve.wait_ge(s["g_pe"], g + 1)
                for half in range(2):
                    pr = slice(half * S, half * S + S)
                    dve.tensor_copy(g_sb[pr], b_out[0][pr].rearrange("p (t c) -> p t c", c=P)[:, :, pr]
                                    ).then_inc(s["g_done"], 1)
                dve.wait_ge(s["g_done"], 2 * (g + 1))
                dve.wait_ge(s["exp_done"], (g + 1) * PAIRS)

                def tap(k, q, j):
                    n = g * PAIRS + k
                    a3 = acc[:, q].rearrange("p (b s) -> p b s", s=S)
                    x3 = b_xc[:].rearrange("p (b s) -> p b s", s=S)
                    if j == 1:
                        dve.wait_ge(s["act_conv"], n + 1)
                    else:
                        dve.wait_ge(s["dve_tap"], TAPS * n + j - 1)
                    w = par[:, bass.ds(k, 1)].squeeze(1)[:, TAPS - 1 - j:TAPS - j]
                    dve.scalar_tensor_tensor(a3[:, :, j:S], x3[:, :, 0:S - j], w, a3[:, :, j:S],
                                             ALU.mult, ALU.add).then_inc(s["dve_tap"], 1)

                def front(k, q):
                    a3 = acc[:, q].rearrange("p (b s) -> p b s", s=S)[:, :, 0:TAPS - 1]
                    dve.wait_ge(s["dve_tap"], TAPS * (g * PAIRS + k) + TAPS - 1)
                    dve.tensor_tensor(a3, a3, spread(par[:, bass.ds(k, 1)].squeeze(1)[:, C_EDGE:C_N], 1, 2 * TILES),
                                      ALU.add).then_inc(s["dve_tap"], 1)

                def init_term(k, q):
                    n = g * PAIRS + k
                    dve.wait_ge(s["pe_ch"], n + 1)
                    dve.wait_ge(s["act_ec"], n + 1)
                    dve.tensor_tensor(ce[:, q], b_ch[:], eb[:, q], ALU.mult).then_inc(s["dve_ce"], 1)

                def decay_mat(k, q, first):
                    n = g * PAIRS + k
                    dve.wait_ge(s["pool_gd"], n + 1)
                    if not first:
                        dve.wait_ge(s["pe_intra"], n - 1)
                    dve.tensor_tensor(mb[0:S, q, :, :, 0:S], e_sb[0:S, bass.ds(k, 1)].squeeze(1), gd[0:S, q],
                                      ALU.mult).then_inc(s["dve_m"], 1)

                def add_init(k, q, first):
                    n = g * PAIRS + k
                    dve.wait_ge(s["pe_intra"], n + 1)
                    dve.wait_ge(s["dve_ce"], n + 1)
                    if not first:
                        dve.wait_ge(s["act_sq"], n - 1)
                    dve.tensor_tensor(y[:, q], b_y[:], ce[:, q], ALU.add).then_inc(s["dve_yadd"], 1)

                def gate(k, q, first):
                    n = g * PAIRS + k
                    dve.wait_ge(s["dve_yadd"], n + 1)
                    dve.wait_ge(s["act_z"], n + 1)
                    if not first:
                        dve.wait_ge(s["pe_out"], n - 1)
                    dve.scalar_tensor_tensor(yz[:, q], y[:, q], par[:, bass.ds(k, 1)].squeeze(1)[:, C_IW:C_IW + 1],
                                             sz[:, q], ALU.mult, ALU.mult).then_inc(s["dve_gate"], 1)

                tap(0, 0, 1)
                tap(0, 0, 2)
                tap(0, 0, 3)
                front(0, 0)
                decay_mat(0, 0, True)
                init_term(0, 0)
                tap(1, 1, 1)
                add_init(0, 0, True)
                tap(1, 1, 2)
                gate(0, 0, True)
                tap(1, 1, 3)
                front(1, 1)
                decay_mat(1, 1, True)
                init_term(1, 1)
                with dve.Fori(1, PAIRS // 2) as j:
                    for q in range(2):
                        k = 2 * j + q
                        tap(k, q, 1)
                        add_init(k - 1, 1 - q, False)
                        tap(k, q, 2)
                        gate(k - 1, 1 - q, False)
                        tap(k, q, 3)
                        front(k, q)
                        decay_mat(k, q, False)
                        init_term(k, q)
                add_init(PAIRS - 1, 1, False)
                gate(PAIRS - 1, 1, False)

                dve.wait_ge(s["sum_pe"], g + 1)
                la = 0

                def step(ins):
                    nonlocal la
                    la += 1
                    ins.then_inc(s["ln_a"], 1)

                def upto():
                    dve.wait_ge(s["ln_a"], LN_STEPS * g + la)

                step(dve.tensor_scalar(ry[:], b_y[:, 0:TILES], 1.0 / INNER, RMS_EPS, ALU.mult, ALU.add))
                upto()
                step(dve.tensor_scalar(r1[:], xa[:], 2.0, None, ALU.mult))
                upto()
                dve.wait_ge(s["pool_pow"], 3 * g + 2)
                for t in range(TILES):
                    step(dve.scalar_tensor_tensor(r1[:, t], b_out[t // 2][:, (t % 2) * D:(t % 2) * D + D],
                                                  ry[:, t:t + 1], r1[:, t], ALU.mult, ALU.add))
                upto()
                for t in range(TILES):
                    step(dve.bn_stats(st6[:, t], r1[:, t]))
                upto()
                step(dve.tensor_tensor(mv[:, :, 0], st6[:, :, 1], st6[:, :, 4], ALU.add))
                step(dve.tensor_tensor(mv[:, :, 1], st6[:, :, 1], st6[:, :, 4], ALU.subtract))
                step(dve.tensor_tensor(mv[:, :, 2], st6[:, :, 2], st6[:, :, 5], ALU.add))
                upto()
                step(dve.tensor_scalar(mv[:, :, 0], mv[:, :, 0], 0.5, None, ALU.mult))
                step(dve.tensor_tensor(mv[:, :, 1], mv[:, :, 1], mv[:, :, 1], ALU.mult))
                step(dve.tensor_scalar(mv[:, :, 2], mv[:, :, 2], 1.0 / D, LN_EPS, ALU.mult, ALU.add))
                upto()
                dve.scalar_tensor_tensor(rl[:], mv[:, :, 1], 0.25, mv[:, :, 2], ALU.mult, ALU.add
                                         ).then_inc(s["var_done"], 1)
                dve.wait_ge(s["pool_pow"], 3 * g + 3)
                dve.wait_ge(s["out_st"], 16 * g)
                for t in range(TILES):
                    dve.tensor_scalar(xo[:, t], r1[:, t], mv[:, t, 0:1], rl[:, t:t + 1], ALU.subtract,
                                      ALU.mult).then_inc(s["ln_done"], 1)
                assert la == LN_STEPS

        @block.tensor
        def _(pe):
            def split_mm(out, w, xs_):
                ops = [(wh, xv) for (wh, wl), (xhv, xlv) in zip(w, xs_) for wh, xv in
                       ((wh, xhv), (wh, xlv), (wl, xhv))]
                for i, (a, b) in enumerate(ops):
                    last = pe.matmul(out, a, b, start=i == 0, stop=i == len(ops) - 1)
                return last

            xparts = [(xh[:, kt], xl[:, kt]) for kt in range(KT)]
            pe.wait_ge(s["par_in"], 16 * 12)
            pe.wait_ge(s["con"], CONST_STEPS)
            pe.wait_ge(s["fill"], 3)
            with pe.Fori(0, GROUPS) as g:
                for t in range(TILES):
                    pe.wait_ge(s["xs_done"], TILES * g + t + 1)
                    for kt, bank in ((0, b_xc), (1, b_z)):
                        last = pe.transpose(bank[:, t * P:(t + 1) * P], xs[:, t, kt * P:(kt + 1) * P], ident[:])
                last.then_inc(s["tr_done"], 1)
                pe.wait_ge(s["xl_done"], KT * (g + 1))
                for bank, lo, n in ((b_ch, 2 * N, HEADS), (b_y, 0, N), (b_xt, N, N)):
                    split_mm(bank[0:n, :], [(aux_hi[:, kt, lo:lo + n], aux_lo[:, kt, lo:lo + n]) for kt in range(KT)],
                             xparts).then_inc(s["aux_done"], 1)
                pe.wait_ge(s["bc_act"], 2 * (g + 1))
                pe.wait_ge(s["ln_a"], LN_STEPS * g)
                for t in range(TILES):
                    ts = slice(t * P, (t + 1) * P)
                    last = pe.matmul(b_out[0][:, ts], b_sb[:, ts], c_sb[:, ts], start=True, stop=True)
                last.then_inc(s["g_pe"], 1)
                pe.wait_ge(s["v_done"], g + 1)
                for k in range(PAIRS):
                    b, q = k // BATCH, (k // BATCH) % 2
                    if k % BATCH == 0:
                        pe.wait_ge(s[f"rows_in{q}"], 32 * (g * (PAIRS // BATCH // 2) + b // 2 + 1))
                    if k >= 4:
                        pe.wait_ge(s["exp_done"], g * PAIRS + k - 3)
                    pe.matmul((b_xc, b_z, b_ch, b_ec)[k % 4][:], sta[:, q, k % BATCH], mov[:, q, k % BATCH],
                              start=True, stop=True).then_inc(s["diff_done"], 1)
                pe.wait_ge(s["exp_done"], (g + 1) * PAIRS)
                pe.wait_ge(s["cc_done"], 2 * (g + 1))
                pe.wait_ge(s["g_done"], 2 * (g + 1))

                def wparts(q, which):
                    c = which * KT * P
                    return [(wst[:, q, 0, c + kt * P:c + (kt + 1) * P], wst[:, q, 1, c + kt * P:c + (kt + 1) * P])
                            for kt in range(KT)]

                def proj_x(k, j, q):
                    n = g * PAIRS + k
                    pe.wait_ge(s[f"wst{q}"], 32 * (g * (PAIRS // 2) + j + 1))
                    pe.wait_ge(s["dve_tap"], TAPS * n)
                    split_mm(b_xc[:], wparts(q, 0), xparts).then_inc(s["pe_xc"], 1)

                def proj_rest(k, q):
                    n = g * PAIRS + k
                    pe.wait_ge(s["act_z"], n)
                    split_mm(b_z[:], wparts(q, 1), xparts).then_inc(s["pe_z"], 1)
                    pe.wait_ge(s["dve_ce"], n)
                    c = 2 * KT * P
                    split_mm(b_ch[:], [(wst[:, q, 0, c:c + P], wst[:, q, 1, c:c + P])], [(ch[:], cl[:])]
                             ).then_inc(s["pe_ch"], 1)
                    pe.wait_ge(s["act_ec"], n)
                    pe.matmul(b_ec[:], ec_sel[:], ecr[:, q], start=True, stop=True).then_inc(s["pe_ec"], 1)

                def to_tokens(k, q):
                    n = g * PAIRS + k
                    pe.wait_ge(s["dve_tap"], TAPS * (n + 1))
                    pe.wait_ge(s["act_xt"], n)
                    for t in range(TILES):
                        last = pe.transpose(b_xt[:, t * P:(t + 1) * P], acc[:, q, t * P:(t + 1) * P], ident[:])
                    last.then_inc(s["pe_xt"], 1)

                def intra(k, q):
                    n = g * PAIRS + k
                    pe.wait_ge(s["act_xt"], n + 1)
                    pe.wait_ge(s["dve_m"], n + 1)
                    pe.wait_ge(s["pool_m"], n + 1)
                    pe.wait_ge(s["dve_yadd"], n)
                    for t in range(TILES):
                        for h in range(2):
                            last = pe.matmul(b_y[h * HP:(h + 1) * HP, t * P:(t + 1) * P],
                                             xt[:, q, t, h * HP:(h + 1) * HP], mb[:, q, t, h], start=True, stop=True)
                    last.then_inc(s["pe_intra"], 1)

                def out_proj(k, q, start=False, stop=False):
                    pe.wait_ge(s["dve_gate"], g * PAIRS + k + 1)
                    for t in range(TILES):
                        last = pe.matmul(b_out[t // 2][:, (t % 2) * D:(t % 2) * D + D], yz[:, q, t * P:(t + 1) * P],
                                         wo[:, bass.ds(k, 1)].squeeze(1), start=start and t % 2 == 0, stop=stop,
                                         skip_group_check=True)
                    last.then_inc(s["pe_out"], 1)

                def step(k, j, q, age):
                    proj_x(k, j, q)
                    if age > 0:
                        intra(k - 1, 1 - q)
                    proj_rest(k, q)
                    if age > 1:
                        out_proj(k - 2, q, start=age == 2)
                    to_tokens(k, q)

                step(0, 0, 0, age=0)
                step(1, 0, 1, age=1)
                step(2, 1, 0, age=2)
                step(3, 1, 1, age=3)
                with pe.Fori(2, PAIRS // 2) as j:
                    step(2 * j, j, 0, age=4)
                    step(2 * j + 1, j, 1, age=5)
                intra(PAIRS - 1, 1)
                out_proj(PAIRS - 2, 0)
                out_proj(PAIRS - 1, 1, stop=True)
                pe.wait_ge(s["pool_sq"], (g + 1) * PAIRS)
                pe.wait_ge(s["dve_yadd"], (g + 1) * PAIRS)
                for t in range(TILES):
                    last = pe.matmul(b_y[:, t:t + 1], ssq[:, t * P:(t + 1) * P], ones[:], start=True, stop=True)
                last.then_inc(s["sum_pe"], 1)


X_HEADS, XD, CTX = 32, 8, 128
CT = D // P
NT = TOKENS // P
PEEL = 4
LN_T = 6
PI2 = 6.283185307179586
PI2_HI = 6.28125
PI2_LO = PI2 - PI2_HI
ROUND = 12582912.0


def cross(nc, x1, ctx_in, pos, wq, wkv, wout, bout, x2, k_ident, k_freq, k_heads, k_ones4):
    x1t = x1.rearrange("(t p) d -> t p d", p=P)
    ctt = ctx_in.rearrange("(t p) d -> t p d", p=P)
    x2t = x2.rearrange("(t p) d -> t p d", p=P)
    with ExitStack() as ctx:
        sb, ps, sem = pools(nc, ctx)
        ident = sb("c_ident", [P, P])
        freq = sb("c_freq", [P, 2])
        heads4 = sb("c_heads4", [P, 4, S])
        ones4 = sb("c_ones4", [P, P])
        mhalf = sb("c_mhalf", [P, 1])
        wq_s = sb("c_wq", [P, KT, D])
        wkv_s = sb("c_wkv", [P, 2 * D])
        wo_s = sb("c_wo", [P, CT, D])
        bo_s = sb("c_bo", [P, D])
        pos_s = sb("c_pos", [P, NT, 2])
        ang = sb("c_ang", [P, NT, 4])
        tmp = sb("c_tmp", [P, NT, 4])
        red = sb("c_red", [P, NT, 4])
        trig = sb("c_trig", [P, 3, NT, 4])
        xin = sb("c_xin", [P, 2, D])
        cin = sb("c_cin", [P, 2, CTX])
        xT = sb("c_xT", [P, 2, 3 * P])
        cdup = sb("c_cdup", [P, 2, 2, 2, S])
        rt = sb("c_rt", [P, 2, 2 * X_HEADS, 4, 2])
        ru = sb("c_ru", [P, 2, 2 * X_HEADS, 4, 2])
        rqk = sb("c_rqk", [P, 2, 2 * D])
        qT = sb("c_qT", [P, 2, CT, P])
        kbd = sb("c_kbd", [P, 2, 2 * CT, 4, S])
        v4 = sb("c_v4", [P, 2, 2, 8, 2, S])
        xb = sb("c_xb", [P, 2, D])
        mx = sb("c_mx", [P, 4, 8])
        pr = sb("c_pr", [P, 4, 8, S])
        pT = sb("c_pT", [P, 4, 4, P])
        rec = sb("c_rec", [P, CT * P])
        aT = sb("c_aT", [P, CT * P])
        r1 = sb("c_r1", [P, D])
        st6 = sb("c_st6", [P, 6])
        mv = sb("c_mv", [P, 3])
        rl = sb("c_rl", [P, 1])
        xo = sb("c_xo", [P, 2, D])
        b_s = [ps(f"c_bank_s{i}") for i in range(4)]
        b_tx, b_qk, b_v, b_t = (ps(f"c_bank_{n}") for n in ("tx", "qk", "v", "t"))

        names = ("par fill trig_dve trig_act in0 in1 t_x act_x act_cd p_qk p_v ropet ropeu ropeu2 rope2 p_t act_q kbd v4 xb "
                 "p_s mx sub ex p_pt pt_act pt_dve p_pv rec at p_out ln lnb var pw xo out0 out1").split()
        s = {n: sem("c_" + n) for n in names}
        block = ctx.enter_context(nc.Block())

        def rounds(eng, body):
            for i in range(PEEL):
                body(i, i, i % 2, True, i >= 1, i >= 2)
            with eng.Fori(PEEL // 2, NT // 2) as j:
                for q in range(2):
                    body(PEEL, 2 * j + q, q, True, True, True)
            body(PEEL, NT, 0, False, True, True)
            body(PEEL, NT + 1, 1, False, False, True)

        @block.sync
        def _(sp):
            for dst, src in ((ident[:], k_ident), (freq[:], k_freq), (heads4[:], k_heads), (ones4[:], k_ones4),
                             (wq_s[:], wq.rearrange("(k p) n -> p k n", p=P)), (wkv_s[:], wkv),
                             (wo_s[:], wout.rearrange("(k p) n -> p k n", p=P)),
                             (bo_s[:], bout.partition_broadcast(P)),
                             (pos_s[:], pos.rearrange("(t p) a -> p t a", p=P))):
                sp.dma_start(dst, src).then_inc(s["par"], 16)

            def store(m, q):
                sp.wait_ge(s["xo"], m + 1)
                sp.dma_start(x2t[bass.ds(m, 1)].squeeze(0), xo[:, q]).then_inc(s[f"out{q}"], 16)

            def body(r, i, q, a, b, c):
                if a:
                    if r >= 2:
                        sp.wait_ge(s["t_x"], i - 1)
                        sp.wait_ge(s["xb"], i - 1)
                    sp.dma_start(xin[:, q], x1t[bass.ds(i, 1)].squeeze(0)).then_inc(s[f"in{q}"], 16)
                    sp.dma_start(cin[:, q], ctt[bass.ds(i, 1)].squeeze(0)).then_inc(s[f"in{q}"], 16)
                if r >= 3:
                    store(i - 3, 1 - q)

            rounds(sp, body)
            store(NT - 1, 1)
            for q in range(2):
                sp.wait_ge(s[f"out{q}"], 16 * (NT // 2))

        @block.gpsimd
        def _(pool):
            pool.memset(v4[:], 0.0).then_inc(s["fill"], 1)
            pool.memset(mhalf[:], -0.5).then_inc(s["fill"], 1)
            pool.wait_ge(s["fill"], 2)
            pool.wait_ge(s["par"], 16 * 9)

            def body(r, i, q, a, b, c):
                if a:
                    pool.wait_ge(s["ropet"], i + 1)
                    pool.wait_ge(s["ropeu"], 2 * (i + 1))
                    if r >= 2:
                        pool.wait_ge(s["p_t"], i - 1)
                    pool.tensor_tensor(rqk[:, q], rt[:, q].rearrange("p h a b -> p (h a b)"),
                                       ru[:, q].rearrange("p h a b -> p (h a b)"), ALU.add).then_inc(s["rope2"], 1)
                if c:
                    pool.wait_ge(s["var"], i - 1)
                    pool.tensor_tensor(rl[:], rl[:], mhalf[:], ALU.pow).then_inc(s["pw"], 1)
                if a:
                    pool.wait_ge(s[f"in{q}"], 16 * (i - q) + 32)
                    if r >= 2:
                        pool.wait_ge(s["ln"], LN_T * (i - 2) + 1)
                    pool.tensor_tensor(xb[:, q], xin[:, q], bo_s[:], ALU.add).then_inc(s["xb"], 1)

            rounds(pool, body)

        @block.scalar
        def _(act):
            act.wait_ge(s["trig_dve"], TRIG_STEPS)
            act.activation(trig[:, 1], ang[:], ACT.Sin).then_inc(s["trig_act"], 1)
            act.activation(trig[:, 0], red[:], ACT.Sin).then_inc(s["trig_act"], 1)

            def body(r, i, q, a, b, c):
                if a:
                    act.wait_ge(s["t_x"], i + 1)
                    if r >= 2:
                        act.wait_ge(s["p_v"], i - 1)
                    act.activation(xT[:, q], b_tx[:, 0:3 * P], ACT.Copy).then_inc(s["act_x"], 1)
                    act.activation(cdup[:, q], spread(b_tx[:, 2 * P:3 * P].rearrange("p (b k) -> p b k", b=2), 2, 2),
                                   ACT.Copy).then_inc(s["act_cd"], 1)
                if b:
                    n = i - 1
                    for r4 in range(4):
                        act.wait_ge(s["sub"], 4 * n + r4 + 1)
                        act.activation(pr[:, r4], pr[:, r4], ACT.Exp, scale=XD ** -0.5).then_inc(s["ex"], 1)
                    for r4 in range(2):
                        act.wait_ge(s["p_pt"], 4 * n + r4 + 1)
                        if r4 == 0 and r >= 2:
                            act.wait_ge(s["p_pv"], n)
                        act.activation(pT[:, r4], b_s[r4][:].rearrange("p (n t) -> p n t", t=P),
                                       ACT.Copy).then_inc(s["pt_act"], 1)
                if a:
                    act.wait_ge(s["kbd"], i + 1)
                    if r >= 2:
                        act.wait_ge(s["p_s"], 4 * (i - 1))
                    act.activation(qT[:, q], b_t[:, 0:CT * P].rearrange("p (c t) -> p c t", c=CT),
                                   ACT.Copy).then_inc(s["act_q"], 1)

            rounds(act, body)

        @block.vector
        def _(dve):
            n_trig = [0]

            def trig_step(ins):
                ins.then_inc(s["trig_dve"], 1)
                n_trig[0] += 1
                dve.wait_ge(s["trig_dve"], n_trig[0])

            dve.wait_ge(s["par"], 16 * 9)
            trig_step(dve.tensor_tensor(ang[:].rearrange("p t (a f) -> p (t a) f", f=2),
                                        spread(pos_s[:].rearrange("p t a -> p (t a)"), 2, 2),
                                        spread(freq[:], 1, NT * 2), ALU.mult))
            trig_step(dve.tensor_scalar(red[:], ang[:], PI2 / 4, None, ALU.add))
            for a in (ang, red):
                trig_step(dve.tensor_scalar(tmp[:], a[:], 1.0 / PI2, ROUND, ALU.mult, ALU.add))
                trig_step(dve.tensor_scalar(tmp[:], tmp[:], -ROUND, None, ALU.add))
                for part in (PI2_HI, PI2_LO):
                    trig_step(dve.scalar_tensor_tensor(a[:], tmp[:], -part, a[:], ALU.mult, ALU.add))
            dve.wait_ge(s["trig_act"], 2)
            dve.tensor_scalar(trig[:, 2], trig[:, 1], -1.0, None, ALU.mult).then_inc(s["trig_dve"], 1)
            dve.wait_ge(s["trig_dve"], n_trig[0] + 1)
            assert n_trig[0] == TRIG_STEPS

            def rope(r, i, q):
                qk = b_qk[:].rearrange("p (h a b) -> p h a b", a=4, b=2)
                tr = [trig[:, n, bass.ds(i, 1)].squeeze(1) for n in range(3)]
                dve.wait_ge(s["p_qk"], i + 1)
                if r >= 2:
                    dve.wait_ge(s["rope2"], i - 1)
                dve.tensor_tensor(rt[:, q], qk, spread(spread(tr[0], 2, 2), 1, 2 * X_HEADS),
                                  ALU.mult).then_inc(s["ropet"], 1)
                for half, t3 in ((0, tr[2]), (1, tr[1])):
                    dve.tensor_tensor(ru[:, q, :, :, half], qk[:, :, :, 1 - half], spread(t3, 1, 2 * X_HEADS),
                                      ALU.mult).then_inc(s["ropeu"], 1)

            def values(r, i, q):
                dve.wait_ge(s["p_v"], i + 1)
                if r >= 2:
                    dve.wait_ge(s["p_pv"], i - 1)
                for b in range(2):
                    for hp in range(2):
                        h = slice(hp * S, hp * S + S)
                        dve.tensor_copy(v4[h, q, b, :, :, hp * XD:(hp + 1) * XD], b_v[h, b * D:(b + 1) * D].rearrange(
                            "p (g r h d) -> p g r h d", g=8, r=2, h=2)[:, :, :, hp]).then_inc(s["v4"], 1)

            def keys(r, i, q):
                dve.wait_ge(s["p_t"], i + 1)
                if r >= 2:
                    dve.wait_ge(s["p_s"], 4 * (i - 1))
                dve.tensor_tensor(kbd[:, q], spread(b_t[:, CT * P:2 * CT * P].rearrange("p (c k) -> p c k", k=S), 2, 4),
                                  spread(heads4[:], 1, 2 * CT), ALU.mult).then_inc(s["kbd"], 1)

            def maxima(r, n):
                def subtract(r4):
                    dve.wait_ge(s["mx"], 4 * n + r4 + 1)
                    if r4 == 0 and r >= 2:
                        dve.wait_ge(s["p_pt"], 4 * n)
                    dve.tensor_tensor(pr[:, r4], b_s[r4][:].rearrange("p (h k) -> p h k", k=S),
                                      spread(mx[:, r4], 2, S), ALU.subtract).then_inc(s["sub"], 1)

                for r4 in range(4):
                    dve.wait_ge(s["p_s"], 4 * n + r4 + 1)
                    dve.tensor_reduce(mx[:, r4], b_s[r4][:].rearrange("p (h k) -> p h k", k=S), AX.X, ALU.max
                                      ).then_inc(s["mx"], 1)
                    if r4 >= 1:
                        subtract(r4 - 1)
                subtract(3)

            def probs_out(r, n):
                for r4 in range(2, 4):
                    dve.wait_ge(s["p_pt"], 4 * n + r4 + 1)
                    if r4 == 2 and r >= 2:
                        dve.wait_ge(s["p_pv"], n)
                    dve.tensor_copy(pT[:, r4], b_s[r4][:].rearrange("p (n t) -> p n t", t=P)).then_inc(s["pt_dve"], 1)

            def normalise(n):
                dve.wait_ge(s["p_pv"], n + 1)
                dve.reciprocal(rec[:], b_v[:, CT * P:2 * CT * P]).then_inc(s["rec"], 1)
                dve.wait_ge(s["rec"], n + 1)
                dve.tensor_tensor(aT[:], b_v[:, 0:CT * P], rec[:], ALU.mult).then_inc(s["at"], 1)

            def finish(r, m, q):
                dve.wait_ge(s["p_out"], m + 1)
                dve.tensor_tensor(r1[:], b_tx[:, 0:D], xb[:, q], ALU.add).then_inc(s["ln"], 1)
                layernorm_tile(dve, s, m, r1, st6, mv, rl)
                dve.wait_ge(s["pw"], m + 1)
                if r >= 4:
                    dve.wait_ge(s[f"out{q}"], 8 * (m - q))
                dve.tensor_scalar(xo[:, q], r1[:], mv[:, 0:1], rl[:], ALU.subtract, ALU.mult).then_inc(s["xo"], 1)

            def body(r, i, q, a, b, c):
                if b:
                    maxima(r, i - 1)
                if a:
                    rope(r, i, q)
                    values(r, i, q)
                if b:
                    probs_out(r, i - 1)
                if a:
                    keys(r, i, q)
                if c:
                    finish(r, i - 2, q)
                if b:
                    normalise(i - 1)

            rounds(dve, body)

        @block.tensor
        def _(pe):
            pe.wait_ge(s["par"], 16 * 9)
            pe.wait_ge(s["fill"], 2)

            def transpose_in(r, i, q):
                pe.wait_ge(s[f"in{q}"], 16 * (i - q) + 32)
                if r >= 3:
                    pe.wait_ge(s["ln"], LN_T * (i - 3) + 1)
                for c in range(CT):
                    pe.transpose(b_tx[:, c * P:(c + 1) * P], xin[:, q, c * P:(c + 1) * P], ident[:])
                pe.transpose(b_tx[:, 2 * P:3 * P], cin[:, q], ident[:]).then_inc(s["t_x"], 1)

            def scores(r, n, q):
                pe.wait_ge(s["act_q"], n + 1)
                pe.wait_ge(s["kbd"], n + 1)
                if r >= 2:
                    pe.wait_ge(s["pt_act"], 2 * n)
                    pe.wait_ge(s["pt_dve"], 2 * n)
                for r4 in range(4):
                    rows = slice(32 * r4, 32 * r4 + 32)
                    for c in range(CT):
                        for b in range(2):
                            last = pe.matmul(b_s[r4][b * S:(b + 1) * S, c * 4 * S:(c + 1) * 4 * S],
                                             qT[rows, q, c, b * S:(b + 1) * S],
                                             kbd[rows, q, 2 * c + b].rearrange("p a k -> p (a k)"),
                                             start=True, stop=True)
                    last.then_inc(s["p_s"], 1)

            def project(r, i, q):
                pe.wait_ge(s["act_x"], i + 1)
                if r >= 1:
                    pe.wait_ge(s["ropeu"], 2 * i)
                    pe.wait_ge(s["ropet"], i)
                for c in range(KT):
                    pe.matmul(b_qk[:, 0:D], xT[:, q, c * P:(c + 1) * P], wq_s[:, c], start=c == 0, stop=c == KT - 1)
                pe.matmul(b_qk[:, D:2 * D], xT[:, q, 2 * P:3 * P], wkv_s[:, 0:D], start=True, stop=True
                          ).then_inc(s["p_qk"], 1)
                pe.wait_ge(s["act_cd"], i + 1)
                if r >= 1:
                    pe.wait_ge(s["v4"], 4 * i)
                if r >= 2:
                    pe.wait_ge(s["at"], i - 1)
                for b in range(2):
                    last = pe.matmul(b_v[:, b * D:(b + 1) * D], cdup[:, q, b].rearrange("p a k -> p (a k)"),
                                     wkv_s[:, D:2 * D], start=True, stop=True)
                last.then_inc(s["p_v"], 1)

            def out_proj(m, a):
                pe.wait_ge(s["at"], m + 1)
                if a:
                    pe.wait_ge(s["act_cd"], m + 3)
                else:
                    pe.wait_ge(s["ln"], LN_T * (m - 1) + 1)
                for c in range(CT):
                    last = pe.matmul(b_tx[:, 0:D], aT[:, c * P:(c + 1) * P], wo_s[:, c], start=c == 0, stop=c == CT - 1)
                last.then_inc(s["p_out"], 1)

            def transpose_probs(n):
                for r4 in range(4):
                    pe.wait_ge(s["ex"], 4 * n + r4 + 1)
                    for m in range(4):
                        last = pe.transpose(b_s[r4][:, m * P:(m + 1) * P],
                                            pr[:, r4, 2 * m:2 * m + 2].rearrange("p h k -> p (h k)"), ident[:])
                    last.then_inc(s["p_pt"], 1)

            def transpose_qk(r, i, q):
                pe.wait_ge(s["rope2"], i + 1)
                if r >= 1:
                    pe.wait_ge(s["act_q"], i)
                    pe.wait_ge(s["kbd"], i)
                for c in range(2 * CT):
                    last = pe.transpose(b_t[:, c * P:(c + 1) * P], rqk[:, q, c * P:(c + 1) * P], ident[:])
                last.then_inc(s["p_t"], 1)

            def attend(n, q, a):
                pe.wait_ge(s["pt_act"], 2 * (n + 1))
                pe.wait_ge(s["pt_dve"], 2 * (n + 1))
                pe.wait_ge(s["v4"], 4 * (n + 2) if a else 4 * (n + 1))
                for r4 in range(4):
                    for c in range(CT):
                        for b in range(2):
                            rows, col = slice(32 * r4, 32 * r4 + 32), c * P + b * S
                            for v, o in ((v4[:, q, b, c * 4 + r4].rearrange("p a k -> p (a k)"), col),
                                         (ones4[:], col + CT * P)):
                                for m in range(2):
                                    last = pe.matmul(b_v[rows, o:o + S], v[:, 48 * m:48 * m + 32],
                                                     pT[:, r4, 2 * c + m, b * S:(b + 1) * S], start=m == 0, stop=m == 1)
                last.then_inc(s["p_pv"], 1)

            def body(r, i, q, a, b, c):
                if a:
                    transpose_in(r, i, q)
                if b:
                    scores(r, i - 1, 1 - q)
                if a:
                    project(r, i, q)
                if c:
                    out_proj(i - 2, a)
                if b:
                    transpose_probs(i - 1)
                if a:
                    transpose_qk(r, i, q)
                if b:
                    attend(i - 1, 1 - q, a)

            rounds(pe, body)


TRIG_STEPS = 10


def layernorm_tile(dve, s, i, r1, st6, mv, rl):
    n = LN_T * i
    dve.wait_ge(s["ln"], n + 1)
    dve.bn_stats(st6[:], r1[:]).then_inc(s["ln"], 1)
    dve.wait_ge(s["ln"], n + 2)
    dve.tensor_tensor(mv[:, 0:2], st6[:, 1:3], st6[:, 4:6], ALU.add).then_inc(s["ln"], 1)
    dve.tensor_tensor(mv[:, 2:3], st6[:, 1:2], st6[:, 4:5], ALU.subtract).then_inc(s["ln"], 1)
    dve.wait_ge(s["ln"], n + 4)
    dve.tensor_scalar(mv[:, 0:1], mv[:, 0:1], 0.5, None, ALU.mult).then_inc(s["ln"], 1)
    dve.tensor_tensor(mv[:, 2:3], mv[:, 2:3], mv[:, 2:3], ALU.mult).then_inc(s["ln"], 1)
    dve.wait_ge(s["ln"], n + 6)
    dve.tensor_scalar(rl[:], mv[:, 1:2], 1.0 / D, LN_EPS, ALU.mult, ALU.add).then_inc(s["lnb"], 1)
    dve.wait_ge(s["lnb"], i + 1)
    dve.scalar_tensor_tensor(rl[:], mv[:, 2:3], 0.25, rl[:], ALU.mult, ALU.add).then_inc(s["var"], 1)


HID = 704
HC = (HID + P - 1) // P
AHEAD = 2


def ffn(nc, x2, wg, wu, wd, sc, sdown, out, k_ident):
    x2g = x2.rearrange("(g t p) d -> g p t d", p=P, t=TILES)
    og = out.rearrange("(g t p) d -> g p t d", p=P, t=TILES)
    with ExitStack() as ctx:
        sb, ps, sem = pools(nc, ctx)
        ident = sb("f_ident", [P, P])
        raw = sb("f_raw", [P, KT, 2, HID], I32)
        w = sb("f_w", [P, KT, 2, HID])
        wh = sb("f_wh", [P, KT, 2, HID], F32R)
        wl = sb("f_wl", [P, KT, 2, HID], F32R)
        raw_d = sb("f_rawdown", [P, HC, D], I32)
        w_d = sb("f_wdown", [P, HC, D])
        scl = sb("f_scl", [P, 2, HC])
        sd = sb("f_sdown", [P, D])
        mhalf = sb("f_mhalf", [P, TILES])
        xin = sb("f_xin", [P, 2, TILES, D])
        xh = sb("f_xh", [P, 2, KT, GT], F32R)
        xl = sb("f_xl", [P, 2, KT, GT], F32R)
        sg = sb("f_sg", [P, 2, GT])
        hid = sb("f_hid", [P, 2, GT])
        r1 = sb("f_r1", [P, TILES, D])
        st6 = sb("f_st6", [P, TILES, 6])
        mv = sb("f_mv", [P, TILES, 3])
        rl = sb("f_rl", [P, TILES])
        xo = sb("f_xo", [P, TILES, D])
        b_t = [ps(f"f_bank_t{i}") for i in range(2)]
        b_g = [ps(f"f_bank_g{i}") for i in range(2)]
        b_u = [ps(f"f_bank_u{i}") for i in range(2)]
        b_o = [ps(f"f_bank_o{i}") for i in range(2)]
        names = "par fill con wh in0 in1 t_x act_x dve_x p_g p_u sg hid p_o ln var pw xo out".split()
        s = {n: sem("f_" + n) for n in names}
        block = ctx.enter_context(nc.Block())
        LN_G = 8 + TILES
        sizes = [min(P, HID - c * P) for c in range(HC)]

        def groups(eng, body):
            body(0, 0, 0, True)
            body(1, 1, 1, True)
            with eng.Fori(1, GROUPS // 2 - 1) as j:
                for q in range(2):
                    body(2, 2 * j + q, q, True)
            body(2, GROUPS - 2, 0, True)
            body(2, GROUPS - 1, 1, False)

        @block.sync
        def _(sp):
            for dst, src in ((ident[:], k_ident), (raw[:, :, 0], wg), (raw[:, :, 1], wu), (raw_d[:], wd),
                             (scl[:], sc), (sd[:], sdown.partition_broadcast(P))):
                sp.dma_start(dst, src).then_inc(s["par"], 16)
            def store(g):
                sp.wait_ge(s["xo"], TILES * (g + 1))
                sp.dma_start(og[bass.ds(g, 1)].squeeze(0), xo[:]).then_inc(s["out"], 16)

            def body(r, g, q, ahead):
                if r >= 2:
                    sp.wait_ge(s["ln"], LN_G * (g - 2) + 2)
                sp.dma_start(xin[:, q], x2g[bass.ds(g, 1)].squeeze(0)).then_inc(s[f"in{q}"], 16)
                if r >= 2:
                    store(g - 2)

            groups(sp, body)
            store(GROUPS - 2)
            store(GROUPS - 1)
            sp.wait_ge(s["out"], 16 * GROUPS)

        @block.gpsimd
        def _(pool):
            pool.memset(mhalf[:], -0.5).then_inc(s["fill"], 1)
            pool.wait_ge(s["fill"], 1)
            pool.wait_ge(s["par"], 16 * 6)
            with pool.Fori(0, GROUPS) as g:
                pool.wait_ge(s["var"], g + 1)
                pool.tensor_tensor(rl[:], rl[:], mhalf[:], ALU.pow).then_inc(s["pw"], 1)

        @block.scalar
        def _(act):
            act.wait_ge(s["par"], 16 * 6)
            act.wait_ge(s["con"], 1)
            act.activation(wh[:], w[:], ACT.Copy).then_inc(s["wh"], 1)

            def round_x(g, q):
                act.wait_ge(s["t_x"], g + 1)
                for kt in range(KT):
                    act.activation(xh[:, q, kt], b_t[kt][:], ACT.Copy).then_inc(s["act_x"], 1)

            def body(r, g, q, ahead):
                for c, n in enumerate(sizes):
                    act.wait_ge(s["p_g"], g * HC + c + 1)
                    if r >= 1 or c >= 2:
                        act.wait_ge(s["hid"], g * HC + c - 1)
                    act.activation(sg[0:n, c % 2], b_g[c % 2][0:n, :], ACT.Silu,
                                   scale=scl[0:n, 0, c:c + 1]).then_inc(s["sg"], 1)
                    if ahead and c == AHEAD:
                        round_x(g + 1, 1 - q)

            round_x(0, 0)
            groups(act, body)

        @block.vector
        def _(dve):
            dve.wait_ge(s["par"], 16 * 6)
            dve.tensor_scalar(w[:], raw[:], -128.0, None, ALU.add).then_inc(s["con"], 1)
            dve.tensor_scalar(w_d[:], raw_d[:], -128.0, None, ALU.add).then_inc(s["con"], 1)
            dve.wait_ge(s["con"], 2)
            dve.tensor_tensor(w_d[:], w_d[:], spread(sd[:], 1, HC), ALU.mult).then_inc(s["con"], 1)
            dve.wait_ge(s["wh"], 1)
            dve.tensor_tensor(wl[:], w[:], wh[:].bitcast(F32), ALU.subtract).then_inc(s["con"], 1)

            def rest_x(g, q):
                for kt in range(KT):
                    dve.wait_ge(s["act_x"], KT * g + kt + 1)
                    dve.tensor_tensor(xl[:, q, kt], b_t[kt][:], xh[:, q, kt].bitcast(F32), ALU.subtract
                                      ).then_inc(s["dve_x"], 1)

            def normalise(r, g):
                dve.wait_ge(s["pw"], g + 1)
                if r >= 1:
                    dve.wait_ge(s["out"], 16 * g)
                for t in range(TILES):
                    dve.tensor_scalar(xo[:, t], r1[:, t], mv[:, t, 0:1], rl[:, t:t + 1], ALU.subtract,
                                      ALU.mult).then_inc(s["xo"], 1)

            def body(r, g, q, ahead):
                for c, n in enumerate(sizes):
                    dve.wait_ge(s["p_u"], g * HC + c + 1)
                    dve.wait_ge(s["sg"], g * HC + c + 1)
                    if r >= 1 or c >= 2:
                        dve.wait_ge(s["p_o"], g * HC + c - 1)
                    dve.scalar_tensor_tensor(hid[0:n, c % 2], b_u[c % 2][0:n, :], scl[0:n, 1, c:c + 1],
                                             sg[0:n, c % 2], ALU.mult, ALU.mult).then_inc(s["hid"], 1)
                    if c == 0 and r >= 1:
                        normalise(r - 1, g - 1)
                    if ahead and c == AHEAD:
                        rest_x(g + 1, 1 - q)
                la = 0

                def step(ins):
                    nonlocal la
                    la += 1
                    ins.then_inc(s["ln"], 1)

                def upto():
                    dve.wait_ge(s["ln"], LN_G * g + la)

                dve.wait_ge(s["p_o"], g * HC + HC)
                for half in range(2):
                    h = slice(2 * half, 2 * half + 2)
                    step(dve.tensor_tensor(r1[:, h], b_o[half][:].rearrange("p (t d) -> p t d", d=D),
                                           xin[:, q, h], ALU.add))
                upto()
                for t in range(TILES):
                    step(dve.bn_stats(st6[:, t], r1[:, t]))
                upto()
                step(dve.tensor_tensor(mv[:, :, 0], st6[:, :, 1], st6[:, :, 4], ALU.add))
                step(dve.tensor_tensor(mv[:, :, 1], st6[:, :, 1], st6[:, :, 4], ALU.subtract))
                step(dve.tensor_tensor(mv[:, :, 2], st6[:, :, 2], st6[:, :, 5], ALU.add))
                upto()
                step(dve.tensor_scalar(mv[:, :, 0], mv[:, :, 0], 0.5, None, ALU.mult))
                step(dve.tensor_tensor(mv[:, :, 1], mv[:, :, 1], mv[:, :, 1], ALU.mult))
                step(dve.tensor_scalar(mv[:, :, 2], mv[:, :, 2], 1.0 / D, LN_EPS, ALU.mult, ALU.add))
                upto()
                dve.scalar_tensor_tensor(rl[:], mv[:, :, 1], 0.25, mv[:, :, 2], ALU.mult, ALU.add
                                         ).then_inc(s["var"], 1)
                assert la == LN_G

            rest_x(0, 0)
            groups(dve, body)
            normalise(2, GROUPS - 1)

        @block.tensor
        def _(pe):
            pe.wait_ge(s["par"], 16 * 6)
            pe.wait_ge(s["con"], 4)

            def transpose_x(r, g, q):
                pe.wait_ge(s[f"in{q}"], 8 * (g - q) + 16)
                if r >= 1:
                    pe.wait_ge(s["act_x"], KT * g)
                    pe.wait_ge(s["dve_x"], KT * g)
                for t in range(TILES):
                    for kt in range(KT):
                        last = pe.transpose(b_t[kt][:, t * P:(t + 1) * P], xin[:, q, t, kt * P:(kt + 1) * P], ident[:])
                last.then_inc(s["t_x"], 1)

            def gate_up(r, g, q, c, n):
                if r >= 1 or c >= 2:
                    pe.wait_ge(s["sg"], g * HC + c - 1)
                    pe.wait_ge(s["hid"], g * HC + c - 1)
                for u, bank, name in ((0, b_g, "p_g"), (1, b_u, "p_u")):
                    parts = [(a[:, kt, u, c * P:c * P + n], b[:, q, kt]) for kt in range(KT)
                             for a, b in ((wh, xh), (wh, xl), (wl, xh))]
                    for i, (a, b) in enumerate(parts):
                        last = pe.matmul(bank[c % 2][0:n, :], a, b, start=i == 0, stop=i == len(parts) - 1)
                    last.then_inc(s[name], 1)

            def down(r, g, c, n):
                pe.wait_ge(s["hid"], g * HC + c + 1)
                if c == 0 and r >= 1:
                    pe.wait_ge(s["ln"], LN_G * (g - 1) + 2)
                for t in range(TILES):
                    last = pe.matmul(b_o[t // 2][:, (t % 2) * D:(t % 2) * D + D],
                                     hid[0:n, c % 2, t * P:(t + 1) * P], w_d[0:n, c],
                                     start=c == 0 and t % 2 == 0, stop=c == HC - 1, skip_group_check=True)
                last.then_inc(s["p_o"], 1)

            def body(r, g, q, ahead):
                pe.wait_ge(s["act_x"], KT * (g + 1))
                pe.wait_ge(s["dve_x"], KT * (g + 1))
                for c, n in enumerate(sizes):
                    gate_up(r, g, q, c, n)
                    if c >= 1:
                        down(r, g, c - 1, sizes[c - 1])
                    if ahead and c == AHEAD:
                        transpose_x(r + 1, g + 1, 1 - q)
                down(r, g, HC - 1, sizes[HC - 1])

            transpose_x(0, 0, 0)
            groups(pe, body)


_SCRATCH = {"pair_split": (PAIRS, P, 2, 5 * P), "mov_rows": (PAIRS, 2, 2, TILES, 2, S),
            "sta_rows": (PAIRS, 2, TILES, 2, P), "ec_rows": (PAIRS, 2, 2, GT),
            "x1": (TOKENS, D), "x2": (TOKENS, D)}


def constants(np):
    r, col = np.arange(R_ALL)[:, None], np.arange(GT)[None]
    mask_row = r - R_MOV - R_STA
    mov = np.where(((r - R_MOV) % 8 == col // S) & (r >= R_MOV) & (mask_row < 0), -1.0, 0.0)
    mov = np.where((mask_row >= 0) & (mask_row > col % S), -1e30, mov)
    p = np.arange(P)[None]
    sta = np.where((r < R_MOV) & (r % 2 == p // S), 1.0, 0.0)
    sta = np.where((mask_row >= 0) & (mask_row == p % S), 1.0, sta)
    pc = np.arange(P)[:, None]
    own = (np.arange(P)[None] % S) // XD == pc // S
    consts = {
        "k_ident": np.eye(P), "k_eye2": np.tile(np.eye(S), (2, 1)),
        "k_reset": np.tile((np.arange(GT) % S != 0) * 1.0, (HEADS, 1)),
        "k_mov": mov, "k_sta": sta,
        "k_sel": (np.arange(4)[:, None] % 2 == p // HP) * 1.0,
        "k_freq": np.tile([[1.0, 10000.0 ** -0.5]], (P, 1)),
        "k_heads": np.repeat((pc % 32 // XD == np.arange(4)[None]) * 1.0, S, axis=1).reshape(P, 4, S),
        "k_ones4": own * 1.0,
    }
    return {k: np.ascontiguousarray(v, np.float32) for k, v in consts.items()}


def arrange(np, i):
    w = i["L0_attn_in_proj_w"]
    wz, wx = w[:INNER], w[INNER:2 * INNER]
    wb, wc, wd = np.split(w[2 * INNER:], [N, 2 * N])
    order = np.concatenate([np.arange(0, HEADS, 2), np.arange(1, HEADS, 2)])

    def pair_major(m):
        return m.reshape(PAIRS, P, KT, P).transpose(0, 3, 2, 1).reshape(PAIRS, P, KT * P)

    def padded(m):
        return np.concatenate([m, np.zeros((HC * P - HID,) + m.shape[1:], m.dtype)])

    h0 = i["L0_attn_ssm_state"][0].reshape(PAIRS, 2, N, HP).transpose(0, 2, 1, 3).reshape(PAIRS, N, P)
    chan = np.concatenate([i["L0_attn_conv_w"], i["L0_attn_conv_b"][:, None], i["L0_attn_inner_norm_w"][:, None],
                           i["L0_attn_conv_state"][0]], axis=1)
    out = {
        "x": i["x"].reshape(TOKENS, D),
        "pair_w": np.concatenate([pair_major(wx), pair_major(wz), h0], axis=2),
        "aux_w": np.concatenate([wb, wc, wd[order]]).T.reshape(KT, P, AUX).transpose(1, 0, 2),
        "dt_par": np.stack([i["L0_attn_dt_bias"][order], i["L0_attn_A_log"][order]], axis=1),
        "chan_par": chan.reshape(PAIRS, P, C_EDGE).transpose(1, 0, 2),
        "d_rows": i["L0_attn_D_param"],
        "norm_w": i["L0_attn_norm_w"].reshape(KT, P).T,
        "wout": i["L0_attn_out_proj_w"].T.reshape(PAIRS, P, D).transpose(1, 0, 2),
        "ctx": i["ctx_1024"].reshape(TOKENS, CTX),
        "pos": i["fside_BxSx2_0"].reshape(TOKENS, 2),
        "x_wq": i["L0_xattn_Wq"], "x_wkv": i["L0_xattn_Wkv"], "x_wout": i["L0_xattn_Wout"], "x_bout": i["L0_xattn_bout"],
        "f_wg": i["L0_ffn_wq_gate"].T.reshape(KT, P, HID).transpose(1, 0, 2),
        "f_wu": i["L0_ffn_wq_up"].T.reshape(KT, P, HID).transpose(1, 0, 2),
        "f_wd": padded(i["L0_ffn_wq_down"].T).reshape(HC, P, D).transpose(1, 0, 2),
        "f_sc": np.stack([padded(i["L0_ffn_s_gate"]), padded(i["L0_ffn_s_up"])]).reshape(2, HC, P).transpose(2, 0, 1),
        "f_sd": i["L0_ffn_s_down"],
    }
    return {k: np.ascontiguousarray(v) for k, v in out.items()}


def program(nc, d, out):
    setup_weights(nc, d["pair_w"], d["pair_split"])
    mixer(nc, d["x"], d["pair_split"], d["aux_w"], d["dt_par"], d["chan_par"], d["d_rows"], d["norm_w"], d["wout"],
          d["x1"], d["mov_rows"], d["sta_rows"], d["ec_rows"],
          d["k_ident"], d["k_eye2"], d["k_reset"], d["k_mov"], d["k_sta"], d["k_sel"])
    cross(nc, d["x1"], d["ctx"], d["pos"], d["x_wq"], d["x_wkv"], d["x_wout"], d["x_bout"], d["x2"],
          d["k_ident"], d["k_freq"], d["k_heads"], d["k_ones4"])
    ffn(nc, d["x2"], d["f_wg"], d["f_wu"], d["f_wd"], d["f_sc"], d["f_sd"], out, d["k_ident"])


def kernel(**inputs):
    import numpy as np
    import concourse.bacc as bacc
    from concourse.bass_utils import run_bass_kernel_spmd

    nc = bacc.Bacc("TRN2", target_bir_lowering=False, num_devices=1)
    arrays = {**arrange(np, {k: np.asarray(v) for k, v in inputs.items()}), **constants(np)}
    d = {k: nc.dram_tensor(k, v.shape, mybir.dt.from_np(v.dtype), kind="ExternalInput").ap() for k, v in arrays.items()}
    d.update({k: nc.dram_tensor(k, shape, F32).ap() for k, shape in _SCRATCH.items()})
    out = nc.dram_tensor("out", (TOKENS, D), F32, kind="ExternalOutput").ap()
    program(nc, d, out)
    r = run_bass_kernel_spmd(nc, [arrays], core_ids=[0])
    return r.results[0]["out"].reshape(SEQS, S, D)
```

```python
import concourse.bass as bass
from concourse import mybir
from contextlib import ExitStack

F32 = mybir.dt.float32
F32R = mybir.dt.float32r
I32 = mybir.dt.int32
ALU = mybir.AluOpType
ACT = mybir.ActivationFunctionType
AX = mybir.AxisListType

P = 128
SEQS, S, D = 64, 64, 256
TOKENS = SEQS * S
KT = D // P
GT = 512
GROUPS = TOKENS // GT
TILES = GT // P
HEADS, HP, N = 48, 64, 128
INNER = HEADS * HP
PAIRS = HEADS // 2
TAPS = 4
BATCH = 6
RMS_EPS = 1e-5
LN_EPS = 1e-5
R_MOV, R_STA = 4, 16
R_ALL = R_MOV + R_STA + S
C_W, C_CB, C_IW, C_CS, C_EDGE, C_N = 0, 4, 5, 6, 9, 12
HL_STEPS = 5
ROW_DMAS = 16
LN_STEPS = 8 + 2 * TILES
AFTER_INTRA, AFTER_OUT, AFTER_SUMS = 3, (5, 8), 12
PEEL = 4
AUX = 2 * N + HEADS


def pools(nc, ctx):
    def sb(name, shape, dt=F32):
        return ctx.enter_context(nc.sbuf_tensor(name, shape, dt))

    def ps(name, shape=(P, 512)):
        return ctx.enter_context(nc.psum_tensor(name, list(shape), F32))

    def sem(name):
        return ctx.enter_context(nc.semaphore(name))

    return sb, ps, sem


def spread(ap, axis, n):
    ap = ap.unsqueeze(axis)
    shape = list(ap.shape)
    shape[axis] = n
    return ap.to_broadcast(shape)


def split_product(pe, out, parts):
    for i, (lhs, rhs) in enumerate(parts):
        last = pe.matmul(out, lhs, rhs, start=i == 0, stop=i == len(parts) - 1)
    return last


def resident(nc, ctx):
    sb, ps, sem = pools(nc, ctx)
    return {
        "ident": sb("ident", [P, P]),
        "ones": sb("ones", [P, 1]),
        "par": sb("par", [P, PAIRS, C_N]),
        "dd": sb("dd", [P, PAIRS, 2, S]),
        "wo": sb("wo", [P, PAIRS, D]),
        "mov": sb("mov", [R_ALL, 2, BATCH, GT], F32R),
        "sta": sb("sta", [R_ALL, 2, BATCH, P], F32R),
        "ec_sel": sb("ec_sel", [4, P], F32R),
    }


def heads(nc, tables, x, aux_w, dt_par, norm_w, chan_par, d_rows, wout, x_t, c_t, g_mat, mov_rows, sta_rows,
          ec_rows, k_ident, k_reset, k_eye2, k_mov, k_sta, k_sel):
    par, dd, mov, sta = (tables[n] for n in ("par", "dd", "mov", "sta"))
    xg = x.rearrange("(g t p) d -> g p t d", p=P, t=TILES)
    with ExitStack() as ctx:
        sb, ps, sem = pools(nc, ctx)
        ident = tables["ident"]
        reset = sb("h_reset", [HEADS, GT])
        norm_c = sb("h_norm", [P, KT])
        aux_raw = sb("h_aux", [P, KT, AUX])
        aux_hi = sb("h_aux_hi", [P, KT, AUX], F32R)
        aux_lo = sb("h_aux_lo", [P, KT, AUX], F32R)
        dtp = sb("h_dtp", [HEADS, 2])
        a_neg = sb("h_a_neg", [HEADS, 1])
        mhalf = sb("h_mhalf", [P, TILES])
        raw_mov = sb("raw_mov", [R_ALL, GT])
        raw_sta = sb("raw_sta", [R_ALL, P])
        raw_sel = sb("raw_sel", [4, P])
        eye2 = sb("eye2", [P, S])
        d_all = sb("d_all", [P, HEADS])
        edge = sb("edge", [P, PAIRS])
        squares = sb("h_squares", [P, TILES, D])
        xs = sb("h_xs", [P, TILES, D])
        b_sb = sb("h_b", [P, GT])
        dt = sb("h_dt", [HEADS, GT])
        cum = sb("h_cum", [HEADS, GT])
        ecs = sb("h_ecs", [HEADS, GT])
        xa = sb("h_xa", [P, 2, TILES, D])
        ss = sb("h_ss", [P, 2, TILES])
        rstd = sb("h_rstd", [P, 2, TILES])
        xt = sb("h_xt", [P, 2, KT, GT])
        xh = sb("h_xh", [P, 2, KT, GT], F32R)
        xl = sb("h_xl", [P, 2, KT, GT], F32R)
        c_sb = sb("h_c", [P, 2, GT])
        g_sb = sb("h_g", [P, 2, TILES, S])
        v = sb("h_v", [HEADS, 2, GT])
        rows = sb("h_rows", [HEADS, 2, 4, GT], F32R)
        b_t = [ps(f"h_bank_t{kt}") for kt in range(KT)]
        b_dt, b_b, b_c, b_g = (ps(f"h_bank_{n}") for n in ("dt", "b", "c", "g"))

        names = ("par con_act con fill tab_in wo_in tab in0 in1 sq rs pw xs t_x xt xh xl p_aux v bc p_g g sp dt cum ecs "
                 "cum_hl ec_hl "
                 "xt_out0 xt_out1 cg_out0 cg_out1 rows_out0 rows_out1").split()
        s = {n: sem("h_" + n) for n in names}
        block = ctx.enter_context(nc.Block())

        def rounds(eng, body):
            for i in range(PEEL):
                body(i, i, i % 2, True, i >= 1, i >= 2)
            with eng.Fori(PEEL // 2, GROUPS // 2) as j:
                for q in range(2):
                    body(PEEL, 2 * j + q, q, True, True, True)
            body(PEEL, GROUPS, 0, False, True, True)
            body(PEEL, GROUPS + 1, 1, False, False, True)

        @block.sync
        def _(sp):
            for dst, src in ((ident[:], k_ident), (reset[:], k_reset), (norm_c[:], norm_w), (aux_raw[:], aux_w),
                             (dtp[:], dt_par)):
                sp.dma_start(dst, src).then_inc(s["par"], 16)

            def at(dram, g):
                return dram[bass.ds(g, 1)].squeeze(0)

            def store_rows(g, q):
                def part(hh, n):
                    return rows[hh * PAIRS:(hh + 1) * PAIRS, q, n].bitcast(F32)

                sp.wait_ge(s["cum_hl"], 2 * (g + 1))
                sp.wait_ge(s["ec_hl"], 2 * (g + 1))
                for hl in range(2):
                    for hh in range(2):
                        for b in range(2):
                            sp.dma_start(at(mov_rows, g)[:, hl, b, :, hh, :], part(hh, hl).rearrange(
                                "k (t b s) -> k t b s", b=2, s=S)[:, :, b]).then_inc(s[f"rows_out{q}"], 16)
                        sp.dma_start(at(sta_rows, g)[:, hl, :, hh, :],
                                     part(hh, hl).rearrange("k (t p) -> k t p", p=P)).then_inc(s[f"rows_out{q}"], 16)
                        sp.dma_start(at(ec_rows, g)[:, hl, hh, :], part(hh, 2 + hl)).then_inc(s[f"rows_out{q}"], 16)

            def body(r, i, q, a, b, c):
                if a:
                    if r >= 2:
                        sp.wait_ge(s["xs"], TILES * (i - 1))
                    sp.dma_start(xa[:, q], at(xg, i)).then_inc(s[f"in{q}"], 16)
                if r == 0:
                    for dst, src in ((par[:, :, 0:C_EDGE], chan_par), (d_all[:], d_rows.partition_broadcast(P)),
                                     (eye2[:], k_eye2), (raw_mov[:], k_mov), (raw_sta[:], k_sta), (raw_sel[:], k_sel)):
                        sp.dma_start(dst, src).then_inc(s["tab_in"], 16)
                if r == 1:
                    sp.dma_start(tables["wo"][:], wout).then_inc(s["wo_in"], 16)
                if b:
                    sp.wait_ge(s["xt"], KT * i)
                    sp.dma_start(at(x_t, i - 1), xt[:, 1 - q]).then_inc(s[f"xt_out{1 - q}"], 16)
                if c:
                    sp.wait_ge(s["bc"], 2 * (i - 1))
                    sp.dma_start(at(c_t, i - 2), c_sb[:, q]).then_inc(s[f"cg_out{q}"], 16)
                    sp.wait_ge(s["g"], 2 * (i - 1))
                    sp.dma_start(at(g_mat, i - 2), g_sb[:, q]).then_inc(s[f"cg_out{q}"], 16)
                if r >= 3:
                    store_rows(i - 3, 1 - q)

            rounds(sp, body)
            store_rows(GROUPS - 1, 1)
            sp.wait_ge(s["wo_in"], 16)
            for q in range(2):
                sp.wait_ge(s[f"xt_out{q}"], 16 * (GROUPS // 2))
                sp.wait_ge(s[f"cg_out{q}"], 16 * 2 * (GROUPS // 2))
                sp.wait_ge(s[f"rows_out{q}"], 16 * ROW_DMAS * (GROUPS // 2))

        @block.gpsimd
        def _(pool):
            pool.memset(mhalf[:], -0.5).then_inc(s["fill"], 1)
            pool.memset(tables["ones"][:], 1.0).then_inc(s["fill"], 1)
            pool.wait_ge(s["fill"], 2)

            def body(r, i, q, a, b, c):
                if a:
                    pool.wait_ge(s["rs"], i + 1)
                    pool.tensor_tensor(rstd[:, q], rstd[:, q], mhalf[:], ALU.pow).then_inc(s["pw"], 1)
                    if r >= 2:
                        pool.wait_ge(s["p_aux"], 3 * (i - 1))
                    for kt in range(KT):
                        pool.wait_ge(s["xt"], KT * i + kt + 1)
                        pool.wait_ge(s["xh"], KT * i + kt + 1)
                        pool.tensor_tensor(xl[:, q, kt], xt[:, q, kt], xh[:, q, kt].bitcast(F32), ALU.subtract
                                           ).then_inc(s["xl"], 1)

            rounds(pool, body)

        @block.scalar
        def _(act):
            act.wait_ge(s["par"], 16 * 5)
            act.activation(aux_hi[:], aux_raw[:], ACT.Copy).then_inc(s["con_act"], 1)
            act.activation(a_neg[:], dtp[:, 1:2], ACT.Exp).then_inc(s["con_act"], 1)

            def body(r, i, q, a, b, c):
                if a:
                    act.wait_ge(s[f"in{q}"], 8 * (i - q) + 16)
                    if r >= 1:
                        act.wait_ge(s["rs"], i)
                    for t in range(TILES):
                        act.activation(squares[:, t], xa[:, q, t], ACT.Square, accum_out=ss[:, q, t:t + 1]
                                       ).then_inc(s["sq"], 1)
                if c:
                    m = i - 2
                    act.wait_ge(s["v"], m + 1)
                    if r >= 3:
                        act.wait_ge(s["dt"], 2 * m)
                    act.activation(dt[:], v[:, q], ACT.Abs).then_inc(s["sp"], 1)
                    act.wait_ge(s["sp"], 3 * m + 1)
                    act.activation(dt[:], dt[:], ACT.Exp, scale=-1.0).then_inc(s["sp"], 1)
                    act.wait_ge(s["sp"], 3 * m + 2)
                    act.activation(dt[:], dt[:], ACT.Ln, bias=1.0).then_inc(s["sp"], 1)
                if a:
                    act.wait_ge(s["t_x"], i + 1)
                    if r >= 2:
                        act.wait_ge(s["xl"], KT * (i - 1))
                        act.wait_ge(s[f"xt_out{q}"], 8 * (i - q))
                    for kt in range(KT):
                        act.activation(xt[:, q, kt], b_t[kt][:], ACT.Copy, scale=norm_c[:, kt:kt + 1]
                                       ).then_inc(s["xt"], 1)
                if c:
                    act.wait_ge(s["cum"], m + 1)
                    if r >= 3:
                        act.wait_ge(s["ec_hl"], 2 * m)
                    act.activation(ecs[:], cum[:], ACT.Exp).then_inc(s["ecs"], 1)
                if b:
                    act.wait_ge(s["p_aux"], 3 * i)
                    if r >= 2:
                        act.wait_ge(s["p_g"], i - 1)
                    act.activation(b_sb[:], b_b[:], ACT.Copy).then_inc(s["bc"], 1)
                    if r >= 3:
                        act.wait_ge(s[f"cg_out{1 - q}"], 16 * (i - 2 + q))
                    act.activation(c_sb[:, 1 - q], b_c[:], ACT.Copy).then_inc(s["bc"], 1)

            rounds(act, body)

        @block.vector
        def _(dve):
            dve.wait_ge(s["con_act"], 2)
            dve.tensor_tensor(aux_lo[:], aux_raw[:], aux_hi[:].bitcast(F32), ALU.subtract).then_inc(s["con"], 1)
            dve.tensor_scalar(a_neg[:], a_neg[:], -1.0, None, ALU.mult).then_inc(s["con"], 1)
            dve.wait_ge(s["con"], 2)

            n_tab = [0]

            def made(ins):
                ins.then_inc(s["tab"], 1)
                n_tab[0] += 1
                dve.wait_ge(s["tab"], n_tab[0])

            def mixer_tables(r):
                if r == 0:
                    dve.wait_ge(s["tab_in"], 16 * 6)
                    for t in range(TAPS - 1):
                        for i in range(TAPS - 1 - t):
                            into = par[:, :, C_EDGE + t] if i == 0 else edge[:]
                            made(dve.tensor_tensor(into, par[:, :, C_W + i], par[:, :, C_CS + t + i], ALU.mult))
                            if i:
                                made(dve.tensor_tensor(par[:, :, C_EDGE + t], par[:, :, C_EDGE + t], edge[:], ALU.add))
                    made(dve.tensor_copy(tables["ec_sel"][:], raw_sel[:]))
                elif r == 1:
                    made(dve.tensor_tensor(dd[:].rearrange("p k h s -> p (k h) s"), spread(d_all[:], 2, S),
                                           spread(eye2[:], 1, HEADS), ALU.mult))
                else:
                    made(dve.tensor_copy(mov[:, r - 2], spread(raw_mov[:], 1, BATCH)))
                    made(dve.tensor_copy(sta[:, r - 2], spread(raw_sta[:], 1, BATCH)))

            def body(r, i, q, a, b, c):
                m = i - 2
                if a:
                    dve.wait_ge(s["sq"], TILES * (i + 1))
                    dve.tensor_scalar(rstd[:, q], ss[:, q], 1.0 / D, RMS_EPS, ALU.mult, ALU.add).then_inc(s["rs"], 1)
                if a:
                    dve.wait_ge(s["pw"], i + 1)
                    if r >= 1:
                        dve.wait_ge(s["t_x"], i)
                    for t in range(TILES):
                        dve.tensor_scalar(xs[:, t], xa[:, q, t], rstd[:, q, t:t + 1], None, ALU.mult
                                          ).then_inc(s["xs"], 1)
                if c:
                    dve.wait_ge(s["sp"], 3 * (m + 1))
                    dve.scalar_tensor_tensor(dt[:], v[:, q], 0.0, dt[:], ALU.max, ALU.add).then_inc(s["dt"], 1)
                    dve.wait_ge(s["dt"], 2 * m + 1)
                    dve.tensor_scalar(dt[:], dt[:], a_neg[:], None, ALU.mult).then_inc(s["dt"], 1)
                    dve.wait_ge(s["dt"], 2 * m + 2)
                    if r >= 3:
                        dve.wait_ge(s["ecs"], m)
                    dve.tensor_tensor_scan(cum[:], reset[:], dt[:], 0.0, ALU.mult, ALU.add).then_inc(s["cum"], 1)
                if a:
                    dve.wait_ge(s["t_x"], i + 1)
                    if r >= 2:
                        dve.wait_ge(s["p_aux"], 3 * (i - 1))
                        dve.wait_ge(s["xl"], KT * (i - 1))
                    for kt in range(KT):
                        dve.wait_ge(s["xt"], KT * i + kt + 1)
                        dve.tensor_copy(xh[:, q, kt], xt[:, q, kt]).then_inc(s["xh"], 1)
                if c:
                    dve.wait_ge(s["cum"], m + 1)
                    if r >= 4:
                        dve.wait_ge(s[f"rows_out{q}"], 8 * ROW_DMAS * (m - q))
                    dve.tensor_copy(rows[:, q, 0], cum[:]).then_inc(s["cum_hl"], 1)
                    dve.wait_ge(s["cum_hl"], 2 * m + 1)
                    dve.tensor_tensor(rows[:, q, 1], cum[:], rows[:, q, 0].bitcast(F32), ALU.subtract
                                      ).then_inc(s["cum_hl"], 1)
                    dve.wait_ge(s["ecs"], m + 1)
                    dve.tensor_copy(rows[:, q, 2], ecs[:]).then_inc(s["ec_hl"], 1)
                    dve.wait_ge(s["ec_hl"], 2 * m + 1)
                    dve.tensor_tensor(rows[:, q, 3], ecs[:], rows[:, q, 2].bitcast(F32), ALU.subtract
                                      ).then_inc(s["ec_hl"], 1)
                if b:
                    dve.wait_ge(s["p_aux"], 3 * (i - 1) + 1)
                    if r >= 3:
                        dve.wait_ge(s["sp"], 3 * (i - 2))
                    dve.tensor_scalar(v[:, 1 - q], b_dt[0:HEADS, :], dtp[:, 0:1], None, ALU.add).then_inc(s["v"], 1)
                    dve.wait_ge(s["p_g"], i)
                    if r >= 3:
                        dve.wait_ge(s[f"cg_out{1 - q}"], 16 * (i - 2 + q))
                    for half in range(2):
                        pr = slice(half * S, half * S + S)
                        dve.tensor_copy(g_sb[pr, 1 - q], b_g[pr].rearrange("p (t c) -> p t c", c=P)[:, :, pr]
                                        ).then_inc(s["g"], 1)
                if r < PEEL:
                    mixer_tables(r)

            rounds(dve, body)

        @block.tensor
        def _(pe):
            pe.wait_ge(s["par"], 16 * 5)
            pe.wait_ge(s["con"], 2)

            def body(r, i, q, a, b, c):
                if a:
                    if r >= 1:
                        pe.wait_ge(s["xt"], KT * i)
                    for t in range(TILES):
                        pe.wait_ge(s["xs"], TILES * i + t + 1)
                        for kt in range(KT):
                            last = pe.transpose(b_t[kt][:, t * P:(t + 1) * P], xs[:, t, kt * P:(kt + 1) * P], ident[:])
                    last.then_inc(s["t_x"], 1)
                if b:
                    pe.wait_ge(s["xl"], KT * i)
                    for n, (bank, lo, size) in enumerate(((b_dt, 2 * N, HEADS), (b_b, 0, N), (b_c, N, N))):
                        if r >= 2:
                            if n == 0:
                                pe.wait_ge(s["v"], i - 1)
                            else:
                                pe.wait_ge(s["bc"], 2 * (i - 1))
                        parts = [(w[:, kt, lo:lo + size], xv[:, 1 - q, kt]) for kt in range(KT)
                                 for w, xv in ((aux_hi, xh), (aux_hi, xl), (aux_lo, xh))]
                        split_product(pe, bank[0:size, :], parts).then_inc(s["p_aux"], 1)
                    pe.wait_ge(s["bc"], 2 * i)
                    if r >= 2:
                        pe.wait_ge(s["g"], 2 * (i - 1))
                    for t in range(TILES):
                        ts = slice(t * P, (t + 1) * P)
                        last = pe.matmul(b_g[:, ts], b_sb[:, ts], c_sb[:, 1 - q, ts], start=True, stop=True)
                    last.then_inc(s["p_g"], 1)

            rounds(pe, body)


def mixer(nc, tables, x, pair_w, x1, x_t, c_t, g_mat, mov_rows, sta_rows, ec_rows):
    xg = x.rearrange("(g t p) d -> g p t d", p=P, t=TILES)
    x1g = x1.rearrange("(g t p) d -> g p t d", p=P, t=TILES)
    with ExitStack() as ctx:
        sb, ps, sem = pools(nc, ctx)
        ident, ones, par, dd, wo, mov, sta, ec_sel = (
            tables[n] for n in ("ident", "ones", "par", "dd", "wo", "mov", "sta", "ec_sel"))
        xo = xa = sb("xa", [P, TILES, D])
        x_raw = sb("x_raw", [P, KT, GT])
        c_raw = sb("c_raw", [P, GT])
        g_raw = sb("g_raw", [P, TILES, S])
        mhalf = sb("mhalf", [P, TILES])
        xh = sb("xh", [P, KT, GT], F32R)
        xl = sb("xl", [P, KT, GT], F32R)
        ch = sb("ch", [P, GT], F32R)
        cl = sb("cl", [P, GT], F32R)
        g_sb = sb("g_sb", [P, TILES, S])
        e_sb = sb("e_sb", [P, PAIRS, TILES, 2, S])
        wraw = sb("wraw", [P, 2, 5 * P])
        wst = sb("wst", [P, 2, 2, 5 * P], F32R)
        ecr = sb("ecr", [4, 2, GT], F32R)
        gd = sb("gd", [P, 2, TILES, 2, S])
        mb = sb("mb", [P, 2, TILES, 2, P])
        acc = sb("acc", [P, 2, GT])
        xt = sb("xt", [P, 2, TILES, P])
        sz = sb("sz", [P, 2, GT])
        eb = sb("eb", [P, 2, GT])
        ce = sb("ce", [P, 2, GT])
        y = sb("y", [P, 2, GT])
        yz = sb("yz", [P, 2, GT])
        sq = sb("sq", [P, 2, GT])
        ssq = sb("ssq", [P, GT])
        ry = sb("ry", [P, TILES])
        r1 = sz[:].rearrange("p a (t d) -> p (a t) d", d=D)
        st6 = sb("st6", [P, TILES, 6])
        mv = sb("mv", [P, TILES, 3])
        rl = sb("rl", [P, TILES])

        b_xc, b_z, b_ch, b_ec, b_xt, b_y = (ps(f"bank_{n}") for n in ("xc", "z", "ch", "ec", "xt", "y"))
        b_out = [ps("bank_out0"), ps("bank_out1")]

        names = ("fill x_in raw_in hl rows_in0 rows_in1 diff_done exp_done "
                 "w_in0 w_in1 ec_in0 ec_in1 w_hi w_lo pe_xc pe_z pe_ch pe_ec pe_xt pe_intra pe_out "
                 "act_conv act_ec act_z act_xt act_sq dve_tap dve_ce dve_m dve_yadd dve_gate "
                 "pool_gd pool_m pool_sq pool_pow var_done sum_pe ln_a ln_done out_st").split()
        s = {n: sem("m_" + n) for n in names}
        block = ctx.enter_context(nc.Block())
        def groups(eng, body):
            body(0, 0)
            with eng.Fori(1, GROUPS) as g:
                body(1, g)

        @block.sync
        def _(sp):
            def store(g):
                sp.wait_ge(s["ln_done"], TILES * (g + 1))
                sp.dma_start(x1g[bass.ds(g, 1)].squeeze(0), xo[:]).then_inc(s["out_st"], 16)

            def body(r, g):
                def of_group(dram):
                    return dram[bass.ds(g, 1)].squeeze(0)

                def load_weights(k, q):
                    sp.dma_start(wraw[:, q], pair_w[bass.ds(k, 1)].squeeze(0)).then_inc(s[f"w_in{q}"], 16)

                def load_ec(k, q):
                    sp.dma_start(ecr[:, q].bitcast(F32), of_group(ec_rows)[bass.ds(k, 1)].rearrange(
                        "k l h t -> (k l h) t")).then_inc(s[f"ec_in{q}"], 16)

                if r:
                    sp.wait_ge(s["w_lo"], g * PAIRS)
                load_weights(0, 0)
                load_weights(1, 1)
                if r:
                    sp.wait_ge(s["hl"], HL_STEPS * g)
                for dst, src in ((x_raw[:], x_t), (c_raw[:], c_t), (g_raw[:], g_mat)):
                    sp.dma_start(dst, of_group(src)).then_inc(s["raw_in"], 16)
                for b in range(PAIRS // BATCH):
                    q = b % 2
                    if r or b >= 2:
                        sp.wait_ge(s["diff_done"], g * PAIRS + max(b - 1, 0) * BATCH)
                    sp.dma_start(mov[0:R_MOV, q].bitcast(F32), of_group(mov_rows)[b * BATCH:(b + 1) * BATCH].rearrange(
                        "k l b t h s -> (l b) k (t h s)")).then_inc(s[f"rows_in{q}"], 16)
                    sp.dma_start(sta[R_MOV:R_MOV + R_STA, q].bitcast(F32), of_group(sta_rows)[
                        b * BATCH:(b + 1) * BATCH].rearrange("k l t h p -> (l t h) k p")).then_inc(s[f"rows_in{q}"], 16)
                if r:
                    sp.wait_ge(s["pe_ec"], g * PAIRS)
                load_ec(0, 0)
                load_ec(1, 1)
                def weights_next(k, q):
                    sp.wait_ge(s["w_lo"], g * PAIRS + k - 1)
                    load_weights(k, q)

                def ec_next(k, q):
                    sp.wait_ge(s["pe_ec"], g * PAIRS + k - 1)
                    load_ec(k, q)

                weights_next(2, 0)
                if r:
                    store(g - 1)
                    sp.wait_ge(s["out_st"], 16 * g)
                sp.dma_start(xa[:], of_group(xg)).then_inc(s["x_in"], 16)
                ec_next(2, 0)
                weights_next(3, 1)
                ec_next(3, 1)
                with sp.Fori(2, PAIRS // 2) as j:
                    for q in range(2):
                        weights_next(2 * j + q, q)
                        ec_next(2 * j + q, q)

            groups(sp, body)
            store(GROUPS - 1)
            sp.wait_ge(s["out_st"], 16 * GROUPS)

        @block.gpsimd
        def _(pool):
            pool.memset(mb[:], 0.0).then_inc(s["fill"], 1)
            pool.memset(mhalf[:], -0.5).then_inc(s["fill"], 1)
            pool.wait_ge(s["fill"], 2)
            def sumsq(g, k, q, last=False):
                pool.wait_ge(s["act_sq"], g * PAIRS + k + 1)
                pool.wait_ge(s["pool_sq"], g * PAIRS + k)
                if not last:
                    pool.wait_ge(s["pool_m"], g * PAIRS + k + 2)
                pool.tensor_tensor(ssq[:], ssq[:], sq[:, q], ALU.add).then_inc(s["pool_sq"], 1)

            def tail(g):
                sumsq(g, PAIRS - 1, 1, last=True)
                pool.wait_ge(s["ln_a"], LN_STEPS * g + 1)
                pool.tensor_tensor(ry[:], ry[:], mhalf[:], ALU.pow).then_inc(s["pool_pow"], 1)

            def tail_var(g):
                pool.wait_ge(s["var_done"], g + 1)
                pool.tensor_tensor(rl[:], rl[:], mhalf[:], ALU.pow).then_inc(s["pool_pow"], 1)

            def body(r, g):
                def gdk(k, q, first):
                    pool.wait_ge(s["pool_m"], g * PAIRS + k)
                    if first:
                        pool.wait_ge(s["hl"], HL_STEPS * g + 1)
                        if r:
                            pool.wait_ge(s["dve_m"], g * PAIRS)
                    else:
                        pool.wait_ge(s["dve_m"], g * PAIRS + k - 1)
                    pool.tensor_tensor(gd[:, q], spread(g_sb[:], 2, 2), spread(
                        dd[:, bass.ds(k, 1)].squeeze(1), 1, TILES), ALU.add).then_inc(s["pool_gd"], 1)

                def mk(k, q, first):
                    pool.wait_ge(s["pool_gd"], g * PAIRS + k + 1)
                    pool.wait_ge(s["exp_done"], (g + 1) * PAIRS)
                    if not first:
                        pool.wait_ge(s["pe_intra"], g * PAIRS + k - 1)
                    pool.tensor_tensor(mb[S:P, q, :, :, S:P], e_sb[S:P, bass.ds(k, 1)].squeeze(1),
                                       gd[S:P, q], ALU.mult).then_inc(s["pool_m"], 1)

                if r:
                    tail(g - 1)
                gdk(0, 0, True)
                if r:
                    tail_var(g - 1)
                    pool.wait_ge(s["pool_pow"], 2 * g)
                mk(0, 0, True)
                gdk(1, 1, True)
                mk(1, 1, True)
                pool.wait_ge(s["act_sq"], g * PAIRS + 1)
                pool.wait_ge(s["pool_m"], g * PAIRS + 2)
                if r:
                    pool.wait_ge(s["sum_pe"], g)
                pool.tensor_tensor(ssq[:], sq[:, 0], ones[:].to_broadcast([P, GT]), ALU.mult).then_inc(s["pool_sq"], 1)
                with pool.Fori(1, PAIRS // 2) as j:
                    for q in range(2):
                        k = 2 * j + q
                        gdk(k, q, False)
                        mk(k, q, False)
                        sumsq(g, k - 1, 1 - q)

            groups(pool, body)
            tail(GROUPS - 1)
            tail_var(GROUPS - 1)

        @block.scalar
        def _(act):
            def square(g, k, q, first):
                act.wait_ge(s["dve_yadd"], g * PAIRS + k + 1)
                if not first:
                    act.wait_ge(s["pool_sq"], g * PAIRS + k - 1)
                act.activation(sq[:, q], y[:, q], ACT.Square).then_inc(s["act_sq"], 1)

            def body(r_g, g):
                def weights_hi(k, j, q, first):
                    act.wait_ge(s[f"w_in{q}"], 16 * (g * (PAIRS // 2) + j + 1))
                    if not first:
                        act.wait_ge(s["pe_ch"], g * PAIRS + k - 1)
                    elif r_g:
                        act.wait_ge(s["pe_ch"], g * PAIRS)
                    act.activation(wst[:, q, 0], wraw[:, q], ACT.Copy).then_inc(s["w_hi"], 1)

                weights_hi(0, 0, 0, True)
                if r_g:
                    act.wait_ge(s["dve_m"], g * PAIRS)
                    act.wait_ge(s["pool_m"], g * PAIRS)
                for k in range(PAIRS):
                    act.wait_ge(s["diff_done"], g * PAIRS + k + 1)
                    act.activation(e_sb[:, k], (b_xc, b_z, b_ch, b_ec)[k % 4][:].rearrange(
                        "p (t h s) -> p t h s", t=TILES, h=2), ACT.Exp).then_inc(s["exp_done"], 1)
                    if r_g and k == AFTER_INTRA:
                        square(g - 1, PAIRS - 1, 1, False)

                def conv0(k, q, first):
                    act.wait_ge(s["pe_xc"], g * PAIRS + k + 1)
                    if not first:
                        act.wait_ge(s["pe_xt"], g * PAIRS + k - 1)
                    pk = par[:, bass.ds(k, 1)].squeeze(1)
                    act.activation(acc[:, q], b_xc[:], ACT.Identity, scale=pk[:, 3:4],
                                   bias=pk[:, C_CB:C_CB + 1]).then_inc(s["act_conv"], 1)

                def gate_decay(k, q, first):
                    act.wait_ge(s["pe_z"], g * PAIRS + k + 1)
                    if first and r_g:
                        act.wait_ge(s["ln_done"], TILES * g)
                    if not first:
                        act.wait_ge(s["dve_gate"], g * PAIRS + k - 1)
                    act.activation(sz[:, q], b_z[:], ACT.Silu).then_inc(s["act_z"], 1)
                    act.wait_ge(s["pe_ec"], g * PAIRS + k + 1)
                    if not first:
                        act.wait_ge(s["dve_ce"], g * PAIRS + k - 1)
                    act.activation(eb[:, q], b_ec[:], ACT.Copy).then_inc(s["act_ec"], 1)

                def tokens(k, q, first):
                    act.wait_ge(s["pe_xt"], g * PAIRS + k + 1)
                    if not first:
                        act.wait_ge(s["pe_intra"], g * PAIRS + k - 1)
                    act.activation(xt[:, q], b_xt[:].rearrange("p (t c) -> p t c", c=P),
                                   ACT.Silu).then_inc(s["act_xt"], 1)

                def step(r, k, j, q):
                    if r < PAIRS - 1:
                        weights_hi(k + 1, j + q, 1 - q, r < 1)
                    conv0(k, q, r < 2)
                    if r >= 1:
                        square(g, k - 1, 1 - q, r == 1)
                    gate_decay(k, q, r < 2)
                    tokens(k, q, r < 2)

                step(0, 0, 0, 0)
                step(1, 1, 0, 1)
                with act.Fori(1, PAIRS // 2 - 1) as j:
                    for q in range(2):
                        step(2, 2 * j + q, j, q)
                step(2, PAIRS - 2, PAIRS // 2 - 1, 0)
                step(PAIRS - 1, PAIRS - 1, PAIRS // 2 - 1, 1)

            groups(act, body)
            square(GROUPS - 1, PAIRS - 1, 1, False)

        @block.vector
        def _(dve):
            def add_init(g, k, q, first):
                n = g * PAIRS + k
                dve.wait_ge(s["pe_intra"], n + 1)
                dve.wait_ge(s["dve_ce"], n + 1)
                if not first:
                    dve.wait_ge(s["act_sq"], n - 1)
                dve.tensor_tensor(y[:, q], b_y[:], ce[:, q], ALU.add).then_inc(s["dve_yadd"], 1)

            def gate(g, k, q, first):
                n = g * PAIRS + k
                dve.wait_ge(s["dve_yadd"], n + 1)
                dve.wait_ge(s["act_z"], n + 1)
                if not first:
                    dve.wait_ge(s["pe_out"], n - 1)
                dve.scalar_tensor_tensor(yz[:, q], y[:, q], par[:, bass.ds(k, 1)].squeeze(1)[:, C_IW:C_IW + 1],
                                         sz[:, q], ALU.mult, ALU.mult).then_inc(s["dve_gate"], 1)

            def normalise(g):
                dve.wait_ge(s["sum_pe"], g + 1)
                dve.wait_ge(s["x_in"], 16 * (g + 1))
                la = 0

                def step(ins):
                    nonlocal la
                    la += 1
                    ins.then_inc(s["ln_a"], 1)

                def upto():
                    dve.wait_ge(s["ln_a"], LN_STEPS * g + la)

                step(dve.tensor_scalar(ry[:], b_y[:, 0:TILES], 1.0 / INNER, RMS_EPS, ALU.mult, ALU.add))
                upto()
                step(dve.tensor_scalar(r1[:], xa[:], 2.0, None, ALU.mult))
                upto()
                dve.wait_ge(s["pool_pow"], 2 * g + 1)
                for t in range(TILES):
                    step(dve.scalar_tensor_tensor(r1[:, t], b_out[t // 2][:, (t % 2) * D:(t % 2) * D + D],
                                                  ry[:, t:t + 1], r1[:, t], ALU.mult, ALU.add))
                upto()
                for t in range(TILES):
                    step(dve.bn_stats(st6[:, t], r1[:, t]))
                upto()
                step(dve.tensor_tensor(mv[:, :, 0], st6[:, :, 1], st6[:, :, 4], ALU.add))
                step(dve.tensor_tensor(mv[:, :, 1], st6[:, :, 1], st6[:, :, 4], ALU.subtract))
                step(dve.tensor_tensor(mv[:, :, 2], st6[:, :, 2], st6[:, :, 5], ALU.add))
                upto()
                step(dve.tensor_scalar(mv[:, :, 0], mv[:, :, 0], 0.5, None, ALU.mult))
                step(dve.tensor_tensor(mv[:, :, 1], mv[:, :, 1], mv[:, :, 1], ALU.mult))
                step(dve.tensor_scalar(mv[:, :, 2], mv[:, :, 2], 1.0 / D, LN_EPS, ALU.mult, ALU.add))
                upto()
                dve.scalar_tensor_tensor(rl[:], mv[:, :, 1], 0.25, mv[:, :, 2], ALU.mult, ALU.add
                                         ).then_inc(s["var_done"], 1)
                dve.wait_ge(s["pool_pow"], 2 * g + 2)
                for t in range(TILES):
                    dve.tensor_scalar(xo[:, t], r1[:, t], mv[:, t, 0:1], rl[:, t:t + 1], ALU.subtract,
                                      ALU.mult).then_inc(s["ln_done"], 1)
                assert la == LN_STEPS

            def body(r_g, g):
                if r_g:
                    add_init(g - 1, PAIRS - 1, 1, False)
                    gate(g - 1, PAIRS - 1, 1, False)
                    dve.wait_ge(s["pe_ch"], PAIRS * g)
                dve.wait_ge(s["raw_in"], 16 * 3 * (g + 1))
                if r_g:
                    dve.wait_ge(s["pool_gd"], g * PAIRS)
                dve.tensor_copy(g_sb[:], g_raw[:]).then_inc(s["hl"], 1)
                for i, (raw, hi, lo) in enumerate(((x_raw, xh, xl), (c_raw, ch, cl))):
                    dve.tensor_copy(hi[:], raw[:]).then_inc(s["hl"], 1)
                    dve.wait_ge(s["hl"], HL_STEPS * g + 2 * (i + 1))
                    dve.tensor_tensor(lo[:], raw[:], hi[:].bitcast(F32), ALU.subtract).then_inc(s["hl"], 1)

                def weights_lo(k, q):
                    dve.wait_ge(s["w_hi"], g * PAIRS + k + 1)
                    dve.tensor_tensor(wst[:, q, 1], wraw[:, q], wst[:, q, 0].bitcast(F32), ALU.subtract
                                      ).then_inc(s["w_lo"], 1)

                weights_lo(0, 0)
                if r_g:
                    normalise(g - 1)
                dve.wait_ge(s["exp_done"], (g + 1) * PAIRS)

                def tap(k, q, j):
                    n = g * PAIRS + k
                    a3 = acc[:, q].rearrange("p (b s) -> p b s", s=S)
                    x3 = b_xc[:].rearrange("p (b s) -> p b s", s=S)
                    if j == 1:
                        dve.wait_ge(s["act_conv"], n + 1)
                    else:
                        dve.wait_ge(s["dve_tap"], TAPS * n + j - 1)
                    w = par[:, bass.ds(k, 1)].squeeze(1)[:, TAPS - 1 - j:TAPS - j]
                    dve.scalar_tensor_tensor(a3[:, :, j:S], x3[:, :, 0:S - j], w, a3[:, :, j:S],
                                             ALU.mult, ALU.add).then_inc(s["dve_tap"], 1)

                def front(k, q):
                    a3 = acc[:, q].rearrange("p (b s) -> p b s", s=S)[:, :, 0:TAPS - 1]
                    dve.wait_ge(s["dve_tap"], TAPS * (g * PAIRS + k) + TAPS - 1)
                    dve.tensor_tensor(a3, a3, spread(par[:, bass.ds(k, 1)].squeeze(1)[:, C_EDGE:C_N], 1, 2 * TILES),
                                      ALU.add).then_inc(s["dve_tap"], 1)

                def init_term(k, q):
                    n = g * PAIRS + k
                    dve.wait_ge(s["pe_ch"], n + 1)
                    dve.wait_ge(s["act_ec"], n + 1)
                    dve.tensor_tensor(ce[:, q], b_ch[:], eb[:, q], ALU.mult).then_inc(s["dve_ce"], 1)

                def decay_mat(k, q, first):
                    n = g * PAIRS + k
                    dve.wait_ge(s["pool_gd"], n + 1)
                    if not first:
                        dve.wait_ge(s["pe_intra"], n - 1)
                    dve.tensor_tensor(mb[0:S, q, :, :, 0:S], e_sb[0:S, bass.ds(k, 1)].squeeze(1), gd[0:S, q],
                                      ALU.mult).then_inc(s["dve_m"], 1)

                def step(r, k, q):
                    if r < PAIRS - 1:
                        weights_lo(k + 1, 1 - q)
                    tap(k, q, 1)
                    if r >= 1:
                        add_init(g, k - 1, 1 - q, r < 3)
                    tap(k, q, 2)
                    tap(k, q, 3)
                    front(k, q)
                    if r >= 1:
                        gate(g, k - 1, 1 - q, r < 3)
                    decay_mat(k, q, r < 2)
                    init_term(k, q)

                step(0, 0, 0)
                step(1, 1, 1)
                step(2, 2, 0)
                step(3, 3, 1)
                with dve.Fori(2, PAIRS // 2 - 1) as j:
                    for q in range(2):
                        step(4, 2 * j + q, q)
                step(4, PAIRS - 2, 0)
                step(PAIRS - 1, PAIRS - 1, 1)
            groups(dve, body)
            add_init(GROUPS - 1, PAIRS - 1, 1, False)
            gate(GROUPS - 1, PAIRS - 1, 1, False)
            normalise(GROUPS - 1)

        @block.tensor
        def _(pe):
            def parts_of(w, xs_):
                return [(wh, xv) if n < 2 else (wl, xv) for (wh, wl), (xhv, xlv) in zip(w, xs_)
                        for n, xv in enumerate((xhv, xlv, xhv))]

            xparts = [(xh[:, kt], xl[:, kt]) for kt in range(KT)]
            pe.wait_ge(s["fill"], 2)
            def intra(g, k, q):
                n = g * PAIRS + k
                pe.wait_ge(s["act_xt"], n + 1)
                pe.wait_ge(s["dve_m"], n + 1)
                pe.wait_ge(s["pool_m"], n + 1)
                pe.wait_ge(s["dve_yadd"], n)
                for t in range(TILES):
                    for h in range(2):
                        last = pe.matmul(b_y[h * HP:(h + 1) * HP, t * P:(t + 1) * P],
                                         xt[:, q, t, h * HP:(h + 1) * HP], mb[:, q, t, h], start=True, stop=True)
                last.then_inc(s["pe_intra"], 1)

            def out_proj(g, k, q, start=False, stop=False):
                pe.wait_ge(s["dve_gate"], g * PAIRS + k + 1)
                for t in range(TILES):
                    last = pe.matmul(b_out[t // 2][:, (t % 2) * D:(t % 2) * D + D], yz[:, q, t * P:(t + 1) * P],
                                     wo[:, bass.ds(k, 1)].squeeze(1), start=start and t % 2 == 0, stop=stop,
                                     skip_group_check=True)
                last.then_inc(s["pe_out"], 1)

            def sums(g):
                pe.wait_ge(s["pool_sq"], (g + 1) * PAIRS)
                pe.wait_ge(s["dve_yadd"], (g + 1) * PAIRS)
                for t in range(TILES):
                    last = pe.matmul(b_y[:, t:t + 1], ssq[:, t * P:(t + 1) * P], ones[:], start=True, stop=True)
                last.then_inc(s["sum_pe"], 1)

            def body(r, g):
                if r:
                    pe.wait_ge(s["dve_tap"], TAPS * PAIRS * g)
                    pe.wait_ge(s["act_z"], PAIRS * g)
                    pe.wait_ge(s["dve_ce"], PAIRS * g)
                    pe.wait_ge(s["act_ec"], PAIRS * g)
                for k in range(PAIRS):
                    b, q = k // BATCH, (k // BATCH) % 2
                    if k % BATCH == 0:
                        pe.wait_ge(s[f"rows_in{q}"], 32 * (g * (PAIRS // BATCH // 2) + b // 2 + 1))
                    if k >= 4:
                        pe.wait_ge(s["exp_done"], g * PAIRS + k - 3)
                    pe.matmul((b_xc, b_z, b_ch, b_ec)[k % 4][:], sta[:, q, k % BATCH], mov[:, q, k % BATCH],
                              start=True, stop=True).then_inc(s["diff_done"], 1)
                    if r and k == AFTER_INTRA:
                        intra(g - 1, PAIRS - 1, 1)
                    if r and k == AFTER_OUT[0]:
                        out_proj(g - 1, PAIRS - 2, 0)
                    if r and k == AFTER_OUT[1]:
                        out_proj(g - 1, PAIRS - 1, 1, stop=True)
                    if r and k == AFTER_SUMS:
                        sums(g - 1)
                pe.wait_ge(s["exp_done"], g * PAIRS + PAIRS - 3)
                pe.wait_ge(s["hl"], HL_STEPS * (g + 1))

                def wparts(q, which):
                    c = which * KT * P
                    return [(wst[:, q, 0, c + kt * P:c + (kt + 1) * P], wst[:, q, 1, c + kt * P:c + (kt + 1) * P])
                            for kt in range(KT)]

                def proj_x(k, q):
                    n = g * PAIRS + k
                    pe.wait_ge(s["w_lo"], n + 1)
                    pe.wait_ge(s["dve_tap"], TAPS * n)
                    split_product(pe, b_xc[:], parts_of(wparts(q, 0), xparts)).then_inc(s["pe_xc"], 1)

                def proj_rest(k, j, q):
                    n = g * PAIRS + k
                    pe.wait_ge(s["act_z"], n)
                    split_product(pe, b_z[:], parts_of(wparts(q, 1), xparts)).then_inc(s["pe_z"], 1)
                    pe.wait_ge(s["dve_ce"], n)
                    c = 2 * KT * P
                    split_product(pe, b_ch[:], parts_of([(wst[:, q, 0, c:c + P], wst[:, q, 1, c:c + P])],
                                                        [(ch[:], cl[:])])).then_inc(s["pe_ch"], 1)
                    pe.wait_ge(s["act_ec"], n)
                    pe.wait_ge(s[f"ec_in{q}"], 16 * (g * (PAIRS // 2) + j + 1))
                    pe.matmul(b_ec[:], ec_sel[:], ecr[:, q], start=True, stop=True).then_inc(s["pe_ec"], 1)

                def to_tokens(k, q):
                    n = g * PAIRS + k
                    pe.wait_ge(s["dve_tap"], TAPS * (n + 1))
                    pe.wait_ge(s["act_xt"], n)
                    for t in range(TILES):
                        last = pe.transpose(b_xt[:, t * P:(t + 1) * P], acc[:, q, t * P:(t + 1) * P], ident[:])
                    last.then_inc(s["pe_xt"], 1)

                def step(k, j, q, age):
                    proj_x(k, q)
                    if age > 0:
                        intra(g, k - 1, 1 - q)
                    if age == 0:
                        pe.wait_ge(s["exp_done"], (g + 1) * PAIRS)
                    proj_rest(k, j, q)
                    if age == 0 and r:
                        pe.wait_ge(s["ln_a"], LN_STEPS * g)
                    if age > 1:
                        out_proj(g, k - 2, q, start=age == 2)
                    to_tokens(k, q)

                step(0, 0, 0, age=0)
                step(1, 0, 1, age=1)
                step(2, 1, 0, age=2)
                step(3, 1, 1, age=3)
                with pe.Fori(2, PAIRS // 2) as j:
                    step(2 * j, j, 0, age=4)
                    step(2 * j + 1, j, 1, age=5)
            groups(pe, body)
            intra(GROUPS - 1, PAIRS - 1, 1)
            out_proj(GROUPS - 1, PAIRS - 2, 0)
            out_proj(GROUPS - 1, PAIRS - 1, 1, stop=True)
            sums(GROUPS - 1)


X_HEADS, XD, CTX = 32, 8, 128
CT = D // P
NT = TOKENS // P
DVE_PT = 3
LN_T = 6
PI2 = 6.283185307179586
PI2_HI = 6.28125
PI2_LO = PI2 - PI2_HI
ROUND = 12582912.0


def cross(nc, x1, ctx_in, pos, wq, wkv, wout, bout, x2, k_ident, k_freq, k_heads, k_ones4):
    x1t = x1.rearrange("(t p) d -> t p d", p=P)
    ctt = ctx_in.rearrange("(t p) d -> t p d", p=P)
    x2t = x2.rearrange("(t p) d -> t p d", p=P)
    with ExitStack() as ctx:
        sb, ps, sem = pools(nc, ctx)
        ident = sb("c_ident", [P, P])
        freq = sb("c_freq", [P, 2])
        heads4 = sb("c_heads4", [P, 4, S])
        ones4 = sb("c_ones4", [P, P])
        mhalf = sb("c_mhalf", [P, 1])
        wq_s = sb("c_wq", [P, KT, D])
        wkv_s = sb("c_wkv", [P, 2 * D])
        wo_s = sb("c_wo", [P, CT, D])
        bo_s = sb("c_bo", [P, D])
        pos_s = sb("c_pos", [P, NT, 2])
        ang = sb("c_ang", [P, NT, 4])
        tmp = sb("c_tmp", [P, NT, 4])
        red = sb("c_red", [P, NT, 4])
        trig = sb("c_trig", [P, 3, NT, 4])
        xin = sb("c_xin", [P, 2, D])
        cin = sb("c_cin", [P, 2, CTX])
        xT = sb("c_xT", [P, 2, 3 * P])
        cdup = sb("c_cdup", [P, 2, 2, 2, S])
        rt = sb("c_rt", [P, 2, 2 * X_HEADS, 4, 2])
        ru = sb("c_ru", [P, 2, 2 * X_HEADS, 4, 2])
        rqk = sb("c_rqk", [P, 2, 2 * D])
        qT = sb("c_qT", [P, 2, CT, P])
        kbd = sb("c_kbd", [P, 2, 2 * CT, 4, S])
        v4 = sb("c_v4", [P, 2, 2, 8, 2, S])
        xb = sb("c_xb", [P, 2, D])
        mx = sb("c_mx", [P, 4, 8])
        pr = sb("c_pr", [P, 4, 8, S])
        pT = sb("c_pT", [P, 4, 4, P])
        rec = sb("c_rec", [P, CT * P])
        aT = sb("c_aT", [P, CT * P])
        r1 = sb("c_r1", [P, D])
        st6 = sb("c_st6", [P, 6])
        mv = sb("c_mv", [P, 3])
        rl = sb("c_rl", [P, 1])
        xo = sb("c_xo", [P, 2, D])
        b_s = [ps(f"c_bank_s{i}") for i in range(4)]
        b_tx, b_qk, b_v, b_t = (ps(f"c_bank_{n}") for n in ("tx", "qk", "v", "t"))

        names = ("par fill trig_dve trig_act in0 in1 t_x act_x act_cd p_qk p_v ropet ropeu rope2 p_t act_q kbd "
                 "v4 xb "
                 "p_s mx sub ex p_pt pt_act pt_dve p_pv rec at p_out ln lnb var pw xo out0 out1").split()
        s = {n: sem("c_" + n) for n in names}
        block = ctx.enter_context(nc.Block())

        def rounds(eng, body):
            for i in range(PEEL):
                body(i, i, i % 2, True, i >= 1, i >= 2)
            with eng.Fori(PEEL // 2, NT // 2) as j:
                for q in range(2):
                    body(PEEL, 2 * j + q, q, True, True, True)
            body(PEEL, NT, 0, False, True, True)
            body(PEEL, NT + 1, 1, False, False, True)

        @block.sync
        def _(sp):
            for dst, src in ((ident[:], k_ident), (freq[:], k_freq), (heads4[:], k_heads), (ones4[:], k_ones4),
                             (wq_s[:], wq.rearrange("(k p) n -> p k n", p=P)), (wkv_s[:], wkv),
                             (wo_s[:], wout.rearrange("(k p) n -> p k n", p=P)),
                             (bo_s[:], bout.partition_broadcast(P)),
                             (pos_s[:], pos.rearrange("(t p) a -> p t a", p=P))):
                sp.dma_start(dst, src).then_inc(s["par"], 16)

            def store(m, q):
                sp.wait_ge(s["xo"], m + 1)
                sp.dma_start(x2t[bass.ds(m, 1)].squeeze(0), xo[:, q]).then_inc(s[f"out{q}"], 16)

            def body(r, i, q, a, b, c):
                if a:
                    if r >= 2:
                        sp.wait_ge(s["t_x"], i - 1)
                        sp.wait_ge(s["xb"], i - 1)
                    sp.dma_start(xin[:, q], x1t[bass.ds(i, 1)].squeeze(0)).then_inc(s[f"in{q}"], 16)
                    sp.dma_start(cin[:, q], ctt[bass.ds(i, 1)].squeeze(0)).then_inc(s[f"in{q}"], 16)
                if r >= 3:
                    store(i - 3, 1 - q)

            rounds(sp, body)
            store(NT - 1, 1)
            for q in range(2):
                sp.wait_ge(s[f"out{q}"], 16 * (NT // 2))

        @block.gpsimd
        def _(pool):
            pool.memset(v4[:], 0.0).then_inc(s["fill"], 1)
            pool.memset(mhalf[:], -0.5).then_inc(s["fill"], 1)
            pool.wait_ge(s["fill"], 2)
            pool.wait_ge(s["par"], 16 * 9)

            def body(r, i, q, a, b, c):
                if a:
                    pool.wait_ge(s["ropet"], i + 1)
                    pool.wait_ge(s["ropeu"], 2 * (i + 1))
                    if r >= 2:
                        pool.wait_ge(s["p_t"], i - 1)
                    pool.tensor_tensor(rqk[:, q], rt[:, q].rearrange("p h a b -> p (h a b)"),
                                       ru[:, q].rearrange("p h a b -> p (h a b)"), ALU.add).then_inc(s["rope2"], 1)
                if c:
                    pool.wait_ge(s["var"], i - 1)
                    pool.tensor_tensor(rl[:], rl[:], mhalf[:], ALU.pow).then_inc(s["pw"], 1)
                if a:
                    pool.wait_ge(s[f"in{q}"], 16 * (i - q) + 32)
                    if r >= 2:
                        pool.wait_ge(s["ln"], LN_T * (i - 2) + 1)
                    pool.tensor_tensor(xb[:, q], xin[:, q], bo_s[:], ALU.add).then_inc(s["xb"], 1)

            rounds(pool, body)

        @block.scalar
        def _(act):
            act.wait_ge(s["trig_dve"], TRIG_STEPS)
            act.activation(trig[:, 1], ang[:], ACT.Sin).then_inc(s["trig_act"], 1)
            act.activation(trig[:, 0], red[:], ACT.Sin).then_inc(s["trig_act"], 1)

            def body(r, i, q, a, b, c):
                if a:
                    act.wait_ge(s["t_x"], i + 1)
                    if r >= 2:
                        act.wait_ge(s["p_v"], i - 1)
                    act.activation(xT[:, q], b_tx[:, 0:3 * P], ACT.Copy).then_inc(s["act_x"], 1)
                    act.activation(cdup[:, q], spread(b_tx[:, 2 * P:3 * P].rearrange("p (b k) -> p b k", b=2), 2, 2),
                                   ACT.Copy).then_inc(s["act_cd"], 1)
                if b:
                    n = i - 1
                    for r4 in range(4):
                        act.wait_ge(s["sub"], 4 * n + r4 + 1)
                        act.activation(pr[:, r4], pr[:, r4], ACT.Exp, scale=XD ** -0.5).then_inc(s["ex"], 1)
                if a:
                    act.wait_ge(s["p_v"], i + 1)
                    if r >= 2:
                        act.wait_ge(s["p_pv"], i - 1)
                    for seq in range(2):
                        for hp in range(2):
                            h = slice(hp * S, hp * S + S)
                            act.activation(v4[h, q, seq, :, :, hp * XD:(hp + 1) * XD],
                                           b_v[h, seq * D:(seq + 1) * D].rearrange(
                                               "p (g r h d) -> p g r h d", g=8, r=2, h=2)[:, :, :, hp],
                                           ACT.Copy).then_inc(s["v4"], 1)
                if b:
                    for r4 in range(DVE_PT):
                        act.wait_ge(s["p_pt"], 4 * n + r4 + 1)
                        if r4 == 0 and r >= 2:
                            act.wait_ge(s["p_pv"], n)
                        act.activation(pT[:, r4], b_s[r4][:].rearrange("p (n t) -> p n t", t=P),
                                       ACT.Copy).then_inc(s["pt_act"], 1)
                if a:
                    act.wait_ge(s["kbd"], i + 1)
                    if r >= 2:
                        act.wait_ge(s["p_s"], 4 * (i - 1))
                    act.activation(qT[:, q], b_t[:, 0:CT * P].rearrange("p (c t) -> p c t", c=CT),
                                   ACT.Copy).then_inc(s["act_q"], 1)

            rounds(act, body)

        @block.vector
        def _(dve):
            n_trig = [0]

            def trig_step(ins):
                ins.then_inc(s["trig_dve"], 1)
                n_trig[0] += 1
                dve.wait_ge(s["trig_dve"], n_trig[0])

            dve.wait_ge(s["par"], 16 * 9)
            trig_step(dve.tensor_tensor(ang[:].rearrange("p t (a f) -> p (t a) f", f=2),
                                        spread(pos_s[:].rearrange("p t a -> p (t a)"), 2, 2),
                                        spread(freq[:], 1, NT * 2), ALU.mult))
            trig_step(dve.tensor_scalar(red[:], ang[:], PI2 / 4, None, ALU.add))
            for a in (ang, red):
                trig_step(dve.tensor_scalar(tmp[:], a[:], 1.0 / PI2, ROUND, ALU.mult, ALU.add))
                trig_step(dve.tensor_scalar(tmp[:], tmp[:], -ROUND, None, ALU.add))
                for part in (PI2_HI, PI2_LO):
                    trig_step(dve.scalar_tensor_tensor(a[:], tmp[:], -part, a[:], ALU.mult, ALU.add))
            dve.wait_ge(s["trig_act"], 2)
            dve.tensor_scalar(trig[:, 2], trig[:, 1], -1.0, None, ALU.mult).then_inc(s["trig_dve"], 1)
            dve.wait_ge(s["trig_dve"], n_trig[0] + 1)
            assert n_trig[0] == TRIG_STEPS

            def rope(r, i, q):
                qk = b_qk[:].rearrange("p (h a b) -> p h a b", a=4, b=2)
                tr = [trig[:, n, bass.ds(i, 1)].squeeze(1) for n in range(3)]
                dve.wait_ge(s["p_qk"], i + 1)
                if r >= 2:
                    dve.wait_ge(s["rope2"], i - 1)
                dve.tensor_tensor(rt[:, q], qk, spread(spread(tr[0], 2, 2), 1, 2 * X_HEADS),
                                  ALU.mult).then_inc(s["ropet"], 1)
                for half, t3 in ((0, tr[2]), (1, tr[1])):
                    dve.tensor_tensor(ru[:, q, :, :, half], qk[:, :, :, 1 - half], spread(t3, 1, 2 * X_HEADS),
                                      ALU.mult).then_inc(s["ropeu"], 1)

            def keys(r, i, q):
                dve.wait_ge(s["p_t"], i + 1)
                if r >= 2:
                    dve.wait_ge(s["p_s"], 4 * (i - 1))
                dve.tensor_tensor(kbd[:, q], spread(b_t[:, CT * P:2 * CT * P].rearrange("p (c k) -> p c k", k=S), 2, 4),
                                  spread(heads4[:], 1, 2 * CT), ALU.mult).then_inc(s["kbd"], 1)

            def maxima(r, n):
                def subtract(r4):
                    dve.wait_ge(s["mx"], 4 * n + r4 + 1)
                    if r4 == 0 and r >= 2:
                        dve.wait_ge(s["p_pt"], 4 * n)
                    dve.tensor_tensor(pr[:, r4], b_s[r4][:].rearrange("p (h k) -> p h k", k=S),
                                      spread(mx[:, r4], 2, S), ALU.subtract).then_inc(s["sub"], 1)

                for r4 in range(4):
                    dve.wait_ge(s["p_s"], 4 * n + r4 + 1)
                    dve.tensor_reduce(mx[:, r4], b_s[r4][:].rearrange("p (h k) -> p h k", k=S), AX.X, ALU.max
                                      ).then_inc(s["mx"], 1)
                    if r4 >= 1:
                        subtract(r4 - 1)
                subtract(3)

            def probs_out(r, n):
                for r4 in range(DVE_PT, 4):
                    dve.wait_ge(s["p_pt"], 4 * n + r4 + 1)
                    if r4 == DVE_PT and r >= 2:
                        dve.wait_ge(s["p_pv"], n)
                    dve.tensor_copy(pT[:, r4], b_s[r4][:].rearrange("p (n t) -> p n t", t=P)).then_inc(s["pt_dve"], 1)

            def normalise(n):
                dve.wait_ge(s["p_pv"], n + 1)
                dve.reciprocal(rec[:], b_v[:, CT * P:2 * CT * P]).then_inc(s["rec"], 1)
                dve.wait_ge(s["rec"], n + 1)
                dve.tensor_tensor(aT[:], b_v[:, 0:CT * P], rec[:], ALU.mult).then_inc(s["at"], 1)

            def finish(r, m, q):
                dve.wait_ge(s["p_out"], m + 1)
                dve.tensor_tensor(r1[:], b_tx[:, 0:D], xb[:, q], ALU.add).then_inc(s["ln"], 1)
                layernorm_tile(dve, s, m, r1, st6, mv, rl)
                dve.wait_ge(s["pw"], m + 1)
                if r >= 4:
                    dve.wait_ge(s[f"out{q}"], 8 * (m - q))
                dve.tensor_scalar(xo[:, q], r1[:], mv[:, 0:1], rl[:], ALU.subtract, ALU.mult).then_inc(s["xo"], 1)

            def body(r, i, q, a, b, c):
                if c:
                    normalise(i - 2)
                if b:
                    maxima(r, i - 1)
                if a:
                    rope(r, i, q)
                if b:
                    probs_out(r, i - 1)
                if a:
                    keys(r, i, q)
                if c:
                    finish(r, i - 2, q)

            rounds(dve, body)

        @block.tensor
        def _(pe):
            pe.wait_ge(s["par"], 16 * 9)
            pe.wait_ge(s["fill"], 2)

            def transpose_in(r, i, q):
                pe.wait_ge(s[f"in{q}"], 16 * (i - q) + 32)
                if r >= 3:
                    pe.wait_ge(s["ln"], LN_T * (i - 3) + 1)
                for c in range(CT):
                    pe.transpose(b_tx[:, c * P:(c + 1) * P], xin[:, q, c * P:(c + 1) * P], ident[:])
                pe.transpose(b_tx[:, 2 * P:3 * P], cin[:, q], ident[:]).then_inc(s["t_x"], 1)

            def scores(r, n, q):
                pe.wait_ge(s["act_q"], n + 1)
                pe.wait_ge(s["kbd"], n + 1)
                if r >= 2:
                    pe.wait_ge(s["pt_act"], DVE_PT * n)
                    pe.wait_ge(s["pt_dve"], (4 - DVE_PT) * n)
                for c in range(CT):
                    for r4 in range(4):
                        rows = slice(32 * r4, 32 * r4 + 32)
                        for b in range(2):
                            last = pe.matmul(b_s[r4][b * S:(b + 1) * S, c * 4 * S:(c + 1) * 4 * S],
                                             qT[rows, q, c, b * S:(b + 1) * S],
                                             kbd[rows, q, 2 * c + b].rearrange("p a k -> p (a k)"),
                                             start=True, stop=True)
                        if c == CT - 1:
                            last.then_inc(s["p_s"], 1)

            def project(r, i, q):
                pe.wait_ge(s["act_x"], i + 1)
                if r >= 1:
                    pe.wait_ge(s["ropeu"], 2 * i)
                    pe.wait_ge(s["ropet"], i)
                for c in range(KT):
                    pe.matmul(b_qk[:, 0:D], xT[:, q, c * P:(c + 1) * P], wq_s[:, c], start=c == 0, stop=c == KT - 1)
                pe.matmul(b_qk[:, D:2 * D], xT[:, q, 2 * P:3 * P], wkv_s[:, 0:D], start=True, stop=True
                          ).then_inc(s["p_qk"], 1)
                pe.wait_ge(s["act_cd"], i + 1)
                if r >= 1:
                    pe.wait_ge(s["v4"], 4 * i)
                if r >= 2:
                    pe.wait_ge(s["at"], i - 1)
                for b in range(2):
                    last = pe.matmul(b_v[:, b * D:(b + 1) * D], cdup[:, q, b].rearrange("p a k -> p (a k)"),
                                     wkv_s[:, D:2 * D], start=True, stop=True)
                last.then_inc(s["p_v"], 1)

            def out_proj(m, a):
                pe.wait_ge(s["at"], m + 1)
                if a:
                    pe.wait_ge(s["act_cd"], m + 3)
                else:
                    pe.wait_ge(s["ln"], LN_T * (m - 1) + 1)
                for c in range(CT):
                    last = pe.matmul(b_tx[:, 0:D], aT[:, c * P:(c + 1) * P], wo_s[:, c], start=c == 0, stop=c == CT - 1)
                last.then_inc(s["p_out"], 1)

            def transpose_probs(n):
                for r4 in range(4):
                    pe.wait_ge(s["ex"], 4 * n + r4 + 1)
                    for m in range(4):
                        last = pe.transpose(b_s[r4][:, m * P:(m + 1) * P],
                                            pr[:, r4, 2 * m:2 * m + 2].rearrange("p h k -> p (h k)"), ident[:])
                    last.then_inc(s["p_pt"], 1)

            def transpose_qk(r, i, q):
                pe.wait_ge(s["rope2"], i + 1)
                if r >= 1:
                    pe.wait_ge(s["act_q"], i)
                    pe.wait_ge(s["kbd"], i)
                for c in range(2 * CT):
                    last = pe.transpose(b_t[:, c * P:(c + 1) * P], rqk[:, q, c * P:(c + 1) * P], ident[:])
                last.then_inc(s["p_t"], 1)

            def attend(n, q, a):
                pe.wait_ge(s["pt_act"], DVE_PT * (n + 1))
                pe.wait_ge(s["pt_dve"], (4 - DVE_PT) * (n + 1))
                pe.wait_ge(s["v4"], 4 * (n + 2) if a else 4 * (n + 1))
                for r4 in range(4):
                    for c in range(CT):
                        for b in range(2):
                            rows, col = slice(32 * r4, 32 * r4 + 32), c * P + b * S
                            for v, o in ((v4[:, q, b, c * 4 + r4].rearrange("p a k -> p (a k)"), col),
                                         (ones4[:], col + CT * P)):
                                for m in range(2):
                                    last = pe.matmul(b_v[rows, o:o + S], v[:, 48 * m:48 * m + 32],
                                                     pT[:, r4, 2 * c + m, b * S:(b + 1) * S], start=m == 0, stop=m == 1)
                last.then_inc(s["p_pv"], 1)

            def body(r, i, q, a, b, c):
                if a:
                    transpose_in(r, i, q)
                if b:
                    scores(r, i - 1, 1 - q)
                if a:
                    project(r, i, q)
                if b:
                    transpose_probs(i - 1)
                if c:
                    out_proj(i - 2, a)
                if a:
                    transpose_qk(r, i, q)
                if b:
                    attend(i - 1, 1 - q, a)

            rounds(pe, body)


TRIG_STEPS = 10


def layernorm_tile(dve, s, i, r1, st6, mv, rl):
    n = LN_T * i
    dve.wait_ge(s["ln"], n + 1)
    dve.bn_stats(st6[:], r1[:]).then_inc(s["ln"], 1)
    dve.wait_ge(s["ln"], n + 2)
    dve.tensor_tensor(mv[:, 0:2], st6[:, 1:3], st6[:, 4:6], ALU.add).then_inc(s["ln"], 1)
    dve.tensor_tensor(mv[:, 2:3], st6[:, 1:2], st6[:, 4:5], ALU.subtract).then_inc(s["ln"], 1)
    dve.wait_ge(s["ln"], n + 4)
    dve.tensor_scalar(mv[:, 0:1], mv[:, 0:1], 0.5, None, ALU.mult).then_inc(s["ln"], 1)
    dve.tensor_tensor(mv[:, 2:3], mv[:, 2:3], mv[:, 2:3], ALU.mult).then_inc(s["ln"], 1)
    dve.wait_ge(s["ln"], n + 6)
    dve.tensor_scalar(rl[:], mv[:, 1:2], 1.0 / D, LN_EPS, ALU.mult, ALU.add).then_inc(s["lnb"], 1)
    dve.wait_ge(s["lnb"], i + 1)
    dve.scalar_tensor_tensor(rl[:], mv[:, 2:3], 0.25, rl[:], ALU.mult, ALU.add).then_inc(s["var"], 1)


HID = 704
HC = (HID + P - 1) // P
AHEAD = 2


def ffn(nc, x2, wg, wu, wd, sc, sdown, out, k_ident):
    x2g = x2.rearrange("(g t p) d -> g p t d", p=P, t=TILES)
    og = out.rearrange("(g t p) d -> g p t d", p=P, t=TILES)
    with ExitStack() as ctx:
        sb, ps, sem = pools(nc, ctx)
        ident = sb("f_ident", [P, P])
        raw = sb("f_raw", [P, KT, 2, HID], I32)
        w = sb("f_w", [P, KT, 2, HID])
        wh = sb("f_wh", [P, KT, 2, HID], F32R)
        wl = sb("f_wl", [P, KT, 2, HID], F32R)
        raw_d = sb("f_rawdown", [P, HC, D], I32)
        w_d = sb("f_wdown", [P, HC, D])
        scl = sb("f_scl", [P, 2, HC])
        sd = sb("f_sdown", [P, D])
        mhalf = sb("f_mhalf", [P, TILES])
        xin = sb("f_xin", [P, 2, TILES, D])
        xh = sb("f_xh", [P, 2, KT, GT], F32R)
        xl = sb("f_xl", [P, 2, KT, GT], F32R)
        sg = sb("f_sg", [P, 2, GT])
        hid = sb("f_hid", [P, 2, GT])
        r1 = sb("f_r1", [P, TILES, D])
        st6 = sb("f_st6", [P, TILES, 6])
        mv = sb("f_mv", [P, TILES, 3])
        rl = sb("f_rl", [P, TILES])
        xo = sb("f_xo", [P, TILES, D])
        b_t = [ps(f"f_bank_t{i}") for i in range(2)]
        b_g = [ps(f"f_bank_g{i}") for i in range(2)]
        b_u = [ps(f"f_bank_u{i}") for i in range(2)]
        b_o = [ps(f"f_bank_o{i}") for i in range(2)]
        names = "par_gu par fill con wh in0 in1 t_x act_x dve_x p_g p_u sg hid p_o ln var pw xo out".split()
        s = {n: sem("f_" + n) for n in names}
        block = ctx.enter_context(nc.Block())
        LN_G = 8 + TILES
        sizes = [min(P, HID - c * P) for c in range(HC)]

        def groups(eng, body):
            body(0, 0, 0, True)
            body(1, 1, 1, True)
            with eng.Fori(1, GROUPS // 2 - 1) as j:
                for q in range(2):
                    body(2, 2 * j + q, q, True)
            body(2, GROUPS - 2, 0, True)
            body(2, GROUPS - 1, 1, False)

        @block.sync
        def _(sp):
            for dst, src in ((raw[:, :, 0], wg), (raw[:, :, 1], wu), (ident[:], k_ident)):
                sp.dma_start(dst, src).then_inc(s["par_gu"], 16)
            for dst, src in ((scl[:], sc), (raw_d[:], wd), (sd[:], sdown.partition_broadcast(P))):
                sp.dma_start(dst, src).then_inc(s["par"], 16)
            def store(g):
                sp.wait_ge(s["xo"], TILES * (g + 1))
                sp.dma_start(og[bass.ds(g, 1)].squeeze(0), xo[:]).then_inc(s["out"], 16)

            def body(r, g, q, ahead):
                if r >= 2:
                    sp.wait_ge(s["ln"], LN_G * (g - 2) + 2)
                sp.dma_start(xin[:, q], x2g[bass.ds(g, 1)].squeeze(0)).then_inc(s[f"in{q}"], 16)
                if r >= 2:
                    store(g - 2)

            groups(sp, body)
            store(GROUPS - 2)
            store(GROUPS - 1)
            sp.wait_ge(s["out"], 16 * GROUPS)

        @block.gpsimd
        def _(pool):
            pool.memset(mhalf[:], -0.5).then_inc(s["fill"], 1)
            pool.wait_ge(s["fill"], 1)
            with pool.Fori(0, GROUPS) as g:
                pool.wait_ge(s["var"], g + 1)
                pool.tensor_tensor(rl[:], rl[:], mhalf[:], ALU.pow).then_inc(s["pw"], 1)

        @block.scalar
        def _(act):
            act.wait_ge(s["con"], 1)
            act.activation(wh[:], w[:], ACT.Copy).then_inc(s["wh"], 1)

            def round_x(g, q):
                act.wait_ge(s["t_x"], g + 1)
                for kt in range(KT):
                    act.activation(xh[:, q, kt], b_t[kt][:], ACT.Copy).then_inc(s["act_x"], 1)

            def body(r, g, q, ahead):
                for c, n in enumerate(sizes):
                    act.wait_ge(s["p_g"], g * HC + c + 1)
                    if r >= 1 or c >= 2:
                        act.wait_ge(s["hid"], g * HC + c - 1)
                    act.activation(sg[0:n, c % 2], b_g[c % 2][0:n, :], ACT.Silu,
                                   scale=scl[0:n, 0, c:c + 1]).then_inc(s["sg"], 1)
                    if ahead and c == AHEAD:
                        round_x(g + 1, 1 - q)

            round_x(0, 0)
            act.wait_ge(s["par"], 16 * 3)
            groups(act, body)

        @block.vector
        def _(dve):
            dve.wait_ge(s["par_gu"], 16 * 3)
            dve.tensor_scalar(w[:], raw[:], -128.0, None, ALU.add).then_inc(s["con"], 1)
            dve.wait_ge(s["wh"], 1)
            dve.tensor_tensor(wl[:], w[:], wh[:].bitcast(F32), ALU.subtract).then_inc(s["con"], 1)

            def rest_x(g, q):
                for kt in range(KT):
                    dve.wait_ge(s["act_x"], KT * g + kt + 1)
                    dve.tensor_tensor(xl[:, q, kt], b_t[kt][:], xh[:, q, kt].bitcast(F32), ALU.subtract
                                      ).then_inc(s["dve_x"], 1)

            def normalise(r, g):
                dve.wait_ge(s["pw"], g + 1)
                if r >= 1:
                    dve.wait_ge(s["out"], 16 * g)
                for t in range(TILES):
                    dve.tensor_scalar(xo[:, t], r1[:, t], mv[:, t, 0:1], rl[:, t:t + 1], ALU.subtract,
                                      ALU.mult).then_inc(s["xo"], 1)

            def body(r, g, q, ahead):
                for c, n in enumerate(sizes):
                    dve.wait_ge(s["p_u"], g * HC + c + 1)
                    dve.wait_ge(s["sg"], g * HC + c + 1)
                    if r >= 1 or c >= 2:
                        dve.wait_ge(s["p_o"], g * HC + c - 1)
                    dve.scalar_tensor_tensor(hid[0:n, c % 2], b_u[c % 2][0:n, :], scl[0:n, 1, c:c + 1],
                                             sg[0:n, c % 2], ALU.mult, ALU.mult).then_inc(s["hid"], 1)
                    if c == 0 and r >= 1:
                        normalise(r - 1, g - 1)
                    if ahead and c == AHEAD:
                        rest_x(g + 1, 1 - q)
                la = 0

                def step(ins):
                    nonlocal la
                    la += 1
                    ins.then_inc(s["ln"], 1)

                def upto():
                    dve.wait_ge(s["ln"], LN_G * g + la)

                dve.wait_ge(s["p_o"], g * HC + HC)
                for half in range(2):
                    h = slice(2 * half, 2 * half + 2)
                    step(dve.tensor_tensor(r1[:, h], b_o[half][:].rearrange("p (t d) -> p t d", d=D),
                                           xin[:, q, h], ALU.add))
                upto()
                for t in range(TILES):
                    step(dve.bn_stats(st6[:, t], r1[:, t]))
                upto()
                step(dve.tensor_tensor(mv[:, :, 0], st6[:, :, 1], st6[:, :, 4], ALU.add))
                step(dve.tensor_tensor(mv[:, :, 1], st6[:, :, 1], st6[:, :, 4], ALU.subtract))
                step(dve.tensor_tensor(mv[:, :, 2], st6[:, :, 2], st6[:, :, 5], ALU.add))
                upto()
                step(dve.tensor_scalar(mv[:, :, 0], mv[:, :, 0], 0.5, None, ALU.mult))
                step(dve.tensor_tensor(mv[:, :, 1], mv[:, :, 1], mv[:, :, 1], ALU.mult))
                step(dve.tensor_scalar(mv[:, :, 2], mv[:, :, 2], 1.0 / D, LN_EPS, ALU.mult, ALU.add))
                upto()
                dve.scalar_tensor_tensor(rl[:], mv[:, :, 1], 0.25, mv[:, :, 2], ALU.mult, ALU.add
                                         ).then_inc(s["var"], 1)
                assert la == LN_G

            rest_x(0, 0)
            dve.wait_ge(s["par"], 16 * 3)
            dve.tensor_scalar(w_d[:], raw_d[:], -128.0, None, ALU.add).then_inc(s["con"], 1)
            dve.wait_ge(s["con"], 3)
            dve.tensor_tensor(w_d[:], w_d[:], spread(sd[:], 1, HC), ALU.mult).then_inc(s["con"], 1)
            groups(dve, body)
            normalise(2, GROUPS - 1)

        @block.tensor
        def _(pe):
            pe.wait_ge(s["par_gu"], 16 * 3)

            def transpose_x(r, g, q):
                pe.wait_ge(s[f"in{q}"], 8 * (g - q) + 16)
                if r >= 1:
                    pe.wait_ge(s["act_x"], KT * g)
                    pe.wait_ge(s["dve_x"], KT * g)
                for t in range(TILES):
                    for kt in range(KT):
                        last = pe.transpose(b_t[kt][:, t * P:(t + 1) * P], xin[:, q, t, kt * P:(kt + 1) * P], ident[:])
                last.then_inc(s["t_x"], 1)

            def gate_up(r, g, q, c, n):
                if r == 0 and c == 0:
                    pe.wait_ge(s["con"], 2)
                if r >= 1 or c >= 2:
                    pe.wait_ge(s["sg"], g * HC + c - 1)
                    pe.wait_ge(s["hid"], g * HC + c - 1)
                for u, bank, name in ((0, b_g, "p_g"), (1, b_u, "p_u")):
                    parts = [(a[:, kt, u, c * P:c * P + n], b[:, q, kt]) for kt in range(KT)
                             for a, b in ((wh, xh), (wh, xl), (wl, xh))]
                    for i, (a, b) in enumerate(parts):
                        last = pe.matmul(bank[c % 2][0:n, :], a, b, start=i == 0, stop=i == len(parts) - 1)
                    last.then_inc(s[name], 1)

            def down(r, g, c, n):
                pe.wait_ge(s["hid"], g * HC + c + 1)
                if c == 0 and r == 0:
                    pe.wait_ge(s["con"], 4)
                if c == 0 and r >= 1:
                    pe.wait_ge(s["ln"], LN_G * (g - 1) + 2)
                for t in range(TILES):
                    last = pe.matmul(b_o[t // 2][:, (t % 2) * D:(t % 2) * D + D],
                                     hid[0:n, c % 2, t * P:(t + 1) * P], w_d[0:n, c],
                                     start=c == 0 and t % 2 == 0, stop=c == HC - 1, skip_group_check=True)
                last.then_inc(s["p_o"], 1)

            def body(r, g, q, ahead):
                pe.wait_ge(s["act_x"], KT * (g + 1))
                pe.wait_ge(s["dve_x"], KT * (g + 1))
                for c, n in enumerate(sizes):
                    gate_up(r, g, q, c, n)
                    if c >= 1:
                        down(r, g, c - 1, sizes[c - 1])
                    if ahead and c == AHEAD:
                        transpose_x(r + 1, g + 1, 1 - q)
                down(r, g, HC - 1, sizes[HC - 1])

            transpose_x(0, 0, 0)
            groups(pe, body)


_SCRATCH = {"x_t": (GROUPS, P, KT, GT), "c_t": (GROUPS, P, GT), "g_mat": (GROUPS, P, TILES, S),
            "mov_rows": (GROUPS, PAIRS, 2, 2, TILES, 2, S), "sta_rows": (GROUPS, PAIRS, 2, TILES, 2, P),
            "ec_rows": (GROUPS, PAIRS, 2, 2, GT), "x1": (TOKENS, D), "x2": (TOKENS, D)}


def constants(np):
    r, col = np.arange(R_ALL)[:, None], np.arange(GT)[None]
    mask_row = r - R_MOV - R_STA
    mov = np.where(((r - R_MOV) % 8 == col // S) & (r >= R_MOV) & (mask_row < 0), -1.0, 0.0)
    mov = np.where((mask_row >= 0) & (mask_row > col % S), -1e30, mov)
    p = np.arange(P)[None]
    sta = np.where((r < R_MOV) & (r % 2 == p // S), 1.0, 0.0)
    sta = np.where((mask_row >= 0) & (mask_row == p % S), 1.0, sta)
    pc = np.arange(P)[:, None]
    own = (np.arange(P)[None] % S) // XD == pc // S
    consts = {
        "k_ident": np.eye(P), "k_eye2": np.tile(np.eye(S), (2, 1)),
        "k_reset": np.tile((np.arange(GT) % S != 0) * 1.0, (HEADS, 1)),
        "k_mov": mov, "k_sta": sta,
        "k_sel": (np.arange(4)[:, None] % 2 == p // HP) * 1.0,
        "k_freq": np.tile([[1.0, 10000.0 ** -0.5]], (P, 1)),
        "k_heads": np.repeat((pc % 32 // XD == np.arange(4)[None]) * 1.0, S, axis=1).reshape(P, 4, S),
        "k_ones4": own * 1.0,
    }
    return {k: np.ascontiguousarray(v, np.float32) for k, v in consts.items()}


def arrange(np, i):
    w = i["L0_attn_in_proj_w"]
    wz, wx = w[:INNER], w[INNER:2 * INNER]
    wb, wc, wd = np.split(w[2 * INNER:], [N, 2 * N])
    order = np.concatenate([np.arange(0, HEADS, 2), np.arange(1, HEADS, 2)])

    def pair_major(m):
        return m.reshape(PAIRS, P, KT, P).transpose(0, 3, 2, 1).reshape(PAIRS, P, KT * P)

    def padded(m):
        return np.concatenate([m, np.zeros((HC * P - HID,) + m.shape[1:], m.dtype)])

    h0 = i["L0_attn_ssm_state"][0].reshape(PAIRS, 2, N, HP).transpose(0, 2, 1, 3).reshape(PAIRS, N, P)
    chan = np.concatenate([i["L0_attn_conv_w"], i["L0_attn_conv_b"][:, None], i["L0_attn_inner_norm_w"][:, None],
                           i["L0_attn_conv_state"][0]], axis=1)
    out = {
        "x": i["x"].reshape(TOKENS, D),
        "pair_w": np.concatenate([pair_major(wx), pair_major(wz), h0], axis=2),
        "aux_w": np.concatenate([wb, wc, wd[order]]).T.reshape(KT, P, AUX).transpose(1, 0, 2),
        "dt_par": np.stack([i["L0_attn_dt_bias"][order], i["L0_attn_A_log"][order]], axis=1),
        "chan_par": chan.reshape(PAIRS, P, C_EDGE).transpose(1, 0, 2),
        "d_rows": i["L0_attn_D_param"],
        "norm_w": i["L0_attn_norm_w"].reshape(KT, P).T,
        "wout": i["L0_attn_out_proj_w"].T.reshape(PAIRS, P, D).transpose(1, 0, 2),
        "ctx": i["ctx_1024"].reshape(TOKENS, CTX),
        "pos": i["fside_BxSx2_0"].reshape(TOKENS, 2),
        "x_wq": i["L0_xattn_Wq"], "x_wkv": i["L0_xattn_Wkv"], "x_wout": i["L0_xattn_Wout"], "x_bout": i["L0_xattn_bout"],
        "f_wg": i["L0_ffn_wq_gate"].T.reshape(KT, P, HID).transpose(1, 0, 2),
        "f_wu": i["L0_ffn_wq_up"].T.reshape(KT, P, HID).transpose(1, 0, 2),
        "f_wd": padded(i["L0_ffn_wq_down"].T).reshape(HC, P, D).transpose(1, 0, 2),
        "f_sc": np.stack([padded(i["L0_ffn_s_gate"]), padded(i["L0_ffn_s_up"])]).reshape(2, HC, P).transpose(2, 0, 1),
        "f_sd": i["L0_ffn_s_down"],
    }
    return {k: np.ascontiguousarray(v) for k, v in out.items()}


def program(nc, d, out):
    with ExitStack() as ctx:
        tables = resident(nc, ctx)
        heads(nc, tables, d["x"], d["aux_w"], d["dt_par"], d["norm_w"], d["chan_par"], d["d_rows"], d["wout"],
              d["x_t"], d["c_t"], d["g_mat"], d["mov_rows"], d["sta_rows"], d["ec_rows"],
              d["k_ident"], d["k_reset"], d["k_eye2"], d["k_mov"], d["k_sta"], d["k_sel"])
        mixer(nc, tables, d["x"], d["pair_w"], d["x1"], d["x_t"], d["c_t"], d["g_mat"],
              d["mov_rows"], d["sta_rows"], d["ec_rows"])
    cross(nc, d["x1"], d["ctx"], d["pos"], d["x_wq"], d["x_wkv"], d["x_wout"], d["x_bout"], d["x2"],
          d["k_ident"], d["k_freq"], d["k_heads"], d["k_ones4"])
    ffn(nc, d["x2"], d["f_wg"], d["f_wu"], d["f_wd"], d["f_sc"], d["f_sd"], out, d["k_ident"])


def kernel(**inputs):
    import numpy as np
    import concourse.bacc as bacc
    from concourse.bass_utils import run_bass_kernel_spmd

    nc = bacc.Bacc("TRN2", target_bir_lowering=False, num_devices=1)
    arrays = {**arrange(np, {k: np.asarray(v) for k, v in inputs.items()}), **constants(np)}
    d = {k: nc.dram_tensor(k, v.shape, mybir.dt.from_np(v.dtype), kind="ExternalInput").ap() for k, v in arrays.items()}
    d.update({k: nc.dram_tensor(k, shape, F32).ap() for k, shape in _SCRATCH.items()})
    out = nc.dram_tensor("out", (TOKENS, D), F32, kind="ExternalOutput").ap()
    program(nc, d, out)
    r = run_bass_kernel_spmd(nc, [arrays], core_ids=[0])
    return r.results[0]["out"].reshape(SEQS, S, D)
```
